# Optimizing a Trainium2 kernel written in Bass

```python
import numpy as np
import jax
import jax.numpy as jnp

def _softmax(x, axis=-1):
    return jax.nn.softmax(x, axis=axis)

def _gelu(x):
    return jax.nn.gelu(x, approximate=True)

def _silu(x):
    return jax.nn.silu(x)

def _sigmoid(x):
    return jax.nn.sigmoid(x)

def _layernorm(x, axis=-1, eps=1e-05):
    m = jnp.mean(x, axis=axis, keepdims=True)
    v = jnp.var(x, axis=axis, keepdims=True)
    return (x - m) / jnp.sqrt(v + eps)

def _scatter_add(tgt, idx, src, axis=0):
    return tgt.at[idx].add(src)

def _segment_sum(src, seg, n):
    return jax.ops.segment_sum(src, seg, n)
kernel_name = 'mk_conv_preact_d4_conv_nchw128_r4_88e4a0'

def setup_inputs(seed: int=0):
    np.random.seed(seed)
    _w = jnp.asarray

    def _rec_inputs():
        import jax
        import jax.numpy as jnp
        _gk = jax.random.key(seed)
        x = -0.0005207 + 1.001 * jax.random.normal(jax.random.fold_in(_gk, 1), (16, 32, 32, 32), jnp.float32)
        return x
    x = _rec_inputs()

    def _L0_conv_setup():
        import jax, jax.numpy as jnp
        import numpy as np
        PATCH = 2
        TOP_K = 2
        key = jax.random.key(seed)
        k1, k2, k3, k4 = jax.random.split(key, 4)
        B, C, H, W = (16, 32, 32, 32)
        d = C * PATCH * PATCH
        E, hidden = (8, 256)
        x = jax.random.normal(k1, (B, C, H, W), dtype=jnp.float32)
        router_w = jax.random.normal(k2, (d, E), dtype=jnp.float32) * 0.02
        w1 = jax.random.normal(k3, (E, d, 2 * hidden), dtype=jnp.float32) * 0.02
        w2 = jax.random.normal(k4, (E, hidden, d), dtype=jnp.float32) * 0.02
        return {'x': x, 'router_w': router_w, 'w1': w1, 'w2': w2}
    _L0_conv_all = _L0_conv_setup()
    _L0_conv_in = {k: v for k, v in _L0_conv_all.items() if k in ('router_w', 'w1', 'w2')}
    del _L0_conv_all

    def _L1_conv_setup():
        import jax, jax.numpy as jnp
        import numpy as np
        K = 3
        K2 = K * K
        EPS = 1e-05

        def _conv3x3(x, w, b):
            y = jax.lax.conv_general_dilated(x, w, window_strides=(1, 1), padding=[(1, 1), (1, 1)], dimension_numbers=('NCHW', 'OIHW', 'NCHW'))
            return y + b[None, :, None, None]

        def _deform_conv(x, w_om, b_om, w, b):
            B, C, H, W_ = x.shape
            CO = w.shape[0]
            om = _conv3x3(x, w_om, b_om)
            o1, o2, m = jnp.split(om, 3, axis=1)
            offset = jnp.concatenate([o1, o2], axis=1)
            mask = jax.nn.sigmoid(m)
            dy = offset[:, 0::2]
            dx = offset[:, 1::2]
            ky, kx = jnp.meshgrid(jnp.arange(K), jnp.arange(K), indexing='ij')
            base_y = (jnp.arange(H)[None, :, None] - 1 + ky.reshape(K2, 1, 1)).astype(jnp.float32)
            base_x = (jnp.arange(W_)[None, None, :] - 1 + kx.reshape(K2, 1, 1)).astype(jnp.float32)
            py = base_y[None] + dy
            px = base_x[None] + dx
            y0 = jnp.floor(py)
            x0 = jnp.floor(px)
            fy = py - y0
            fx = px - x0

            def gather_corner(yi, xi, wgt):
                valid = (yi >= 0) & (yi < H) & (xi >= 0) & (xi < W_)
                yc = jnp.clip(yi, 0, H - 1).astype(jnp.int32)
                xc = jnp.clip(xi, 0, W_ - 1).astype(jnp.int32)
                idx = yc * W_ + xc

                def g(img, ind):
                    return jnp.take(img.reshape(C, -1), ind.reshape(-1), axis=1).reshape(C, K2, H, W_)
                v = jax.vmap(g)(x, idx)
                return v * (wgt * valid)[:, None]
            sampled = gather_corner(y0, x0, (1 - fy) * (1 - fx)) + gather_corner(y0, x0 + 1, (1 - fy) * fx) + gather_corner(y0 + 1, x0, fy * (1 - fx)) + gather_corner(y0 + 1, x0 + 1, fy * fx)
            sampled = sampled * mask[:, None]
            out = jnp.einsum('bckhw,ock->bohw', sampled, w.reshape(CO, C, K2))
            return out + b[None, :, None, None]
        key = jax.random.key(seed)
        ks = jax.random.split(key, 9)
        B, C, H, W = (4, 32, 32, 32)
        CO = 32
        x = jax.random.normal(ks[0], (B, C, H, W), jnp.float32)
        w_om = jax.random.normal(ks[1], (3 * K2, C, K, K), jnp.float32) * 0.05
        b_om = jax.random.normal(ks[2], (3 * K2,), jnp.float32) * 0.05
        w = jax.random.normal(ks[3], (CO, C, K, K), jnp.float32) * (1.0 / np.sqrt(C * K2))
        b = jax.random.normal(ks[4], (CO,), jnp.float32) * 0.01
        gamma = jax.random.uniform(ks[5], (CO,), jnp.float32, minval=0.5, maxval=1.5)
        beta = jax.random.normal(ks[6], (CO,), jnp.float32) * 0.1
        bn_mean = jax.random.normal(ks[7], (CO,), jnp.float32) * 0.1
        bn_var = jax.random.uniform(ks[8], (CO,), jnp.float32, minval=0.5, maxval=1.5)
        return dict(x=x, w_om=w_om, b_om=b_om, w=w, b=b, gamma=gamma, beta=beta, bn_mean=bn_mean, bn_var=bn_var)
    _L1_conv_all = _L1_conv_setup()
    _L1_conv_in = {k: v for k, v in _L1_conv_all.items() if k in ('w_om', 'b_om', 'w', 'b', 'gamma', 'beta', 'bn_mean', 'bn_var')}
    del _L1_conv_all

    def _L2_conv_setup():
        import jax, jax.numpy as jnp
        import numpy as np
        import math
        BATCH, SEQ, HH, WW = (32, 32, 32, 32)
        D_MODEL = 256
        N2 = 4
        L_MAX = 16

        def _layernorm(x, gamma, beta, eps=1e-05):
            mu = jnp.mean(x, axis=-1, keepdims=True)
            var = jnp.var(x, axis=-1, keepdims=True)
            return (x - mu) * jax.lax.rsqrt(var + eps) * gamma + beta
        key = jax.random.key(seed)
        ks = jax.random.split(key, 12)
        d_in = SEQ
        inp = {'x': jax.random.normal(ks[0], (BATCH, SEQ, HH, WW), dtype=jnp.float32), 'W_enc': jax.random.normal(ks[1], (d_in, D_MODEL), dtype=jnp.float32) / math.sqrt(d_in), 'b_enc': jnp.zeros((D_MODEL,), dtype=jnp.float32), 'log_dt': jax.random.uniform(ks[2], (D_MODEL,), dtype=jnp.float32) * (math.log(0.1) - math.log(0.001)) + math.log(0.001), 'A_log_real': jnp.full((D_MODEL, N2), math.log(0.5), dtype=jnp.float32), 'A_imag': jnp.broadcast_to(math.pi * jnp.arange(N2, dtype=jnp.float32), (D_MODEL, N2)).copy(), 'C_real': jax.random.normal(ks[3], (D_MODEL, N2), dtype=jnp.float32) * 0.5, 'C_imag': jax.random.normal(ks[4], (D_MODEL, N2), dtype=jnp.float32) * 0.5, 'D': jax.random.normal(ks[5], (D_MODEL,), dtype=jnp.float32), 'W_glu': jax.random.normal(ks[6], (D_MODEL, 2 * D_MODEL), dtype=jnp.float32) / math.sqrt(D_MODEL), 'b_glu': jnp.zeros((2 * D_MODEL,), dtype=jnp.float32), 'ln_gamma': jnp.ones((D_MODEL,), dtype=jnp.float32), 'ln_beta': jnp.zeros((D_MODEL,), dtype=jnp.float32), 'W_dec': jax.random.normal(ks[7], (D_MODEL, d_in), dtype=jnp.float32) / math.sqrt(D_MODEL), 'b_dec': jnp.zeros((d_in,), dtype=jnp.float32)}
        return inp
    _L2_conv_all = _L2_conv_setup()
    _L2_conv_in = {k: v for k, v in _L2_conv_all.items() if k in ('W_enc', 'b_enc', 'log_dt', 'A_log_real', 'A_imag', 'C_real', 'C_imag', 'D', 'W_glu', 'b_glu', 'ln_gamma', 'ln_beta', 'W_dec', 'b_dec')}
    del _L2_conv_all

    def _L3_conv_setup():
        import jax, jax.numpy as jnp
        import numpy as np
        C = 32
        HID = 4 * C
        K = 7
        PAD = K // 2
        B, T, F = (4, 128, 32)
        LN_EPS = 1e-05
        LS_INIT = 0.01
        key = jax.random.key(seed)
        ks = jax.random.split(key, 4)
        x = jax.random.normal(ks[0], (B, C, T, F), dtype=jnp.float32)
        dw_w = jax.random.normal(ks[1], (C, 1, K, K), dtype=jnp.float32) * (1.0 / K)
        dw_b = jnp.zeros((C,), dtype=jnp.float32)
        ln_g = jnp.ones((C,), dtype=jnp.float32)
        ln_b = jnp.zeros((C,), dtype=jnp.float32)
        w1 = jax.random.normal(ks[2], (HID, C), dtype=jnp.float32) * (1.0 / np.sqrt(C))
        b1 = jnp.zeros((HID,), dtype=jnp.float32)
        w2 = jax.random.normal(ks[3], (C, HID), dtype=jnp.float32) * (1.0 / np.sqrt(HID))
        b2 = jnp.zeros((C,), dtype=jnp.float32)
        ls = jnp.full((C,), LS_INIT, dtype=jnp.float32)
        return {'x': x, 'dw_w': dw_w, 'dw_b': dw_b, 'ln_g': ln_g, 'ln_b': ln_b, 'w1': w1, 'b1': b1, 'w2': w2, 'b2': b2, 'ls': ls}
    _L3_conv_all = _L3_conv_setup()
    _L3_conv_in = {k: v for k, v in _L3_conv_all.items() if k in ('dw_w', 'dw_b', 'ln_g', 'ln_b', 'w1', 'b1', 'w2', 'b2', 'ls')}
    del _L3_conv_all
    return {'x': x, 'L0_conv_router_w': _L0_conv_in['router_w'], 'L0_conv_w1': _L0_conv_in['w1'], 'L0_conv_w2': _L0_conv_in['w2'], 'L1_conv_w_om': _L1_conv_in['w_om'], 'L1_conv_b_om': _L1_conv_in['b_om'], 'L1_conv_w': _L1_conv_in['w'], 'L1_conv_b': _L1_conv_in['b'], 'L1_conv_gamma': _L1_conv_in['gamma'], 'L1_conv_beta': _L1_conv_in['beta'], 'L1_conv_bn_mean': _L1_conv_in['bn_mean'], 'L1_conv_bn_var': _L1_conv_in['bn_var'], 'L2_conv_W_enc': _L2_conv_in['W_enc'], 'L2_conv_b_enc': _L2_conv_in['b_enc'], 'L2_conv_log_dt': _L2_conv_in['log_dt'], 'L2_conv_A_log_real': _L2_conv_in['A_log_real'], 'L2_conv_A_imag': _L2_conv_in['A_imag'], 'L2_conv_C_real': _L2_conv_in['C_real'], 'L2_conv_C_imag': _L2_conv_in['C_imag'], 'L2_conv_D': _L2_conv_in['D'], 'L2_conv_W_glu': _L2_conv_in['W_glu'], 'L2_conv_b_glu': _L2_conv_in['b_glu'], 'L2_conv_ln_gamma': _L2_conv_in['ln_gamma'], 'L2_conv_ln_beta': _L2_conv_in['ln_beta'], 'L2_conv_W_dec': _L2_conv_in['W_dec'], 'L2_conv_b_dec': _L2_conv_in['b_dec'], 'L3_conv_dw_w': _L3_conv_in['dw_w'], 'L3_conv_dw_b': _L3_conv_in['dw_b'], 'L3_conv_ln_g': _L3_conv_in['ln_g'], 'L3_conv_ln_b': _L3_conv_in['ln_b'], 'L3_conv_w1': _L3_conv_in['w1'], 'L3_conv_b1': _L3_conv_in['b1'], 'L3_conv_w2': _L3_conv_in['w2'], 'L3_conv_b2': _L3_conv_in['b2'], 'L3_conv_ls': _L3_conv_in['ls']}

def reference(x, L0_conv_router_w, L0_conv_w1, L0_conv_w2, L1_conv_w_om, L1_conv_b_om, L1_conv_w, L1_conv_b, L1_conv_gamma, L1_conv_beta, L1_conv_bn_mean, L1_conv_bn_var, L2_conv_W_enc, L2_conv_b_enc, L2_conv_log_dt, L2_conv_A_log_real, L2_conv_A_imag, L2_conv_C_real, L2_conv_C_imag, L2_conv_D, L2_conv_W_glu, L2_conv_b_glu, L2_conv_ln_gamma, L2_conv_ln_beta, L2_conv_W_dec, L2_conv_b_dec, L3_conv_dw_w, L3_conv_dw_b, L3_conv_ln_g, L3_conv_ln_b, L3_conv_w1, L3_conv_b1, L3_conv_w2, L3_conv_b2, L3_conv_ls):
    import jax
    import jax.numpy as jnp

    def _L0_conv_ref(x, router_w, w1, w2):
        import jax, jax.numpy as jnp
        import numpy as np
        PATCH = 2
        TOP_K = 2
        B, C, H, W = x.shape
        p = PATCH
        E = w1.shape[0]
        d = C * p * p
        xp = x.reshape(B, C, H // p, p, W // p, p)
        xp = xp.transpose(0, 2, 4, 1, 3, 5).reshape(-1, d)
        logits = xp @ router_w
        probs = jax.nn.softmax(logits, axis=-1)
        topv, topi = jax.lax.top_k(probs, TOP_K)
        topv = topv / jnp.sum(topv, axis=-1, keepdims=True)
        onehot = jax.nn.one_hot(topi, E, dtype=probs.dtype)
        gate = jnp.sum(onehot * topv[..., None], axis=1)
        out = jnp.zeros_like(xp)
        for e in range(E):
            h = xp @ w1[e]
            val, g = jnp.split(h, 2, axis=-1)
            he = val * jax.nn.sigmoid(g)
            out = out + gate[:, e:e + 1] * (he @ w2[e])
        y = out.reshape(B, H // p, W // p, C, p, p)
        y = y.transpose(0, 3, 1, 4, 2, 5).reshape(B, C, H, W)
        return y

    def _L1_conv_ref(x, w_om, b_om, w, b, gamma, beta, bn_mean, bn_var):
        import jax, jax.numpy as jnp
        import numpy as np
        K = 3
        K2 = K * K
        EPS = 1e-05

        def _conv3x3(x, w, b):
            y = jax.lax.conv_general_dilated(x, w, window_strides=(1, 1), padding=[(1, 1), (1, 1)], dimension_numbers=('NCHW', 'OIHW', 'NCHW'))
            return y + b[None, :, None, None]

        def _deform_conv(x, w_om, b_om, w, b):
            B, C, H, W_ = x.shape
            CO = w.shape[0]
            om = _conv3x3(x, w_om, b_om)
            o1, o2, m = jnp.split(om, 3, axis=1)
            offset = jnp.concatenate([o1, o2], axis=1)
            mask = jax.nn.sigmoid(m)
            dy = offset[:, 0::2]
            dx = offset[:, 1::2]
            ky, kx = jnp.meshgrid(jnp.arange(K), jnp.arange(K), indexing='ij')
            base_y = (jnp.arange(H)[None, :, None] - 1 + ky.reshape(K2, 1, 1)).astype(jnp.float32)
            base_x = (jnp.arange(W_)[None, None, :] - 1 + kx.reshape(K2, 1, 1)).astype(jnp.float32)
            py = base_y[None] + dy
            px = base_x[None] + dx
            y0 = jnp.floor(py)
            x0 = jnp.floor(px)
            fy = py - y0
            fx = px - x0

            def gather_corner(yi, xi, wgt):
                valid = (yi >= 0) & (yi < H) & (xi >= 0) & (xi < W_)
                yc = jnp.clip(yi, 0, H - 1).astype(jnp.int32)
                xc = jnp.clip(xi, 0, W_ - 1).astype(jnp.int32)
                idx = yc * W_ + xc

                def g(img, ind):
                    return jnp.take(img.reshape(C, -1), ind.reshape(-1), axis=1).reshape(C, K2, H, W_)
                v = jax.vmap(g)(x, idx)
                return v * (wgt * valid)[:, None]
            sampled = gather_corner(y0, x0, (1 - fy) * (1 - fx)) + gather_corner(y0, x0 + 1, (1 - fy) * fx) + gather_corner(y0 + 1, x0, fy * (1 - fx)) + gather_corner(y0 + 1, x0 + 1, fy * fx)
            sampled = sampled * mask[:, None]
            out = jnp.einsum('bckhw,ock->bohw', sampled, w.reshape(CO, C, K2))
            return out + b[None, :, None, None]
        y = _deform_conv(x, w_om, b_om, w, b)
        scale = (gamma / jnp.sqrt(bn_var + EPS))[None, :, None, None]
        y = (y - bn_mean[None, :, None, None]) * scale + beta[None, :, None, None]
        return jax.nn.relu(y)

    def _L2_conv_ref(x, W_enc, b_enc, log_dt, A_log_real, A_imag, C_real, C_imag, D, W_glu, b_glu, ln_gamma, ln_beta, W_dec, b_dec):
        import jax, jax.numpy as jnp
        import numpy as np
        import math
        BATCH, SEQ, HH, WW = (32, 32, 32, 32)
        D_MODEL = 256
        N2 = 4
        L_MAX = 16

        def _layernorm(x, gamma, beta, eps=1e-05):
            mu = jnp.mean(x, axis=-1, keepdims=True)
            var = jnp.var(x, axis=-1, keepdims=True)
            return (x - mu) * jax.lax.rsqrt(var + eps) * gamma + beta
        Bsz, S, Hh, Ww = x.shape
        L = Hh * Ww
        u = x.reshape(Bsz, S, L)
        h = jnp.einsum('bdl,de->ble', u, W_enc) + b_enc
        dt = jnp.exp(log_dt)
        A = -jnp.exp(A_log_real) + 1j * A_imag
        Cc = C_real + 1j * C_imag
        dtA = A * dt[:, None]
        Bd = (jnp.exp(dtA) - 1.0) / A
        t = jnp.arange(L_MAX)
        vand = jnp.exp(dtA[:, :, None] * t)
        K = 2.0 * jnp.einsum('dn,dnl->dl', Cc * Bd, vand).real
        z = jnp.swapaxes(h, 1, 2)
        n_fft = L + L_MAX
        y = jnp.fft.irfft(jnp.fft.rfft(z, n=n_fft) * jnp.fft.rfft(K, n=n_fft), n=n_fft)[..., :L]
        y = y + D[:, None] * z
        y = jax.nn.gelu(jnp.swapaxes(y, 1, 2))
        g = y @ W_glu + b_glu
        g = g[..., :D_MODEL] * jax.nn.sigmoid(g[..., D_MODEL:])
        h = _layernorm(h + g, ln_gamma, ln_beta)
        out = h @ W_dec + b_dec
        out = jnp.swapaxes(out, 1, 2).reshape(Bsz, S, Hh, Ww)
        return out

    def _L3_conv_ref(x, dw_w, dw_b, ln_g, ln_b, w1, b1, w2, b2, ls):
        import jax, jax.numpy as jnp
        import numpy as np
        C = 32
        HID = 4 * C
        K = 7
        PAD = K // 2
        B, T, F = (4, 128, 32)
        LN_EPS = 1e-05
        LS_INIT = 0.01
        y = jax.lax.conv_general_dilated(x, dw_w, window_strides=(1, 1), padding=[(PAD, PAD), (PAD, PAD)], feature_group_count=x.shape[1], dimension_numbers=('NCHW', 'OIHW', 'NCHW'))
        y = y + dw_b[None, :, None, None]
        y = jnp.transpose(y, (0, 2, 3, 1))
        mu = jnp.mean(y, axis=-1, keepdims=True)
        var = jnp.mean(jnp.square(y - mu), axis=-1, keepdims=True)
        y = (y - mu) * jax.lax.rsqrt(var + LN_EPS) * ln_g + ln_b
        h = jax.nn.gelu(jnp.einsum('btfc,hc->btfh', y, w1) + b1)
        y = jnp.einsum('btfh,ch->btfc', h, w2) + b2
        y = y * ls
        return jnp.transpose(y, (0, 3, 1, 2))

    def _gn(v, G=32, eps=1e-05):
        B_, C_, H_, W_ = v.shape
        g = v.reshape(B_, G, C_ // G, H_, W_)
        m = jnp.mean(g, axis=(2, 3, 4), keepdims=True)
        s = jnp.var(g, axis=(2, 3, 4), keepdims=True)
        return ((g - m) / jnp.sqrt(s + eps)).reshape(v.shape)

    def _ln_c(v, eps=1e-06):
        m = jnp.mean(v, axis=1, keepdims=True)
        s = jnp.var(v, axis=1, keepdims=True)
        return (v - m) / jnp.sqrt(s + eps)

    def _ln_t(v, eps=1e-05):
        m = jnp.mean(v, axis=-1, keepdims=True)
        s = jnp.var(v, axis=-1, keepdims=True)
        return (v - m) / jnp.sqrt(s + eps)

    def _to_tokens(v):
        B_, C_, H_, W_ = v.shape
        return v.reshape(B_, C_, H_ * W_).transpose(0, 2, 1)

    def _from_tokens(t, like):
        B_, C_, H_, W_ = like.shape
        return t.transpose(0, 2, 1).reshape(B_, C_, H_, W_)
    x = x + _L0_conv_ref(_gn(x), L0_conv_router_w, L0_conv_w1, L0_conv_w2)
    x = x + _L1_conv_ref(_gn(x), L1_conv_w_om, L1_conv_b_om, L1_conv_w, L1_conv_b, L1_conv_gamma, L1_conv_beta, L1_conv_bn_mean, L1_conv_bn_var)
    x = x + _L2_conv_ref(_gn(x), L2_conv_W_enc, L2_conv_b_enc, L2_conv_log_dt, L2_conv_A_log_real, L2_conv_A_imag, L2_conv_C_real, L2_conv_C_imag, L2_conv_D, L2_conv_W_glu, L2_conv_b_glu, L2_conv_ln_gamma, L2_conv_ln_beta, L2_conv_W_dec, L2_conv_b_dec)
    x = x + _L3_conv_ref(_gn(x), L3_conv_dw_w, L3_conv_dw_b, L3_conv_ln_g, L3_conv_ln_b, L3_conv_w1, L3_conv_b1, L3_conv_w2, L3_conv_b2, L3_conv_ls)
    return x

_drawn_inputs = setup_inputs


def setup_inputs(seed=0):
    import zlib

    import numpy as np

    out = dict(_drawn_inputs(seed))
    spreads = {'L2_conv_b_enc': (0.0, 0.1),
     'L2_conv_A_log_real': (-0.6931471824645996, 0.6),
     'L2_conv_b_glu': (0.0, 0.287),
     'L2_conv_ln_gamma': (1.0, 0.2),
     'L2_conv_ln_beta': (0.0, 0.1),
     'L2_conv_b_dec': (0.0, 0.1),
     'L3_conv_dw_b': (0.0, 0.8),
     'L3_conv_ln_g': (1.0, 0.6),
     'L3_conv_ln_b': (0.0, 0.8),
     'L3_conv_b1': (0.0, 2.0),
     'L3_conv_b2': (0.0, 2.0),
     'L3_conv_ls': (0.009999999776482582, 0.6)}
    factors = {'L1_conv_b': 8.0, 'L3_conv_dw_w': 8.0, 'L3_conv_w1': 8.0, 'L3_conv_w2': 8.0}
    for name, (base, spread) in spreads.items():
        noise = np.random.default_rng([zlib.crc32(name.encode()), seed]).standard_normal(out[name].shape)
        drawn = base * np.exp(spread * noise) if base else spread * noise
        out[name] = jnp.asarray(drawn.astype(out[name].dtype))
    for name, factor in factors.items():
        out[name] = (out[name] * factor).astype(out[name].dtype)
    return out
```

```python
from contextlib import ExitStack

import numpy as np

import concourse.bass as bass
from concourse import mybir

B, C, H, W = 16, 32, 32, 32
P = 128
GI = P // C
NS = B // GI
HW = H * W
HALF = 512
EPS = 1e-5
PT = 2
NE = 8
HID = 256
TOK = (H // PT) * (W // PT)
D0 = C * PT * PT
NU = GI * NE
KK = 9
OMC = 3 * GI * KK
PW = W + 2
TQ = 9
TROWS = TQ * P
TRING = 3
PADLEN = 1200
NT = HW // P
DM = 256
NB2 = DM // P
NST = 4
LM = 16
JJ = 4
UL = LM + HW + 4
K7 = 7
FROM = 1
PW3 = W + K7 - 1

F32 = mybir.dt.float32
I32 = mybir.dt.int32
U32 = mybir.dt.uint32
ALU = mybir.AluOpType
ACT = mybir.ActivationFunctionType
AX = mybir.AxisListType


def columns(fields):
    at, out = 0, {}
    for name, n in fields:
        out[name] = (at, at + n)
        at += n
    return out, at


PARAMS, NPARAM = columns([
    ("l1_b", 1), ("l1_gamma", 1), ("l1_beta", 1), ("l1_mean", 1), ("l1_var", 1), ("b_dec", 1),
    ("dw_b", 1), ("ln3_g", 1), ("ln3_b", 1), ("b2", 1), ("ls", 1), ("dw", K7 * K7), ("b1", 1),
    ("b_enc", NB2), ("log_dt", NB2), ("a_real", NB2 * NST), ("a_imag", NB2 * NST),
    ("c_real", NB2 * NST), ("c_imag", NB2 * NST), ("d", NB2), ("b_glu", 2 * NB2),
    ("ln2_g", NB2), ("ln2_b", NB2), ("w_enc_t", NB2 * C), ("b_om", OMC), ("router", NE),
])
CONSTS, NCONST = columns([
    ("ident", P), ("image_row", GI * KK), ("mean32", P), ("mean256", P),
    ("rank", NE),
])
WEIGHTS, NWEIGHT = columns([
    ("w_om", KK * OMC), ("w_dcn", 3 * C), ("w_glu", NB2 * 2 * DM), ("w_dec", NB2 * P),
    ("w1_3", P), ("w2_3", C),
])


class Banks:

    def __init__(self, full, free, plan):
        self.full, self.free = full, free
        self.where, self.per = {}, {}
        for name, bank in plan:
            self.where[name] = (bank, self.per.get(bank, 0))
            self.per[bank] = self.per.get(bank, 0) + 1

    def bank(self, name):
        return self.where[name][0]

    def vacant(self, eng, s, name):
        b, k = self.where[name]
        eng.wait_ge(self.free[b], FROM + s * self.per[b] + k)

    def filled(self, eng, s, name):
        b, k = self.where[name]
        eng.wait_ge(self.full[b], FROM + s * self.per[b] + k + 1)

    def read(self, eng, s, name):
        b, k = self.where[name]
        eng.wait_ge(self.free[b], FROM + s * self.per[b] + k + 1)

    def last_step_filled(self, eng, s, bank):
        eng.wait_ge(self.full[bank], FROM + s * self.per[bank])


class Chain:

    def __init__(self, eng, sem):
        self.eng, self.sem, self.n = eng, sem, 0

    def did(self, op):
        op.then_inc(self.sem, 1)
        self.n += 1
        return self.n

    def wait(self, n=None):
        self.eng.wait_ge(self.sem, self.n if n is None else n)

    def then(self, op):
        self.did(op)
        self.wait()

    def restart(self):
        self.wait()
        self.eng.sem_clear(self.sem)
        self.n = 0


def plan_l0():
    plan = [("router", 2)]
    for u in range(NU):
        plan += [(("gate", u), 0), (("value", u), 1)]
        if u:
            plan.append((("out", u - 1), 2))
    return plan + [(("out", NU - 1), 2), (("back", 0), 0), (("back", 1), 1)]


def plan_l1():
    plan = [(("omc", 0), 3), (("omc", 1), 4), (("om", 0), 3), (("om", 1), 4)]
    plan += [(("table", q), 3 + q % 2) for q in range(TQ)]
    for half in range(2):
        plan.append((("dcn", half), 4))
        plan += [(("sampled", half * 4 + j, g), 3) for j in range(4) for g in range(GI)]
    return plan


def plan_l2():
    names = []
    for n in range(2):
        for g in range(GI):
            names += [("y", n, g, 0), ("y", n, g, 1)]
            for d in range(NB2):
                names += [("gb", n, g, d), ("ga", n, g, d), ("z", n, g, d)]
        names += [("dec", n), ("mu", n), ("sq", n)]
    names += [("mu3", 0), ("mu3", 1), ("sq3", 0), ("sq3", 1)]
    for n in range(2):
        names += [("hid", n, g) for g in range(GI)] + [("mlp", n)]
    return [(name, 5 + i % 3) for i, name in enumerate(names)]


def build(nc, x, w1, w2, w_enc, params, consts, weights, places, out):
    x_v = x.rearrange("(s b) c h w -> (b c) s (h w)", s=NS)
    out_v = out.rearrange("(s b) c h w -> (b c) s (h w)", s=NS)
    table = nc.dram_tensor("corner_table", (GI * TROWS, 4 * C), F32, kind="Internal").ap()

    with ExitStack() as ctx:
        def sb(name, shape, dt=F32):
            return ctx.enter_context(nc.sbuf_tensor(name, shape, dt))

        def sem(name):
            return ctx.enter_context(nc.semaphore(name))

        psum = [ctx.enter_context(nc.psum_tensor(f"bank{b}", [P, HALF], F32)) for b in range(8)]
        full = [sem(f"bank{b}_full") for b in range(8)]
        free = [sem(f"bank{b}_free") for b in range(8)]
        B0, B1, B2 = (Banks(full, free, plan) for plan in (plan_l0(), plan_l1(), plan_l2()))

        par = sb("par", [P, NPARAM])
        cst = sb("cst", [P, NCONST])
        wts = sb("wts", [P, NWEIGHT])
        w1_sb = sb("w1_sb", [P, NE, 4, P])
        w2_sb = sb("w2_sb", [P, NE, 2, P])
        wenc = sb("wenc", [C, DM])

        def prm(name):
            a, b = PARAMS[name]
            return par[:, a:b]

        def con(name):
            a, b = CONSTS[name]
            return cst[:, a:b]

        def wt(name):
            a, b = WEIGHTS[name]
            return wts[:, a:b]

        ident = con("ident")
        w_om = wt("w_om").rearrange("p (k m) -> p k m", k=KK)
        w_dcn = wt("w_dcn").rearrange("p (b m) -> p b m", b=3)
        w_glu = wt("w_glu").rearrange("p (k m) -> p k m", k=NB2)
        w_dec4 = wt("w_dec").rearrange("p (k m) -> p k m", k=NB2)

        X = sb("X", [P, NS, HW])
        bst = sb("bst", [P, 4, 2, 6])
        mv = sb("mv", [P, 4, 2])
        std = sb("std", [P, 4])
        rs = sb("rs", [P, 4])
        epst = sb("epst", [P, 1])

        xp = sb("xp", [P, GI, TOK])
        lg = sb("lg", [P, 8, NE])
        ex = sb("ex", [P, 8, NE])
        m1 = sb("m1", [P, 8])
        oh = sb("oh", [P, 8, NE])
        oh2 = sb("oh2", [P, 8, NE])
        gate = sb("gate", [P, 8, NE])
        he = sb("he", [P, 2, HALF])
        acc = sb("acc", [P, 2, PT * PT, GI, C])
        xn0 = acc[:, :, :, :, :].rearrange("p t a g c -> p (t a g c)").rearrange("p (a b n) -> p a b n", a=PT, b=PT)

        xpad = sb("xpad", [P, PADLEN])
        bb = sb("bb", [P, NT, OMC])
        om = sb("om", [P, NT, OMC])
        fr = sb("fr", [P, NT, 2 * GI * KK])
        mk = sb("mk", [P, NT, GI * KK])
        mk1 = sb("mk1", [P, NT, GI * KK])
        idf = sb("idf", [P, NT, GI * KK])
        idx = sb("idx", [P, NT, GI * KK], U32)
        cw = sb("cw", [P, NT, GI * KK, 4])
        cwf = cw[:, :, :, :].rearrange("p t k a -> p t (k a)")
        fi = cwf[:, :, 0:2 * GI * KK].bitcast(I32)
        fl = cwf[:, :, 2 * GI * KK:4 * GI * KK]
        tb = sb("tb", [P, TRING, GI, 4 * C])
        gt = sb("gt", [P, GI, KK, 4, C])
        sm = sb("sm", [P, 2, 3 * P])
        st = sb("st", [P, GI, 3 * P])
        omt = st[:, :, :].rearrange("p g m -> p (g m)")[:, 0:HW]
        r1 = sb("r1", [P, HALF])
        sc1 = sb("sc1", [P, 1])
        bi1 = sb("bi1", [P, 1])

        u4 = sb("u4", [P, GI, UL])
        wk = sb("wk", [P, JJ, NB2, P])
        corr = sb("corr", [LM, NB2, P])
        yg = sb("yg", [P, 2, NB2, HALF])
        tg = sb("tg", [P, 2, HALF])
        ae = sb("ae", [P, 2, HALF])
        rb = sb("rb", [P, GI, NB2, HALF])
        sqb = sb("sqb", [P, GI, NB2, HALF])
        xn2 = sqb[:, GI - 1].rearrange("p d n -> p (d n)")
        musq = sb("musq", [P, HALF])
        var2 = sb("var2", [P, HALF])
        hb_glu = sb("hb_glu", [P, 2 * NB2])
        wdp = sb("wdp", [P, NB2, C])
        wg2 = sb("wg2", [P, NB2, C])
        dconst = sb("dconst", [P, 1])
        s4 = {n: sb("s4" + n, [P, NB2, NST]) for n in
              ("ea", "ar", "am", "ra", "zr", "zi", "hr", "hi", "t1", "t2", "t3", "t4", "wr", "wi", "er", "ei",
               "cr", "ci")}
        dt_t = sb("dt_t", [P, NB2])
        gflat = gt[:, :, :, :, :].rearrange("p g k a c -> p (g k a c)")
        nv = NB2 * NST * LM
        vr = gflat[:, 0:nv].rearrange("p (d n l) -> p d n l", d=NB2, n=NST)
        vi = gflat[:, nv:2 * nv].rearrange("p (d n l) -> p d n l", d=NB2, n=NST)
        kw = gflat[:, 2 * nv:2 * nv + NB2 * LM * C].rearrange("p (d l s) -> p d l s", d=NB2, l=LM)
        v1 = sb("v1", [P, NB2, NST, LM // 2])
        v2 = sb("v2", [P, NB2, NST, LM // 2])
        kr = sb("kr", [P, 4, NB2, LM])
        cum = sb("cum", [P, 2, NB2, LM])
        cor = sb("cor", [P, NB2, LM])
        cb15 = sb("cb15", [P, NB2])

        xp3 = sb("xp3", [P, PW3 * PW3])
        rbf = rb[:, :, :, :].rearrange("p g d n -> p (g d n)")
        sqf = sqb[:, :, :, :].rearrange("p g d n -> p (g d n)")
        ya = rbf[:, 0:2 * HW].rearrange("p (i n) -> p i n", i=2)
        yc, ysq = sqf[:, 0:HW], sqf[:, HW:2 * HW]
        hg = yg[:, :, :, :].rearrange("p a d n -> p (a d) n")
        t3 = (musq, var2)

        xpad_v = xpad[:, 0:PW * PW].rearrange("p (y x) -> p y x", y=PW)
        xp3_v = xp3[:, :].rearrange("p (y x) -> p y x", y=PW3)

        names = """x_in par_in wts_in w1_in w2_in zeros_set exp_done a_inv s4_done wg_done cm_done
            k_turned k_there dec_there s1_var s1_std s1_there
            var_ready0 var_ready1 var_ready2 var_ready3 std_ready0 std_ready1 std_ready2 std_ready3
            xn0_ready xp_in max_ready exp_ready
            xpad_ready om_ready mask_ready idx_ready smp_ready st_used x1_added
            u_ready u_in glu_done sq_ready var2_ready std2_ready x2_added
            y3_ready ysq_ready yn_ready x3_ready out_done
            dve_chain act_chain pool_chain held""".split()
        S = {n: sem(n) for n in names}
        table_out = [sem(f"table_out{t}") for t in range(TRING)]
        gathered = [sem(f"gathered{g}") for g in range(GI)]

        block = ctx.enter_context(nc.Block())

        def hold(eng):
            eng.sem_inc(S["held"])

        @block.sync
        def _(sp):
            sp.dma_start(X[:, :, :], x_v).then_inc(S["x_in"], 16)
            sp.dma_start(par[:, :], params).then_inc(S["par_in"], 16)
            sp.dma_start(cst[:, :], consts).then_inc(S["par_in"], 16)
            sp.dma_start(wenc[:, :], w_enc).then_inc(S["par_in"], 16)
            sp.dma_start(bb[:, :, :].rearrange("p t m -> p (t m)"), places).then_inc(S["par_in"], 16)
            sp.dma_start(w1_sb[:, :, :, :].rearrange("p e b m -> p (e b m)"), w1).then_inc(S["w1_in"], 16)
            sp.dma_start(w2_sb[:, :, :, :].rearrange("p e b m -> p (e b m)"), w2).then_inc(S["w2_in"], 16)
            sp.dma_start(wts[:, :], weights).then_inc(S["wts_in"], 16)
            for started in [S["xp_in"], S["u_in"]] + table_out:
                sp.sem_inc(started, FROM)
            sp.wait_ge(S["zeros_set"], 1)
            with sp.Fori(0, NS) as s:
                sp.wait_ge(S["xn0_ready"], s + 1)
                hold(sp)
                B0.last_step_filled(sp, s, 1)
                hold(sp)
                for dyx in range(PT * PT):
                    for g in range(GI):
                        sp.dma_start(xp[dyx * C:(dyx + 1) * C, g, :],
                                     xn0[g * C:(g + 1) * C, dyx // PT, dyx % PT, :]).then_inc(S["xp_in"], 16)
                sp.wait_ge(S["smp_ready"], FROM + s * NT * GI)
                hold(sp)
                rows = table.rearrange("(g q p) e -> q p g e", g=GI, p=P)
                for t in range(TQ):
                    B1.read(sp, s, ("table", t))
                    hold(sp)
                    sp.dma_start(rows[t], tb[:, t % TRING]).then_inc(table_out[t % TRING], 16)
                sp.wait_ge(S["u_ready"], s + 1)
                hold(sp)
                B2.last_step_filled(sp, s, 5)
                hold(sp)
                for g in range(GI):
                    for j in range(JJ):
                        sp.dma_start(u4[j * C:(j + 1) * C, g, LM + j:LM + j + HW],
                                     xn2[g * C:(g + 1) * C, :]).then_inc(S["u_in"], 16)
                for n in range(2):
                    sp.wait_ge(S["x3_ready"], s * 2 + n + 1)
                    hold(sp)
                    sp.dma_start(out_v[:, bass.ds(s, 1), n * HALF:(n + 1) * HALF],
                                 X[:, bass.ds(s, 1), n * HALF:(n + 1) * HALF]).then_inc(S["out_done"], 16)
            sp.wait_ge(S["out_done"], 16 * 2 * NS)

        @block.gpsimd
        def _(pool):
            ch = Chain(pool, S["pool_chain"])
            pool.memset(u4[:, :, :], 0.0)
            pool.memset(xp3[:, :], 0.0)
            pool.memset(xpad[:, :], 0.0)
            pool.memset(sm[:, :, :], 0.0).then_inc(S["zeros_set"], 1)

            def mul(o, a, b):
                ch.did(pool.tensor_tensor(o, a, b, ALU.mult))

            def add(o, a, b, op=ALU.add):
                ch.did(pool.tensor_tensor(o, a, b, op))

            def cmul(ore, oim, ar, ai, br, bi, ta, tb_):
                mul(ta[0], ar, br)
                mul(ta[1], ai, bi)
                mul(tb_[0], ar, bi)
                mul(tb_[1], ai, br)
                ch.wait()
                add(ore, ta[0], ta[1], ALU.subtract)
                add(oim, tb_[0], tb_[1])
                ch.wait()

            q = {n: t[:, :, :] for n, t in s4.items()}
            ta, tb_ = (q["t1"], q["t2"]), (q["t3"], q["t4"])
            pool.wait_ge(S["a_inv"], 1)
            pool.wait_ge(S["par_in"], 64)
            a_im = prm("a_imag").rearrange("p (d n) -> p d n", d=NB2)
            dt_b = dt_t[:, :].unsqueeze(2).to_broadcast([P, NB2, NST])
            mul(q["t1"], q["ar"], dt_b)
            mul(q["t2"], a_im, dt_b)
            ch.wait()
            ch.did(pool.tensor_scalar(q["zr"], q["t1"], 2.0 ** -6, None, ALU.mult))
            ch.did(pool.tensor_scalar(q["zi"], q["t2"], 2.0 ** -6, None, ALU.mult))
            ch.did(pool.memset(q["hr"], 1.0))
            ch.did(pool.memset(q["hi"], 0.0))
            ch.wait()
            for k in range(9, 1, -1):
                cmul(q["wr"], q["wi"], q["zr"], q["zi"], q["hr"], q["hi"], ta, tb_)
                ch.did(pool.tensor_scalar(q["hr"], q["wr"], 1.0 / k, 1.0, ALU.mult, ALU.add))
                ch.did(pool.tensor_scalar(q["hi"], q["wi"], 1.0 / k, None, ALU.mult))
                ch.wait()
            cmul(q["wr"], q["wi"], q["zr"], q["zi"], q["hr"], q["hi"], ta, tb_)
            for _ in range(6):
                ch.did(pool.tensor_scalar(q["hr"], q["wr"], 2.0, None, ALU.add))
                ch.wait()
                cmul(q["er"], q["ei"], q["wr"], q["wi"], q["hr"], q["wi"], ta, tb_)
                ch.did(pool.tensor_copy(q["wr"], q["er"]))
                ch.did(pool.tensor_copy(q["wi"], q["ei"]))
                ch.wait()
            ch.did(pool.tensor_scalar(q["er"], q["wr"], 1.0, None, ALU.add))
            ch.did(pool.tensor_scalar(q["hi"], a_im, -1.0, None, ALU.mult))
            ch.wait()
            cmul(q["zr"], q["zi"], q["wr"], q["wi"], q["ar"], q["hi"], ta, tb_)
            mul(q["hr"], q["zr"], q["ra"])
            mul(q["wr"], q["zi"], q["ra"])
            ch.wait()
            c_re = prm("c_real").rearrange("p (d n) -> p d n", d=NB2)
            c_im = prm("c_imag").rearrange("p (d n) -> p d n", d=NB2)
            cmul(vr[:, :, :, 0], vi[:, :, :, 0], c_re, c_im, q["hr"], q["wr"], ta, tb_)
            er, ei, nr, ni = q["er"], q["wi"], q["cr"], q["ci"]
            m = 1
            while m < LM:
                eb = er.unsqueeze(3).to_broadcast([P, NB2, NST, m])
                ib = ei.unsqueeze(3).to_broadcast([P, NB2, NST, m])
                for d in range(NB2):
                    mul(v1[:, d, :, 0:m], vr[:, d, :, 0:m], eb[:, d])
                    mul(v2[:, d, :, 0:m], vi[:, d, :, 0:m], ib[:, d])
                    ch.wait()
                    add(vr[:, d, :, m:2 * m], v1[:, d, :, 0:m], v2[:, d, :, 0:m], ALU.subtract)
                    ch.wait()
                    mul(v1[:, d, :, 0:m], vr[:, d, :, 0:m], ib[:, d])
                    mul(v2[:, d, :, 0:m], vi[:, d, :, 0:m], eb[:, d])
                    ch.wait()
                    add(vi[:, d, :, m:2 * m], v1[:, d, :, 0:m], v2[:, d, :, 0:m])
                    ch.wait()
                m *= 2
                if m < LM:
                    cmul(nr, ni, er, ei, er, ei, ta, tb_)
                    er, ei, nr, ni = nr, ni, er, ei
            add(kr[:, 0], vr[:, :, 0], vr[:, :, 1])
            add(kr[:, 1], vr[:, :, 2], vr[:, :, 3])
            ch.wait()
            add(kr[:, 2], kr[:, 0], kr[:, 1])
            ch.wait()
            ch.did(pool.tensor_scalar(kr[:, 3], kr[:, 2], 2.0, None, ALU.mult))
            ch.wait()
            add(kr[:, 3, :, 0], kr[:, 3, :, 0], prm("d"))
            ch.wait()
            src, dst, sh = kr[:, 3], cum[:, 0], 1
            while sh < LM:
                ch.did(pool.tensor_copy(dst[:, :, 0:sh], src[:, :, 0:sh]))
                add(dst[:, :, sh:LM], src[:, :, sh:LM], src[:, :, 0:LM - sh])
                ch.wait()
                src, dst, sh = dst, cum[:, 1] if sh in (1, 4) else cum[:, 0], sh * 2
            b_enc = prm("b_enc")
            mul(cb15[:, :], src[:, :, LM - 1], b_enc)
            add(kr[:, 0], src, src[:, :, LM - 1:LM].to_broadcast([P, NB2, LM]), ALU.subtract)
            ch.wait()
            mul(cor[:, :, :], kr[:, 0], b_enc.unsqueeze(2).to_broadcast([P, NB2, LM]))
            enc_t = prm("w_enc_t").rearrange("p (d s) -> p d s", d=NB2)
            for d in range(NB2):
                mul(kw[:, d], enc_t[:, d].unsqueeze(1).to_broadcast([P, LM, C]),
                    kr[:, 3, d].unsqueeze(2).to_broadcast([P, LM, C]))
            ch.wait()
            pool.memset(q["t1"], 0.0).then_inc(S["s4_done"], 1)

            with pool.Fori(0, NS) as s:
                pool.wait_ge(S["idx_ready"], s + 1)
                for t in range(TRING):
                    pool.wait_ge(table_out[t], FROM + (s + 1) * 16 * (TQ // TRING))
                for j in range(NT):
                    for g in range(GI):
                        pool.wait_ge(S["smp_ready"], FROM + s * NT * GI + (j - 1) * GI + g + 1 if j else FROM + s * NT * GI)
                        hold(pool)
                        for k in range(KK):
                            pool.indirect_dma_start(
                                gt[:, g, k].rearrange("p a c -> p (a c)"), None, table,
                                bass.IndirectOffsetOnAxis(ap=idx[:, j, g * KK + k:g * KK + k + 1], axis=0),
                            ).then_inc(gathered[g], 16)

        @block.scalar
        def _(act):
            act.wait_ge(S["par_in"], 64)
            act.activation(dt_t[:, :], prm("log_dt"), ACT.Exp)
            act.activation(s4["ea"][:, :, :], prm("a_real").rearrange("p (d n) -> p d n", d=NB2), ACT.Exp)\
               .then_inc(S["exp_done"], 1)
            act.activation(hb_glu[:, :], prm("b_glu"), ACT.Copy, scale=0.5).then_inc(S["act_chain"], 1)
            act.wait_ge(S["s1_var"], 1)
            act.activation(std[:, 0:1], epst[:, :], ACT.Sqrt).then_inc(S["s1_std"], 1)
            act.wait_ge(S["k_turned"], 1)
            act.activation(wk[:, 0:2].rearrange("p t d m -> p (t d m)"), psum[5][:, :], ACT.Copy)
            act.wait_ge(S["k_turned"], 2)
            act.activation(wk[:, 2:4].rearrange("p t d m -> p (t d m)"), psum[6][:, :], ACT.Copy)
            act.wait_ge(S["k_turned"], 3)
            act.activation(corr[:, :, :].rearrange("p d m -> p (d m)"), psum[7][0:LM, 0:NB2 * P], ACT.Copy)\
               .then_inc(S["k_there"], 1)
            act.wait_ge(S["s1_there"], 1)
            act.wait_ge(S["act_chain"], 1)

            def root(s, layer):
                act.wait_ge(S[f"var_ready{layer}"], s + 1)
                act.activation(std[:, layer:layer + 1], mv[:, layer, 1:2], ACT.Sqrt, bias=epst[:, :])\
                   .then_inc(S[f"std_ready{layer}"], 1)

            def l0_head(s):
                root(s, 0)
                act.wait_ge(S["max_ready"], s + 1)
                act.activation(ex[:, :, :], lg[:, :, :], ACT.Exp).then_inc(S["exp_ready"], 1)

            def l0_unit(s, u):
                B0.filled(act, s, ("gate", u))
                if u >= 2:
                    B0.filled(act, s, ("out", u - 2))
                act.activation(he[:, u % 2], psum[0][:, :], ACT.Tanh, scale=0.5).then_inc(free[0], 1)

            def l1_head(s):
                root(s, 1)
                B1.last_step_filled(act, s, 3)
                B1.last_step_filled(act, s, 4)
                for n in range(2):
                    B1.filled(act, s, ("omc", n))
                    act.activation(omt[0:OMC, n * HALF:(n + 1) * HALF], psum[3 + n][0:OMC, :], ACT.Copy)\
                       .then_inc(free[3 + n], 1)
                for t in range(TQ):
                    name = ("table", t)
                    B1.filled(act, s, name)
                    b = B1.bank(name)
                    act.wait_ge(table_out[t % TRING], FROM + s * 16 * (TQ // TRING) + 16 * (t // TRING))
                    act.activation(tb[:, t % TRING].rearrange("p g (a c) -> p a g c", a=4),
                                   psum[b][:, :].rearrange("p (a g c) -> p a g c", a=4, g=GI), ACT.Copy)\
                       .then_inc(free[b], 1)
                act.wait_ge(S["om_ready"], s + 1)
                act.activation(mk[:, :, :], om[:, :, 2 * GI * KK:OMC], ACT.Tanh, scale=0.5)\
                   .then_inc(S["mask_ready"], 1)

            def l1_tile(s, j):
                for g in range(GI):
                    B1.filled(act, s, ("sampled", j, g))
                    if g == 0:
                        if j % 4:
                            act.wait_ge(S["st_used"], s * 6 + j // 4 * 3 + j % 4)
                        elif j:
                            B1.filled(act, s, ("dcn", 0))
                        else:
                            B1.last_step_filled(act, s, 4)
                    act.activation(st[:, g], psum[3][:, 0:3 * P], ACT.Copy).then_inc(free[3], 1)
                if j % 4 == 3:
                    n = j // 4
                    B1.filled(act, s, ("dcn", n))
                    act.wait_ge(S["x1_added"], FROM + s * 2 + n)
                    act.activation(r1[:, :], psum[4][:, :], ACT.Relu, bias=bi1[:, :], scale=sc1[:, :])\
                       .then_inc(free[4], 1)

            def l2_chunk(s, n, g):
                c = n * GI + g
                for d in range(NB2):
                    name = ("y", n, g, d)
                    B2.filled(act, s, name)
                    if c >= 2:
                        B2.filled(act, s, ("ga", (c - 2) // GI, (c - 2) % GI, NB2 - 1))
                    act.activation(yg[:, c % 2, d], psum[B2.bank(name)][:, :], ACT.Gelu_apprx_tanh,
                                   bias=cb15[:, d:d + 1]).then_inc(free[B2.bank(name)], 1)
                for d in range(NB2):
                    if c:
                        B2.read(act, s, ("z", (c - 1) // GI, (c - 1) % GI, d))
                    b = B2.bank(("gb", n, g, d))
                    B2.filled(act, s, ("gb", n, g, d))
                    act.activation(tg[:, d], psum[b][:, :], ACT.Tanh, scale=0.5,
                                   bias=hb_glu[:, NB2 + d:NB2 + d + 1]).then_inc(free[b], 1)
                    b = B2.bank(("ga", n, g, d))
                    B2.filled(act, s, ("ga", n, g, d))
                    act.activation(ae[:, d], psum[b][:, :], ACT.Identity, scale=0.5,
                                   bias=hb_glu[:, d:d + 1]).then_inc(free[b], 1)
                for d in range(NB2):
                    B2.read(act, s, ("z", n, g, d))
                    if n:
                        B2.filled(act, s, ("sq", 0))
                    else:
                        B2.last_step_filled(act, s, 5)
                    act.activation(sqb[:, g, d], rb[:, g, d], ACT.Square).then_inc(S["sq_ready"], 1)

            def l2_close(s, n):
                B2.filled(act, s, ("mu", n))
                b = B2.bank(("mu", n))
                act.activation(musq[:, :], psum[b][:, :], ACT.Square).then_inc(free[b], 1)
                act.wait_ge(S["var2_ready"], s * 2 + n + 1)
                act.activation(var2[:, :], var2[:, :], ACT.Sqrt, bias=epst[:, :]).then_inc(S["std2_ready"], 1)

            def l3(s):
                root(s, 3)
                for n in range(2):
                    B2.read(act, s, ("mu3", n))
                    act.activation(ysq[:, n * HALF:(n + 1) * HALF], yc[:, n * HALF:(n + 1) * HALF], ACT.Square)\
                       .then_inc(S["ysq_ready"], 1)
                for n in range(2):
                    B2.filled(act, s, ("sq3", n))
                    b = B2.bank(("sq3", n))
                    act.activation(ysq[:, n * HALF:(n + 1) * HALF], psum[b][:, :], ACT.Sqrt, bias=epst[:, :])\
                       .then_inc(free[b], 1)
                for n in range(2):
                    for g in range(GI):
                        B2.filled(act, s, ("hid", n, g))
                        if n and g == 0:
                            B2.filled(act, s, ("mlp", 0))
                        b = B2.bank(("hid", n, g))
                        act.activation(hg[:, g], psum[b][:, :], ACT.Gelu_apprx_tanh, bias=prm("b1"))\
                           .then_inc(free[b], 1)

            with act.Fori(0, NS) as s:
                l0_head(s)
                for u in range(NU):
                    l0_unit(s, u)
                l1_head(s)
                for j in range(NT):
                    l1_tile(s, j)
                root(s, 2)
                for n in range(2):
                    for g in range(GI):
                        l2_chunk(s, n, g)
                    l2_close(s, n)
                l3(s)

        @block.vector
        def _(dve):
            ch = Chain(dve, S["dve_chain"])
            for started in (S["smp_ready"], S["x1_added"]):
                dve.sem_inc(started, FROM)
            tt, ts, stt = dve.tensor_tensor, dve.tensor_scalar, dve.scalar_tensor_tensor
            dve.wait_ge(S["par_in"], 64)
            ts(epst[:, :], prm("l1_var"), EPS, None, ALU.add).then_inc(S["s1_var"], 1)
            dve.wait_ge(S["exp_done"], 1)
            a_im = prm("a_imag").rearrange("p (d n) -> p d n", d=NB2)
            ch.did(ts(s4["ar"][:, :, :], s4["ea"][:, :, :], -1.0, None, ALU.mult))
            ch.did(tt(s4["am"][:, :, :], s4["ea"][:, :, :], s4["ea"][:, :, :], ALU.mult))
            ch.then(tt(s4["t1"][:, :, :], a_im, a_im, ALU.mult))
            ch.then(tt(s4["am"][:, :, :], s4["am"][:, :, :], s4["t1"][:, :, :], ALU.add))
            dve.reciprocal(s4["ra"][:, :, :], s4["am"][:, :, :]).then_inc(S["a_inv"], 1)
            dve.wait_ge(S["s1_std"], 1)
            ch.then(dve.reciprocal(rs[:, 0:1], std[:, 0:1]))
            ch.did(tt(sc1[:, :], rs[:, 0:1], prm("l1_gamma"), ALU.mult))
            ch.then(tt(bi1[:, :], prm("l1_b"), prm("l1_mean"), ALU.subtract))
            ch.then(stt(out=bi1[:, :], in0=bi1[:, :], scalar=sc1[:, 0:1], in1=prm("l1_beta"),
                        op0=ALU.mult, op1=ALU.add))
            dve.memset(epst[:, :], EPS).then_inc(S["s1_there"], 1)
            ch.did(tt(bb[:, :, :], bb[:, :, :], prm("b_om").unsqueeze(1).to_broadcast([P, NT, OMC]), ALU.add))
            dve.wait_ge(S["wts_in"], 16)
            for d in range(NB2):
                op = ts(wg2[:, d], w_dec4[:, d, 0:C], prm("ln2_g")[:, d:d + 1], None, ALU.mult)
                if d:
                    op.then_inc(S["wg_done"], 1)
            dve.wait_ge(S["wg_done"], 1)
            dve.wait_ge(S["cm_done"], 1)
            ch.did(tt(wdp[:, :, :], wg2[:, :, :],
                      psum[4][:, 0:C].unsqueeze(1).to_broadcast([P, NB2, C]), ALU.subtract))
            dve.wait_ge(S["cm_done"], 2)
            tt(dconst[:, :], psum[3][:, 0:1], prm("b_dec"), ALU.add).then_inc(S["dec_there"], 1)
            dve.wait_ge(S["zeros_set"], 1)
            dve.wait_ge(S["x_in"], 16)
            dve.wait_ge(S["dec_there"], 1)
            ch.restart()

            def norm(s, layer):
                for n in range(2):
                    ch.did(dve.bn_stats(bst[:, layer, n], X[:, bass.ds(s, 1), n * HALF:(n + 1) * HALF]
                                        .rearrange("p o n -> p (o n)")))
                ch.wait()
                dve.bn_aggr(mv[:, layer], bst[:, layer].rearrange("p a b -> p (a b)"))\
                   .then_inc(S[f"var_ready{layer}"], 1)
                dve.wait_ge(S[f"std_ready{layer}"], s + 1)
                ch.then(dve.reciprocal(rs[:, layer:layer + 1], std[:, layer:layer + 1]))
                return mv[:, layer, 0:1], rs[:, layer:layer + 1]

            def l0_head(s):
                mean, r = norm(s, 0)
                dve.wait_ge(S["xp_in"], FROM + s * 256)
                xv = X[:, bass.ds(s, 1), :].rearrange("p o (h a w b) -> p (o h) a w b", a=PT, b=PT, w=W // PT)
                for dy in range(PT):
                    for dx in range(PT):
                        op = ts(xn0[:, dy, dx].rearrange("p (h w) -> p h w", h=H // PT), xv[:, :, dy, :, dx],
                                mean, r, ALU.subtract, ALU.mult)
                        if dy and dx:
                            op.then_inc(S["xn0_ready"], 1)
                        else:
                            ch.did(op)
                B0.filled(dve, s, "router")
                logit = psum[2][:, 0:8 * NE].rearrange("p (t e) -> p t e", t=8)
                ch.then(dve.tensor_reduce(m1[:, :], logit, AX.X, ALU.max))

                def over(v):
                    return v[:, :].unsqueeze(2).to_broadcast([P, 8, NE])
                tt(lg[:, :, :], logit, over(m1), ALU.subtract).then_inc(free[2], 1)
                B0.read(dve, s, "router")
                rank = con("rank").unsqueeze(1).to_broadcast([P, 8, NE])

                def first_max(o, src):
                    ch.then(dve.tensor_reduce(m1[:, :], src, AX.X, ALU.max))
                    ch.then(tt(o, src, over(m1), ALU.is_equal))
                    ch.then(tt(o, o, rank, ALU.mult))
                    ch.then(dve.tensor_reduce(m1[:, :], o, AX.X, ALU.max))
                    ch.then(tt(o, o, over(m1), ALU.is_equal))
                ch.then(ts(gate[:, :, :], lg[:, :, :], 1.0, None, ALU.mult))
                dve.memset(m1[:, :], 0.0).then_inc(S["max_ready"], 1)
                dve.wait_ge(S["max_ready"], s + 1)
                first_max(oh[:, :, :], gate[:, :, :])
                ch.then(stt(out=gate[:, :, :], in0=oh[:, :, :], scalar=-1e30, in1=gate[:, :, :],
                            op0=ALU.mult, op1=ALU.add))
                first_max(oh2[:, :, :], gate[:, :, :])
                ch.then(tt(oh[:, :, :], oh[:, :, :], oh2[:, :, :], ALU.add))
                dve.wait_ge(S["exp_ready"], s + 1)
                ch.then(tt(gate[:, :, :], ex[:, :, :], oh[:, :, :], ALU.mult))
                ch.then(dve.tensor_reduce(m1[:, :], gate[:, :, :], AX.X, ALU.add))
                ch.then(dve.reciprocal(m1[:, :], m1[:, :]))
                ch.then(stt(out=gate[:, :, :], in0=gate[:, :, :], scalar=0.5, in1=over(m1),
                            op0=ALU.mult, op1=ALU.mult))

            def l0_he(s, u):
                B0.filled(dve, s, ("value", u))
                B0.read(dve, s, ("gate", u))
                stt(out=he[:, u % 2], in0=he[:, u % 2], scalar=1.0, in1=psum[1][:, :],
                    op0=ALU.add, op1=ALU.mult).then_inc(free[1], 1)

            def l0_acc(s, u):
                g, e = divmod(u, NE)
                B0.filled(dve, s, ("out", u))
                if e:
                    B0.read(dve, s, ("out", u - 1))
                for t in range(2):
                    sc = gate[:, g * 2 + t, e:e + 1]
                    o = psum[2][:, t * D0:(t + 1) * D0].rearrange("p (a c) -> p a c", c=C)
                    a = acc[:, t, :, g]
                    if e:
                        op = stt(out=a, in0=o, scalar=sc, in1=a, op0=ALU.mult, op1=ALU.add)
                    else:
                        op = ts(a, o, sc, None, ALU.mult)
                    if t:
                        op.then_inc(free[2], 1)

            def l0_tail(s):
                for t in range(2):
                    B0.filled(dve, s, ("back", t))
                    for dy in range(PT):
                        xv = X[:, bass.ds(s, 1), :].rearrange("p o (h a w b) -> p (o h) a b w", a=PT, b=PT,
                                                              w=W // PT)
                        xv = xv[:, t * 8:(t + 1) * 8, dy].rearrange("p h b w -> p b h w")
                        bk = psum[t][:, dy * 2 * P:(dy + 1) * 2 * P].rearrange("p (b h w) -> p b h w", b=PT, h=8)
                        op = tt(xv, xv, bk, ALU.add)
                        if dy:
                            op.then_inc(free[t], 1)
                        else:
                            ch.did(op)
                B0.read(dve, s, ("back", 0))
                B0.read(dve, s, ("back", 1))
                hold(dve)

            def l1_head(s):
                mean, r = norm(s, 1)
                B1.last_step_filled(dve, s, 3)
                B1.last_step_filled(dve, s, 4)
                xv = X[:, bass.ds(s, 1), :].rearrange("p o (h w) -> p (o h) w", w=W)
                ts(xpad_v[:, 1:H + 1, 1:W + 1], xv, mean, r, ALU.subtract, ALU.mult).then_inc(S["xpad_ready"], 1)
                for n in range(2):
                    B1.filled(dve, s, ("om", n))
                    tt(om[:, n * 4:(n + 1) * 4], psum[3 + n][:, 0:4 * OMC].rearrange("p (t m) -> p t m", t=4),
                       bb[:, n * 4:(n + 1) * 4], ALU.add).then_inc(free[3 + n], 1)
                B1.read(dve, s, ("om", 0))
                B1.read(dve, s, ("om", 1))
                NXY = 2 * GI * KK
                pos = om[:, :, 0:NXY]
                ts(pos, pos, 0.0, float(H + 1), ALU.max, ALU.min).then_inc(S["om_ready"], 1)
                dve.wait_ge(S["om_ready"], s + 1)
                ch.then(dve.tensor_copy(fi[:, :, :], pos))
                ch.then(dve.tensor_copy(fl[:, :, :], fi[:, :, :]))
                ch.then(tt(fr[:, :, :], fl[:, :, :], pos, ALU.is_gt))
                ch.then(tt(fl[:, :, :], fl[:, :, :], fr[:, :, :], ALU.subtract))
                ch.then(ts(fl[:, :, :], fl[:, :, :], float(H), None, ALU.min))
                NK = GI * KK
                ch.did(tt(fr[:, :, :], pos, fl[:, :, :], ALU.subtract))
                ch.then(stt(out=idf[:, :, :], in0=fl[:, :, 0:NK], scalar=float(PW), in1=fl[:, :, NK:NXY],
                            op0=ALU.mult, op1=ALU.add))
                tt(idx[:, :, :], idf[:, :, :], con("image_row").unsqueeze(1).to_broadcast([P, NT, NK]),
                   ALU.add).then_inc(S["idx_ready"], 1)
                dve.wait_ge(S["mask_ready"], s + 1)
                ch.then(ts(mk1[:, :, :], mk[:, :, :], 0.5, 0.5, ALU.mult, ALU.add))
                fy, fx = fr[:, :, 0:NK], fr[:, :, NK:NXY]
                ch.then(tt(mk[:, :, :], mk1[:, :, :], fy, ALU.mult))
                ch.did(tt(cw[:, :, :, 3], mk[:, :, :], fx, ALU.mult))
                ch.then(tt(mk1[:, :, :], mk1[:, :, :], mk[:, :, :], ALU.subtract))
                ch.did(tt(cw[:, :, :, 2], mk[:, :, :], cw[:, :, :, 3], ALU.subtract))
                ch.then(tt(cw[:, :, :, 1], mk1[:, :, :], fx, ALU.mult))
                ch.then(tt(cw[:, :, :, 0], mk1[:, :, :], cw[:, :, :, 1], ALU.subtract))

            def l1_tile(s, j):
                for g in range(GI):
                    u = j * GI + g
                    dve.wait_ge(gathered[g], (s * NT + j + 1) * 16 * KK)
                    rows = gt[:, g].rearrange("p k a c -> p (k a) c")
                    share = cw[:, j, g * KK:(g + 1) * KK].rearrange("p k a -> p (k a)")
                    ch.then(tt(rows, rows, share.unsqueeze(2).to_broadcast([P, 4 * KK, C]), ALU.mult))
                    ch.then(tt(gt[:, g, :, 0:2], gt[:, g, :, 0:2], gt[:, g, :, 2:4], ALU.add))
                    if u >= 2:
                        B1.filled(dve, s, ("sampled", (u - 2) // GI, (u - 2) % GI))
                    else:
                        B1.last_step_filled(dve, s, 3)
                    tt(sm[:, u % 2, 0:KK * C].rearrange("p (k c) -> p k c", k=KK), gt[:, g, :, 0], gt[:, g, :, 1],
                       ALU.add).then_inc(S["smp_ready"], 1)
                if j % 4 == 3:
                    n = j // 4
                    B1.read(dve, s, ("dcn", n))
                    xh = X[:, bass.ds(s, 1), n * HALF:(n + 1) * HALF].rearrange("p o n -> p (o n)")
                    tt(xh, xh, r1[:, :], ALU.add).then_inc(S["x1_added"], 1)

            def l2_head(s):
                dve.wait_ge(S["x1_added"], FROM + s * 2 + 2)
                hold(dve)
                mean, r = norm(s, 2)
                dve.wait_ge(S["u_in"], FROM + s * 256)
                xv = X[:, bass.ds(s, 1), :].rearrange("p o n -> p (o n)")
                ts(xn2[:, :], xv, mean, r, ALU.subtract, ALU.mult).then_inc(S["u_ready"], 1)

            def l2_chunk(s, n, g):
                for d in range(NB2):
                    B2.read(dve, s, ("ga", n, g, d))
                    stt(out=tg[:, d], in0=tg[:, d], scalar=1.0, in1=ae[:, d], op0=ALU.add, op1=ALU.mult)\
                        .then_inc(S["glu_done"], 1)
                    dve.wait_ge(S["glu_done"], s * 8 * NB2 + (n * GI + g) * NB2 + d + 1)
                    B2.filled(dve, s, ("z", n, g, d))
                    if n:
                        B2.filled(dve, s, ("sq", 0))
                        dve.wait_ge(S["sq_ready"], s * 8 * NB2 + GI * NB2)
                    else:
                        B2.last_step_filled(dve, s, 5)
                    b = B2.bank(("z", n, g, d))
                    stt(out=rb[:, g, d], in0=psum[b][:, :], scalar=prm("b_enc")[:, d:d + 1], in1=tg[:, d],
                        op0=ALU.add, op1=ALU.add).then_inc(free[b], 1)

            def l2_close(s, n):
                b = B2.bank(("sq", n))
                B2.filled(dve, s, ("sq", n))
                B2.read(dve, s, ("mu", n))
                tt(var2[:, :], psum[b][:, :], musq[:, :], ALU.subtract).then_inc(S["var2_ready"], 1)
                dve.wait_ge(S["std2_ready"], s * 2 + n + 1)
                ch.then(dve.reciprocal(var2[:, :], var2[:, :]))
                B2.filled(dve, s, ("dec", n))
                b = B2.bank(("dec", n))
                ch.then(tt(musq[:, :], psum[b][:, :], var2[:, :], ALU.mult))
                xh = X[:, bass.ds(s, 1), n * HALF:(n + 1) * HALF].rearrange("p o n -> p (o n)")
                ch.then(stt(out=xh, in0=musq[:, :], scalar=dconst[:, 0:1], in1=xh, op0=ALU.add, op1=ALU.add))
                dve.memset(m1[:, 0:1], 0.0).then_inc(free[b], 1)
                B2.read(dve, s, ("dec", n))
                dve.memset(m1[:, 0:1], 0.0).then_inc(free[B2.bank(("sq", n))], 1)

            def l3(s):
                B2.read(dve, s, ("sq", 1))
                hold(dve)
                mean, r = norm(s, 3)
                xv = X[:, bass.ds(s, 1), :].rearrange("p o (h w) -> p (o h) w", w=W)
                pd = K7 // 2
                ch.then(ts(xp3_v[:, pd:pd + H, pd:pd + W], xv, mean, r, ALU.subtract, ALU.mult))
                taps = prm("dw")
                yv = [ya[:, i].rearrange("p (h w) -> p h w", h=H) for i in range(2)]
                last = [0, 0]
                for t in range(K7 * K7):
                    win = xp3_v[:, t // K7:t // K7 + H, t % K7:t % K7 + W]
                    a = t % 2
                    if t == 0:
                        op = ts(yv[0], win, taps[:, 0:1], prm("dw_b"), ALU.mult, ALU.add)
                    elif t == 1:
                        op = ts(yv[1], win, taps[:, 1:2], None, ALU.mult)
                    else:
                        ch.wait(last[a])
                        op = stt(out=yv[a], in0=win, scalar=taps[:, t:t + 1], in1=yv[a], op0=ALU.mult, op1=ALU.add)
                    last[a] = ch.did(op)
                ch.wait()
                tt(ya[:, 0], ya[:, 0], ya[:, 1], ALU.add).then_inc(S["y3_ready"], 1)
                dve.wait_ge(S["y3_ready"], s + 1)
                for n in range(2):
                    h = slice(n * HALF, (n + 1) * HALF)
                    B2.filled(dve, s, ("mu3", n))
                    b = B2.bank(("mu3", n))
                    tt(yc[:, h], ya[:, 0, h], psum[b][:, :], ALU.subtract).then_inc(free[b], 1)
                for n in range(2):
                    h = slice(n * HALF, (n + 1) * HALF)
                    B2.read(dve, s, ("sq3", n))
                    B2.read(dve, s, ("mu3", n))
                    ch.then(dve.reciprocal(ysq[:, h], ysq[:, h]))
                    ch.then(tt(yc[:, h], yc[:, h], ysq[:, h], ALU.mult))
                    ts(yc[:, h], yc[:, h], prm("ln3_g"), prm("ln3_b"), ALU.mult, ALU.add)\
                        .then_inc(S["yn_ready"], 1)
                for n in range(2):
                    B2.filled(dve, s, ("mlp", n))
                    b = B2.bank(("mlp", n))
                    ts(t3[n][:, :], psum[b][:, :], prm("b2"), prm("ls"), ALU.add, ALU.mult).then_inc(free[b], 1)
                    B2.read(dve, s, ("mlp", n))
                    xh = X[:, bass.ds(s, 1), n * HALF:(n + 1) * HALF].rearrange("p o n -> p (o n)")
                    tt(xh, xh, t3[n][:, :], ALU.add).then_inc(S["x3_ready"], 1)

            with dve.Fori(0, NS) as s:
                l0_head(s)
                for u in range(NU):
                    l0_he(s, u)
                    if u:
                        l0_acc(s, u - 1)
                l0_acc(s, NU - 1)
                l0_tail(s)
                l1_head(s)
                for j in range(NT):
                    l1_tile(s, j)
                l2_head(s)
                for n in range(2):
                    for g in range(GI):
                        l2_chunk(s, n, g)
                    l2_close(s, n)
                l3(s)
                ch.restart()

        @block.tensor
        def _(pe):
            mm = pe.matmul
            for started in full + free:
                pe.sem_inc(started, FROM)
            pe.wait_ge(S["par_in"], 64)
            pe.wait_ge(S["wts_in"], 16)
            pe.wait_ge(S["wg_done"], 1)
            for d in range(NB2):
                op = mm(psum[4][:, 0:C], con("mean256"), wg2[:, d], start=d == 0, stop=d == NB2 - 1)
            op.then_inc(S["cm_done"], 1)
            for d in range(NB2):
                op = mm(psum[3][:, 0:1], w_dec4[:, d], prm("ln2_b")[:, d:d + 1], start=d == 0, stop=d == NB2 - 1)
            op.then_inc(S["cm_done"], 1)
            pe.wait_ge(S["s4_done"], 1)
            for t in range(JJ):
                for d in range(NB2):
                    op = pe.transpose(psum[5 + t // 2][:, (t % 2 * NB2 + d) * P:(t % 2 * NB2 + d + 1) * P],
                                      kw[:, d, t * JJ:(t + 1) * JJ].rearrange("p j s -> p (j s)"), ident)
                if t % 2:
                    op.then_inc(S["k_turned"], 1)
            for d in range(NB2):
                op = pe.transpose(psum[7][0:LM, d * P:(d + 1) * P], cor[:, d], ident)
            op.then_inc(S["k_turned"], 1)
            pe.wait_ge(S["k_there"], 1)
            pe.wait_ge(S["dec_there"], 1)
            pe.wait_ge(S["w1_in"], 16)
            pe.wait_ge(S["w2_in"], 16)

            def l0_head(s):
                pe.wait_ge(S["xp_in"], FROM + s * 256 + 256)
                B0.vacant(pe, s, "router")
                for t in range(8):
                    op = mm(psum[2][:, t * NE:(t + 1) * NE], xp[:, t // 2, t % 2 * P:(t % 2 + 1) * P],
                            prm("router"), start=True, stop=True)
                op.then_inc(full[2], 1)

            def l0_h(s, u):
                g, e = divmod(u, NE)
                for kind, b, first in (("gate", 0, 2), ("value", 1, 0)):
                    B0.vacant(pe, s, (kind, u))
                    for h in range(2):
                        op = mm(psum[b][:, h * TOK:(h + 1) * TOK], w1_sb[:, e, first + h], xp[:, g],
                                start=True, stop=True)
                    op.then_inc(full[b], 1)

            def l0_out(s, u):
                g, e = divmod(u, NE)
                B0.read(pe, s, ("value", u))
                B0.vacant(pe, s, ("out", u))
                for t in range(2):
                    for h in range(2):
                        op = mm(psum[2][:, t * D0:(t + 1) * D0],
                                he[:, u % 2, h * TOK + t * P:h * TOK + (t + 1) * P], w2_sb[:, e, h],
                                start=h == 0, stop=h == 1)
                op.then_inc(full[2], 1)

            def l0_tail(s):
                B0.read(pe, s, ("out", NU - 1))
                for t in range(2):
                    B0.vacant(pe, s, ("back", t))
                    for dyx in range(4):
                        op = pe.transpose(psum[t][:, dyx * P:(dyx + 1) * P], acc[:, t, dyx].rearrange("p g c -> p (g c)"),
                                          ident)
                    op.then_inc(full[t], 1)

            def l1_head(s):
                pe.wait_ge(S["xpad_ready"], s + 1)
                for n in range(2):
                    B1.vacant(pe, s, ("omc", n))
                    for k in range(KK):
                        y0 = n * (H // 2) + k // 3
                        op = mm(psum[3 + n][0:OMC, :], w_om[:, k],
                                xpad_v[:, y0:y0 + H // 2, k % 3:k % 3 + W], start=k == 0, stop=k == KK - 1)
                    op.then_inc(full[3 + n], 1)
                for n in range(2):
                    B1.vacant(pe, s, ("om", n))
                    for t in range(4):
                        at = (n * 4 + t) * P
                        op = pe.transpose(psum[3 + n][:, t * OMC:(t + 1) * OMC], omt[0:OMC, at:at + P],
                                          ident[0:OMC, 0:OMC])
                    op.then_inc(full[3 + n], 1)
                for t in range(TQ):
                    B1.vacant(pe, s, ("table", t))
                    b = B1.bank(("table", t))
                    for a in range(4):
                        at = t * P + a // 2 * PW + a % 2
                        op = pe.transpose(psum[b][:, a * P:(a + 1) * P], xpad[:, at:at + P], ident)
                    op.then_inc(full[b], 1)

            def l1_tile(s, j):
                for g in range(GI):
                    u = j * GI + g
                    pe.wait_ge(S["smp_ready"], FROM + s * NT * GI + u + 1)
                    B1.vacant(pe, s, ("sampled", j, g))
                    for k in range(3):
                        op = pe.transpose(psum[3][:, k * P:(k + 1) * P], sm[:, u % 2, k * P:(k + 1) * P], ident)
                    op.then_inc(full[3], 1)
                if j % 4 == 0:
                    B1.vacant(pe, s, ("dcn", j // 4))
                B1.read(pe, s, ("sampled", j, GI - 1))
                for k in range(3):
                    for g in range(GI):
                        op = mm(psum[4][g * C:(g + 1) * C, j % 4 * P:(j % 4 + 1) * P], w_dcn[:, k],
                                st[:, g, k * P:(k + 1) * P], start=k == 0, stop=k == 2)
                op.then_inc(full[4] if j % 4 == 3 else S["st_used"], 1)

            def l2_chunk(s, n, g):
                if n == 0 and g == 0:
                    pe.wait_ge(S["u_in"], FROM + s * 256 + 256)
                c = n * GI + g
                for d in range(NB2):
                    name = ("y", n, g, d)
                    B2.vacant(pe, s, name)
                    o = psum[B2.bank(name)]
                    for t in range(JJ):
                        at = LM + n * HALF - JJ * t
                        op = mm(o[:, :], wk[:, t, d], u4[:, g, at:at + HALF], start=t == 0,
                                stop=t == JJ - 1 and n > 0)
                    if n == 0:
                        op = mm(o[:, 0:LM], corr[:, d], ident[0:LM, 0:LM], start=False, stop=True)
                    op.then_inc(full[B2.bank(name)], 1)
                B2.read(pe, s, ("y", n, g, NB2 - 1))
                B2.read(pe, s, ("y", n, g, 0))
                for d in range(NB2):
                    for kind, col in (("gb", DM), ("ga", 0)):
                        name = (kind, n, g, d)
                        B2.vacant(pe, s, name)
                        for k in range(NB2):
                            op = mm(psum[B2.bank(name)][:, :], w_glu[:, k, col + d * P:col + (d + 1) * P],
                                    yg[:, c % 2, k], start=k == 0, stop=k == NB2 - 1)
                        op.then_inc(full[B2.bank(name)], 1)
                    name = ("z", n, g, d)
                    B2.vacant(pe, s, name)
                    mm(psum[B2.bank(name)][:, :], wenc[:, d * P:(d + 1) * P],
                       u4[0:C, g, LM + n * HALF:LM + (n + 1) * HALF], start=True, stop=True)\
                        .then_inc(full[B2.bank(name)], 1)

            def l2_close(s, n):
                pe.wait_ge(S["sq_ready"], s * 8 * NB2 + (n + 1) * GI * NB2)
                B2.read(pe, s, ("z", n, GI - 1, NB2 - 1))
                B2.read(pe, s, ("z", n, GI - 1, 0))
                for kind, weight, src in (("dec", wdp, rb), ("mu", None, rb), ("sq", None, sqb)):
                    b = B2.bank((kind, n))
                    B2.vacant(pe, s, (kind, n))
                    for d in range(NB2):
                        for g in range(GI):
                            lhs = weight[:, d] if weight is not None else con("mean256")[:, 0:C]
                            op = mm(psum[b][g * C:(g + 1) * C, :], lhs, src[:, g, d], start=d == 0,
                                    stop=d == NB2 - 1)
                    op.then_inc(full[b], 1)

            def l3(s):
                pe.wait_ge(S["y3_ready"], s + 1)
                for n in range(2):
                    b = B2.bank(("mu3", n))
                    B2.vacant(pe, s, ("mu3", n))
                    mm(psum[b][:, :], con("mean32"), ya[:, 0, n * HALF:(n + 1) * HALF], start=True, stop=True)\
                        .then_inc(full[b], 1)
                for n in range(2):
                    pe.wait_ge(S["ysq_ready"], s * 2 + n + 1)
                    b = B2.bank(("sq3", n))
                    B2.vacant(pe, s, ("sq3", n))
                    mm(psum[b][:, :], con("mean32"), ysq[:, n * HALF:(n + 1) * HALF], start=True, stop=True)\
                        .then_inc(full[b], 1)
                for n in range(2):
                    pe.wait_ge(S["yn_ready"], s * 2 + n + 1)
                    for g in range(GI):
                        b = B2.bank(("hid", n, g))
                        B2.vacant(pe, s, ("hid", n, g))
                        mm(psum[b][:, :], wt("w1_3")[g * C:(g + 1) * C, :], yc[g * C:(g + 1) * C, n * HALF:(n + 1) * HALF],
                           start=True, stop=True).then_inc(full[b], 1)
                    b = B2.bank(("mlp", n))
                    B2.vacant(pe, s, ("mlp", n))
                    B2.read(pe, s, ("hid", n, GI - 1))
                    B2.read(pe, s, ("hid", n, GI - 2))
                    for g in range(GI):
                        op = mm(psum[b][g * C:(g + 1) * C, :], wt("w2_3"), hg[:, g], start=True, stop=True)
                    op.then_inc(full[b], 1)

            with pe.Fori(0, NS) as s:
                l0_head(s)
                l0_h(s, 0)
                for u in range(1, NU):
                    l0_h(s, u)
                    l0_out(s, u - 1)
                l0_out(s, NU - 1)
                l0_tail(s)
                l1_head(s)
                for j in range(NT):
                    l1_tile(s, j)
                for n in range(2):
                    for g in range(GI):
                        l2_chunk(s, n, g)
                    l2_close(s, n)
                l3(s)


def shape_constants():
    c = np.zeros((P, NCONST), np.float32)

    def put(name, a):
        lo, hi = CONSTS[name]
        c[:, lo:hi] = a.reshape(P, hi - lo)
    put("ident", np.eye(P, dtype=np.float32))
    put("image_row", np.broadcast_to(np.repeat(np.arange(GI) * TROWS, KK).astype(np.float32), (P, GI * KK)))
    put("mean32", np.kron(np.eye(GI), np.full((C, C), 1.0 / C)).astype(np.float32))
    put("mean256", np.full((P, P), 1.0 / DM, np.float32))
    put("rank", np.broadcast_to(np.arange(NE, 0, -1).astype(np.float32), (P, NE)))
    return c


def tap_places():
    base = np.zeros((P, NT, 3, GI, KK), np.float32)
    p, t, k = np.arange(P)[:, None, None], np.arange(NT)[None, :, None], np.arange(KK)[None, None, :]
    base[:, :, 0] = (t * (P // W) + p // W + k // 3)[:, :, None]
    base[:, :, 1] = (p % W + k % 3 + 0 * t)[:, :, None]
    return base.reshape(P, NT * OMC)


def lay_out(a):
    f = {n: np.asarray(v) for n, v in a.items()}
    L0, L1, L2, L3 = (f"L{i}_conv_" for i in range(4))

    def patch(w, axis):
        w = np.moveaxis(w, axis, 0)
        w = w.reshape((C, PT, PT) + w.shape[1:])
        w = np.moveaxis(w, 0, 2)
        return np.moveaxis(w.reshape((D0,) + w.shape[3:]), 0, axis)

    w1 = patch(f[L0 + "w1"], 1).transpose(1, 0, 2).reshape(P, NE * 4 * P)
    w2 = patch(f[L0 + "w2"], 2).reshape(NE, 2, P, D0).transpose(2, 0, 1, 3).reshape(P, NE * 2 * P)
    params = np.zeros((P, NPARAM), np.float32)

    def put(name, v):
        lo, hi = PARAMS[name]
        params[:, lo:hi] = v.reshape(P, hi - lo)

    def by_image(v):
        return np.concatenate([v.reshape(C, -1)] * GI, axis=0)

    def by_state(v):
        return v.reshape(NB2, P, -1).transpose(1, 0, 2)
    for name, src in (("l1_b", L1 + "b"), ("l1_gamma", L1 + "gamma"), ("l1_beta", L1 + "beta"),
                      ("l1_mean", L1 + "bn_mean"), ("l1_var", L1 + "bn_var"), ("b_dec", L2 + "b_dec"),
                      ("dw_b", L3 + "dw_b"), ("ln3_g", L3 + "ln_g"), ("ln3_b", L3 + "ln_b"),
                      ("b2", L3 + "b2"), ("ls", L3 + "ls"), ("dw", L3 + "dw_w")):
        put(name, by_image(f[src]))
    put("b1", f[L3 + "b1"])
    for name, src in (("b_enc", "b_enc"), ("log_dt", "log_dt"), ("a_real", "A_log_real"), ("a_imag", "A_imag"),
                      ("c_real", "C_real"), ("c_imag", "C_imag"), ("d", "D"), ("ln2_g", "ln_gamma"),
                      ("ln2_b", "ln_beta")):
        put(name, by_state(f[L2 + src]))
    put("b_glu", f[L2 + "b_glu"].reshape(2 * NB2, P).T)
    put("w_enc_t", f[L2 + "W_enc"].T.reshape(NB2, P, C).transpose(1, 0, 2))
    kinds = [list(range(0, 2 * KK, 2)), list(range(1, 2 * KK, 2)), list(range(2 * KK, 3 * KK))]
    b_om = np.stack([f[L1 + "b_om"][k] for k in kinds])
    put("b_om", np.broadcast_to(b_om[:, None], (3, GI, KK)).reshape(1, OMC).repeat(P, 0))
    put("router", patch(f[L0 + "router_w"], 0))

    weights = np.zeros((P, NWEIGHT), np.float32)

    def put_w(name, v):
        lo, hi = WEIGHTS[name]
        weights[:, lo:hi] = v.reshape(P, hi - lo)
    w_om = np.zeros((GI, C, KK, 3, GI, KK), np.float32)
    per = np.stack([f[L1 + "w_om"][k] for k in kinds]).reshape(3, KK, C, KK)
    for g in range(GI):
        w_om[g, :, :, :, g] = per.transpose(2, 3, 0, 1)
    put_w("w_om", w_om)
    w_dcn = np.zeros((3 * P, C), np.float32)
    w_dcn[:KK * C] = f[L1 + "w"].reshape(C, C, KK).transpose(2, 1, 0).reshape(KK * C, C)
    put_w("w_dcn", w_dcn.reshape(3, P, C).transpose(1, 0, 2))
    put_w("w_glu", f[L2 + "W_glu"].reshape(NB2, P, 2 * DM).transpose(1, 0, 2))
    w_dec = f[L2 + "W_dec"].reshape(NB2, P, C).transpose(1, 0, 2)
    put_w("w_dec", np.concatenate([w_dec] * GI, axis=2))
    put_w("w1_3", np.concatenate([f[L3 + "w1"].T] * GI, axis=0))
    put_w("w2_3", f[L3 + "w2"].T)
    return {"x": f["x"], "w1": w1, "w2": w2, "w_enc": f[L2 + "W_enc"], "params": params,
            "consts": shape_constants(), "weights": weights,
            "places": tap_places()}


def kernel(**inputs):
    import concourse.bacc as _bacc
    from concourse.bass_utils import run_bass_kernel_spmd as _run

    nc = _bacc.Bacc("TRN2", target_bir_lowering=False, num_devices=1)
    arrays = {k: np.ascontiguousarray(v) for k, v in lay_out(inputs).items()}
    args = [nc.dram_tensor(name, a.shape, mybir.dt.from_np(a.dtype), kind="ExternalInput").ap()
            for name, a in arrays.items()]
    out = nc.dram_tensor("out", (B, C, H, W), F32, kind="ExternalOutput").ap()
    build(nc, *args, out)
    r = _run(nc, [arrays], core_ids=[0])
    return r.results[0]["out"]
```

```python
from contextlib import ExitStack

import numpy as np

import concourse.bass as bass
from concourse import mybir

B, C, H, W = 16, 32, 32, 32
P = 128
GI = P // C
NS = B // GI
HW = H * W
HALF = 512
EPS = 1e-5
PT = 2
NE = 8
HID = 256
TOK = (H // PT) * (W // PT)
D0 = C * PT * PT
NU = GI * NE
KK = 9
OMC = 3 * GI * KK
PW = W + 2
TQ = 9
TROWS = TQ * P
TRING = 2
PADLEN = 1200
NT = HW // P
DM = 256
NB2 = DM // P
NST = 4
LM = 16
JJ = 4
UL = LM + HW + 4
K7 = 7
A_PLACES = [(0, 2, 6), (2, 17, 8), (17, 24, NU + 2 - 14), (24, 28, 5 + TQ - 2)]
C_PLACES = [(0, 1, 1), (2, 17, 18), (17, 17.5, 1), (17.5, 29, K7 * K7), (29, 31.5, 3)]
HEAD_PLACE, SWAP_PLACE = 28, 28.5
FROM = 1
PW3 = W + K7 - 1

F32 = mybir.dt.float32
I32 = mybir.dt.int32
U32 = mybir.dt.uint32
ALU = mybir.AluOpType
ACT = mybir.ActivationFunctionType
AX = mybir.AxisListType


def columns(fields):
    at, out = 0, {}
    for name, n in fields:
        out[name] = (at, at + n)
        at += n
    return out, at


PARAMS, NPARAM = columns([
    ("l1_b", 1), ("l1_gamma", 1), ("l1_beta", 1), ("l1_mean", 1), ("l1_var", 1), ("b_dec", 1),
    ("dw_b", 1), ("ln3_g", 1), ("ln3_b", 1), ("b2", 1), ("ls", 1), ("dw", K7 * K7), ("b1", 1),
    ("b_enc", NB2), ("log_dt", NB2), ("a_real", NB2 * NST), ("a_imag", NB2 * NST),
    ("c_real", NB2 * NST), ("c_imag", NB2 * NST), ("d", NB2), ("b_glu", 2 * NB2),
    ("ln2_g", NB2), ("ln2_b", NB2), ("w_enc_t", NB2 * C), ("b_om", OMC), ("router", NE),
])
CONSTS, NCONST = columns([
    ("ident", P), ("image_row", GI * KK), ("mean32", P), ("mean256", P),
    ("rank", NE),
])
WEIGHTS, NWEIGHT = columns([
    ("w_om", KK * OMC), ("w_dcn", 3 * C), ("w_glu", NB2 * 2 * DM), ("w_dec", NB2 * P),
    ("w1_3", P), ("w2_3", C),
])


class Banks:

    def __init__(self, full, free, plan):
        self.full, self.free = full, free
        self.where, self.per = {}, {}
        for name, bank in plan:
            self.where[name] = (bank, self.per.get(bank, 0))
            self.per[bank] = self.per.get(bank, 0) + 1

    def bank(self, name):
        return self.where[name][0]

    def vacant(self, eng, s, name):
        b, k = self.where[name]
        eng.wait_ge(self.free[b], FROM + s * self.per[b] + k)

    def filled(self, eng, s, name):
        b, k = self.where[name]
        eng.wait_ge(self.full[b], FROM + s * self.per[b] + k + 1)

    def read(self, eng, s, name):
        b, k = self.where[name]
        eng.wait_ge(self.free[b], FROM + s * self.per[b] + k + 1)

    def last_step_filled(self, eng, s, bank):
        eng.wait_ge(self.full[bank], FROM + s * self.per[bank])


class Chain:

    def __init__(self, eng, sem):
        self.eng, self.sem, self.n = eng, sem, 0

    def did(self, op):
        op.then_inc(self.sem, 1)
        self.n += 1
        return self.n

    def wait(self, n=None):
        self.eng.wait_ge(self.sem, self.n if n is None else n)

    def then(self, op):
        self.did(op)
        self.wait()

    def restart(self):
        self.wait()
        self.eng.sem_clear(self.sem)
        self.n = 0


def plan_a():
    plan = [("router", 2)]
    for u in range(NU):
        plan += [(("gate", u), 0), (("value", u), 1)]
        if u:
            plan.append((("out", u - 1), 2))
    plan += [(("out", NU - 1), 2), (("back", 0), 0), (("back", 1), 1)]
    head = [("omc", 0), ("omc", 1), ("table", 0), ("table", 1), ("om", 0), ("om", 1)]
    head += [("table", t) for t in range(2, TQ)]
    return plan + [(name, (i + 2) % 3) for i, name in enumerate(head)]


def plan_b():
    plan = []
    for half in range(2):
        plan.append((("dcn", half), 4))
        plan += [(("sampled", half * 4 + j, g), 3) for j in range(4) for g in range(GI)]
    return plan


def plan_c():
    names = []
    for kind, *k in order_c():
        if kind == "l2_y":
            names += [("y", k[0], d) for d in range(NB2)]
        elif kind == "l2_glu":
            for d in range(NB2):
                names += [("gb", k[0], d), ("ga", k[0], d), ("z", k[0], d)]
        elif kind == "l2_close":
            names += [(x, k[0]) for x in ("dec", "mu", "sq")]
    names += [("mu3", 0), ("mu3", 1), ("sq3", 0), ("sq3", 1)]
    for n in range(2):
        names += [("hid", n, g) for g in range(GI)] + [("mlp", n)]
    return [(name, 5 + i % 3) for i, name in enumerate(names)]


def order_a():
    parts = [("l0_unit", u) for u in range(NU + 1)] + [("l0_tail",), ("l1_norm",), ("l1_conv",), ("l1_om",)]
    return parts + [("l1_index",), ("l1_share",)] + [("l1_table", t) for t in range(2, TQ)]


def order_b():
    parts = []
    for t in range(NT * GI + 1):
        if t:
            parts.append((t, "turn", t - 1))
        if t and t % GI == 0:
            parts.append((t, "dcn", t // GI - 1))
        if t < NT * GI:
            parts.append((t, "sample", t))
    return parts


def order_c():
    parts = [("l2_head",), ("l2_y", 0)]
    for c in range(2 * GI):
        if c < 2 * GI - 1:
            parts.append(("l2_y", c + 1))
        parts.append(("l2_glu", c))
        if c % GI == GI - 1:
            parts.append(("l2_close", c // GI))
    parts.append(("l3_head",))
    parts += [("tap", t) for t in range(K7 * K7)]
    return parts + [("l3_norm",), ("l3_mlp", 0), ("l3_mlp", 1)]


def spread(stage, parts, places):
    out, parts = [], list(parts)
    for lo, hi, n in places:
        for i in range(n):
            out.append((lo + (i + 0.5) * (hi - lo) / n, stage, *parts.pop(0)))
    assert not parts
    return out


def order(a, b, c):
    if not b and a:
        parts = [("head", "l0_head"), ("a", "weights")] + [("a", *x) for x in order_a()]
        parts.insert(parts.index(("a", "l1_index")), ("a", "s4d"))
        return parts + [("a", "swap", 0), ("a", "swap", 1), ("next", "l0_head")]
    if not b:
        return [("c", *x) for x in order_c()]
    parts = [(t, "b", *x) for t, *x in order_b()]
    if c:
        parts += spread("c", order_c(), C_PLACES)
    if a:
        parts += spread("a", order_a(), A_PLACES)
        parts += [(HEAD_PLACE, "next", "l0_head"), (SWAP_PLACE, "a", "swap", 0), (NT * GI, "a", "swap", 1)]
    return [x[1:] for x in sorted(parts, key=lambda x: x[0])]


def build(nc, x, w1, w2, w_enc, params, consts, weights, places, out):
    x_v = x.rearrange("(s b) c h w -> (b c) s (h w)", s=NS)
    out_v = out.rearrange("(s b) c h w -> (b c) s (h w)", s=NS)
    table = nc.dram_tensor("corner_table", (2 * GI * TROWS, 4 * C), F32, kind="Internal").ap()

    with ExitStack() as ctx:
        def sb(name, shape, dt=F32):
            return ctx.enter_context(nc.sbuf_tensor(name, shape, dt))

        def sem(name):
            return ctx.enter_context(nc.semaphore(name))

        psum = [ctx.enter_context(nc.psum_tensor(f"bank{b}", [P, HALF], F32)) for b in range(8)]
        full = [sem(f"bank{b}_full") for b in range(8)]
        free = [sem(f"bank{b}_free") for b in range(8)]
        B0, B1, B2 = (Banks(full, free, plan) for plan in (plan_a(), plan_b(), plan_c()))

        par = sb("par", [P, NPARAM])
        cst = sb("cst", [P, NCONST])
        wts = sb("wts", [P, NWEIGHT])
        w1_sb = sb("w1_sb", [P, NE, 4, P])
        w2_sb = sb("w2_sb", [P, NE, 2, P])
        wenc = sb("wenc", [C, DM])

        def prm(name):
            a, b = PARAMS[name]
            return par[:, a:b]

        def con(name):
            a, b = CONSTS[name]
            return cst[:, a:b]

        def wt(name):
            a, b = WEIGHTS[name]
            return wts[:, a:b]

        ident = con("ident")
        w_om = wt("w_om").rearrange("p (k m) -> p k m", k=KK)
        w_dcn = wt("w_dcn").rearrange("p (b m) -> p b m", b=3)
        w_glu = wt("w_glu").rearrange("p (k m) -> p k m", k=NB2)
        w_dec4 = wt("w_dec").rearrange("p (k m) -> p k m", k=NB2)

        X = sb("X", [P, NS, HW])
        bst = sb("bst", [P, 4, 2, 6])
        mv = sb("mv", [P, 4, 2])
        std = sb("std", [P, 4])
        rs = sb("rs", [P, 4])
        epst = sb("epst", [P, 1])
        tick = sb("tick", [P, 1])

        xp = sb("xp", [P, GI, TOK])
        lg = sb("lg", [P, 8, NE])
        ex = sb("ex", [P, 8, NE])
        m1 = sb("m1", [P, 8])
        oh = sb("oh", [P, 8, NE])
        oh2 = sb("oh2", [P, 8, NE])
        gate = sb("gate", [P, 8, NE])
        he = sb("he", [P, 2, HALF])
        acc = sb("acc", [P, 2, PT * PT, GI, C])
        xn0 = acc[:, :, :, :, :].rearrange("p t a g c -> p (t a g c)").rearrange("p (a b n) -> p a b n", a=PT, b=PT)

        xpad = sb("xpad", [P, PADLEN])
        bb = sb("bb", [P, NT, OMC])
        NK = GI * KK
        NXY = 2 * NK
        cwn = sb("cwn", [P, NT, NK, 4])
        om = cwn[:, :, :, :].rearrange("p t k a -> p (t k a)")[:, 0:NT * OMC].rearrange("p (t m) -> p t m", t=NT)
        fl = sb("fl", [P, NT, 2 * NK])
        fi = fl[:, :, :].bitcast(I32)
        fr = sb("fr", [P, NT, 2 * NK])
        mk = sb("mk", [P, NT, NK])
        mk1 = sb("mk1", [P, NT, NK])
        idxn = sb("idxn", [P, NT, NK], U32)
        idx = sb("idx", [P, NT, NK], U32)
        cw = sb("cw", [P, NT, NK, 4])
        rowoff = sb("rowoff", [P, 1])
        tb = sb("tb", [P, TRING, GI, 4 * C])
        gt = sb("gt", [P, GI, KK, 4, C])
        sm = sb("sm", [P, 2, 3 * P])
        st = sb("st", [P, GI, 3 * P])
        omt = acc[:, :, :, :, :].rearrange("p t a g c -> p (t a g c)")
        r1 = sb("r1", [P, HALF])
        sc1 = sb("sc1", [P, 1])
        bi1 = sb("bi1", [P, 1])

        u4 = sb("u4", [P, GI, UL])
        wk = sb("wk", [P, JJ, NB2, P])
        corr = sb("corr", [LM, NB2, P])
        yg = sb("yg", [P, 2, NB2, HALF])
        tg = sb("tg", [P, 2, HALF])
        ae = sb("ae", [P, 2, HALF])
        rb = sb("rb", [P, GI, NB2, HALF])
        sqb = sb("sqb", [P, GI, NB2, HALF])
        xn2 = sqb[:, GI - 1].rearrange("p d n -> p (d n)")
        musq = sb("musq", [P, HALF])
        var2 = sb("var2", [P, HALF])
        hb_glu = sb("hb_glu", [P, 2 * NB2])
        wdp = sb("wdp", [P, NB2, C])
        wg2 = sb("wg2", [P, NB2, C])
        dconst = sb("dconst", [P, 1])
        s4 = {n: sb("s4" + n, [P, NB2, NST]) for n in
              ("ea", "ar", "am", "ra", "zr", "zi", "hr", "hi", "t1", "t2", "t3", "t4", "wr", "wi", "er", "ei",
               "cr", "ci")}
        dt_t = sb("dt_t", [P, NB2])
        gflat = gt[:, :, :, :, :].rearrange("p g k a c -> p (g k a c)")
        nv = NB2 * NST * LM
        vr = gflat[:, 0:nv].rearrange("p (d n l) -> p d n l", d=NB2, n=NST)
        vi = gflat[:, nv:2 * nv].rearrange("p (d n l) -> p d n l", d=NB2, n=NST)
        kw = gflat[:, 2 * nv:2 * nv + NB2 * LM * C].rearrange("p (d l s) -> p d l s", d=NB2, l=LM)
        at = 2 * nv + NB2 * LM * C
        v1, v2 = (gflat[:, at + i * nv // 2:at + (i + 1) * nv // 2]
                  .rearrange("p (d n l) -> p d n l", d=NB2, n=NST) for i in range(2))
        kr = sb("kr", [P, 4, NB2, LM])
        cum = sb("cum", [P, 2, NB2, LM])
        cor = sb("cor", [P, NB2, LM])
        cb15 = sb("cb15", [P, NB2])

        xp3 = sb("xp3", [P, PW3 * PW3])
        rbf = rb[:, :, :, :].rearrange("p g d n -> p (g d n)")
        sqf = sqb[:, :, :, :].rearrange("p g d n -> p (g d n)")
        ya = rbf[:, 0:2 * HW].rearrange("p (i n) -> p i n", i=2)
        yc, ysq = sqf[:, 0:HW], sqf[:, HW:2 * HW]
        hg = yg[:, :, :, :].rearrange("p a d n -> p (a d) n")
        t3 = (musq, var2)

        xpad_v = xpad[:, 0:PW * PW].rearrange("p (y x) -> p y x", y=PW)
        xp3_v = xp3[:, :].rearrange("p (y x) -> p y x", y=PW3)

        names = """x0_in x_in par_in wts_in w1_in w2_in zeros_set exp_done a_inv s4_done wg_done cm_done
            k_turned k_there dec_there s1_var s1_std s1_there
            var_ready0 var_ready1 var_ready2 var_ready3 std_ready0 std_ready1 std_ready2 std_ready3
            xn0_ready xp_in max_ready exp_ready
            xpad_ready om_ready mask_ready idx_ready smp_ready st_used x1_added
            u_ready u_in glu_done sq_ready var2_ready std2_ready x2_added
            y3_ready ysq_ready yn_ready x3_ready out_done
            table_zero zero_there dve_chain act_chain pool_chain held""".split()
        S = {n: sem(n) for n in names}
        table_out = [sem(f"table_out{t}") for t in range(TRING)]
        gathered = [sem(f"gathered{g}") for g in range(GI)]

        block = ctx.enter_context(nc.Block())

        def hold(eng):
            eng.sem_inc(S["held"])

        def run(eng, parts, end=None):
            def body(s, a, b, c):
                step = {"head": s + 1, "next": s + 2, "a": s + 1, "b": s, "c": s - 1}
                for stage, name, *args in order(a, b, c):
                    if name in parts:
                        parts[name](step[stage], *args)
                if end:
                    end()
            body(-1, True, False, False)
            body(0, True, True, False)
            with eng.Fori(1, NS - 1) as s:
                body(s, True, True, True)
            body(NS - 1, False, True, True)
            body(NS, False, False, True)

        @block.sync
        def _(sp):
            sp.dma_start(X[:, 0], x_v[:, 0]).then_inc(S["x0_in"], 16)
            sp.dma_start(par[:, :], params).then_inc(S["par_in"], 16)
            sp.dma_start(cst[:, :], consts).then_inc(S["par_in"], 16)
            sp.dma_start(w1_sb[:, :, :, :].rearrange("p e b m -> p (e b m)"), w1).then_inc(S["w1_in"], 16)
            sp.dma_start(w2_sb[:, :, :, :].rearrange("p e b m -> p (e b m)"), w2).then_inc(S["w2_in"], 16)
            sp.dma_start(wenc[:, :], w_enc).then_inc(S["wts_in"], 16)
            sp.dma_start(bb[:, :, :].rearrange("p t m -> p (t m)"), places).then_inc(S["wts_in"], 16)
            sp.dma_start(wts[:, :], weights).then_inc(S["wts_in"], 16)
            sp.dma_start(X[:, 1:NS], x_v[:, 1:NS]).then_inc(S["x_in"], 16)
            for started in [S["xp_in"], S["u_in"]] + table_out:
                sp.sem_inc(started, FROM)
            sp.wait_ge(S["zeros_set"], 1)
            tables = table.rearrange("(h g q p) e -> h q p g e", h=2, g=GI, p=P)
            for t in range(TQ):
                sp.dma_start(tables[1, t], tb[:, 0]).then_inc(S["table_zero"], 16)

            def l0_head(s):
                sp.wait_ge(S["xn0_ready"], s + 1)
                hold(sp)
                B0.last_step_filled(sp, s, 1)
                hold(sp)
                for dyx in range(PT * PT):
                    for g in range(GI):
                        sp.dma_start(xp[dyx * C:(dyx + 1) * C, g, :],
                                     xn0[g * C:(g + 1) * C, dyx // PT, dyx % PT, :]).then_inc(S["xp_in"], 16)

            def l1_table(s, t):
                if t == 0 and (not isinstance(s, int) or s > 1):
                    sp.wait_ge(S["smp_ready"], FROM + (s - 1) * NT * GI)
                    hold(sp)
                B0.read(sp, s, ("table", t))
                hold(sp)
                half = s % 2
                dst = tables[half, t] if isinstance(half, int) else tables[bass.ds(half, 1), t]
                if not isinstance(half, int):
                    dst = dst.rearrange("h p g e -> p (h g) e")
                sp.dma_start(dst, tb[:, t % TRING]).then_inc(table_out[t % TRING], 16)

            def l1_conv(s):
                for t in range(TRING):
                    l1_table(s, t)

            def l2_head(s):
                sp.wait_ge(S["u_ready"], s + 1)
                hold(sp)
                B2.last_step_filled(sp, s, 5)
                hold(sp)
                for g in range(GI):
                    for j in range(JJ):
                        sp.dma_start(u4[j * C:(j + 1) * C, g, LM + j:LM + j + HW],
                                     xn2[g * C:(g + 1) * C, :]).then_inc(S["u_in"], 16)

            def l3_mlp(s, n):
                sp.wait_ge(S["x3_ready"], s * 2 + n + 1)
                hold(sp)
                sp.dma_start(out_v[:, bass.ds(s, 1), n * HALF:(n + 1) * HALF],
                             X[:, bass.ds(s, 1), n * HALF:(n + 1) * HALF]).then_inc(S["out_done"], 16)

            run(sp, dict(l0_head=l0_head, l1_conv=l1_conv, l1_table=l1_table, l2_head=l2_head, l3_mlp=l3_mlp))
            sp.wait_ge(S["out_done"], 16 * 2 * NS)

        @block.gpsimd
        def _(pool):
            ch = Chain(pool, S["pool_chain"])
            pool.memset(u4[:, :, :], 0.0)
            pool.memset(xp3[:, :], 0.0)
            pool.memset(xpad[:, :], 0.0)
            pool.memset(sm[:, :, :], 0.0)
            pool.memset(rowoff[:, :], 0.0)
            pool.memset(tb[:, :, :, :], 0.0).then_inc(S["zeros_set"], 1)

            def mul(o, a, b):
                ch.did(pool.tensor_tensor(o, a, b, ALU.mult))

            def add(o, a, b, op=ALU.add):
                ch.did(pool.tensor_tensor(o, a, b, op))

            def cmul(ore, oim, ar, ai, br, bi, ta, tb_):
                mul(ta[0], ar, br)
                mul(ta[1], ai, bi)
                mul(tb_[0], ar, bi)
                mul(tb_[1], ai, br)
                ch.wait()
                add(ore, ta[0], ta[1], ALU.subtract)
                add(oim, tb_[0], tb_[1])
                ch.wait()

            q = {n: t[:, :, :] for n, t in s4.items()}
            ta, tb_ = (q["t1"], q["t2"]), (q["t3"], q["t4"])
            pool.wait_ge(S["a_inv"], 1)
            pool.wait_ge(S["par_in"], 32)
            a_im = prm("a_imag").rearrange("p (d n) -> p d n", d=NB2)
            dt_b = dt_t[:, :].unsqueeze(2).to_broadcast([P, NB2, NST])
            mul(q["t1"], q["ar"], dt_b)
            mul(q["t2"], a_im, dt_b)
            ch.wait()
            ch.did(pool.tensor_scalar(q["zr"], q["t1"], 2.0 ** -6, None, ALU.mult))
            ch.did(pool.tensor_scalar(q["zi"], q["t2"], 2.0 ** -6, None, ALU.mult))
            ch.did(pool.memset(q["hr"], 1.0))
            ch.did(pool.memset(q["hi"], 0.0))
            ch.wait()
            for k in range(9, 1, -1):
                cmul(q["wr"], q["wi"], q["zr"], q["zi"], q["hr"], q["hi"], ta, tb_)
                ch.did(pool.tensor_scalar(q["hr"], q["wr"], 1.0 / k, 1.0, ALU.mult, ALU.add))
                ch.did(pool.tensor_scalar(q["hi"], q["wi"], 1.0 / k, None, ALU.mult))
                ch.wait()
            cmul(q["wr"], q["wi"], q["zr"], q["zi"], q["hr"], q["hi"], ta, tb_)
            for _ in range(6):
                ch.did(pool.tensor_scalar(q["hr"], q["wr"], 2.0, None, ALU.add))
                ch.wait()
                cmul(q["er"], q["ei"], q["wr"], q["wi"], q["hr"], q["wi"], ta, tb_)
                ch.did(pool.tensor_copy(q["wr"], q["er"]))
                ch.did(pool.tensor_copy(q["wi"], q["ei"]))
                ch.wait()
            ch.did(pool.tensor_scalar(q["er"], q["wr"], 1.0, None, ALU.add))
            ch.did(pool.tensor_scalar(q["hi"], a_im, -1.0, None, ALU.mult))
            ch.wait()
            cmul(q["zr"], q["zi"], q["wr"], q["wi"], q["ar"], q["hi"], ta, tb_)
            mul(q["hr"], q["zr"], q["ra"])
            mul(q["wr"], q["zi"], q["ra"])
            ch.wait()
            c_re = prm("c_real").rearrange("p (d n) -> p d n", d=NB2)
            c_im = prm("c_imag").rearrange("p (d n) -> p d n", d=NB2)
            cmul(vr[:, :, :, 0], vi[:, :, :, 0], c_re, c_im, q["hr"], q["wr"], ta, tb_)
            er, ei, nr, ni = q["er"], q["wi"], q["cr"], q["ci"]
            m = 1
            while m < LM:
                eb = er.unsqueeze(3).to_broadcast([P, NB2, NST, m])
                ib = ei.unsqueeze(3).to_broadcast([P, NB2, NST, m])
                for d in range(NB2):
                    mul(v1[:, d, :, 0:m], vr[:, d, :, 0:m], eb[:, d])
                    mul(v2[:, d, :, 0:m], vi[:, d, :, 0:m], ib[:, d])
                    ch.wait()
                    add(vr[:, d, :, m:2 * m], v1[:, d, :, 0:m], v2[:, d, :, 0:m], ALU.subtract)
                    ch.wait()
                    mul(v1[:, d, :, 0:m], vr[:, d, :, 0:m], ib[:, d])
                    mul(v2[:, d, :, 0:m], vi[:, d, :, 0:m], eb[:, d])
                    ch.wait()
                    add(vi[:, d, :, m:2 * m], v1[:, d, :, 0:m], v2[:, d, :, 0:m])
                    ch.wait()
                m *= 2
                if m < LM:
                    cmul(nr, ni, er, ei, er, ei, ta, tb_)
                    er, ei, nr, ni = nr, ni, er, ei
            add(kr[:, 0], vr[:, :, 0], vr[:, :, 1])
            add(kr[:, 1], vr[:, :, 2], vr[:, :, 3])
            ch.wait()
            add(kr[:, 2], kr[:, 0], kr[:, 1])
            ch.wait()
            ch.did(pool.tensor_scalar(kr[:, 3], kr[:, 2], 2.0, None, ALU.mult))
            ch.wait()
            add(kr[:, 3, :, 0], kr[:, 3, :, 0], prm("d"))
            ch.wait()
            src, dst, sh = kr[:, 3], cum[:, 0], 1
            while sh < LM:
                ch.did(pool.tensor_copy(dst[:, :, 0:sh], src[:, :, 0:sh]))
                add(dst[:, :, sh:LM], src[:, :, sh:LM], src[:, :, 0:LM - sh])
                ch.wait()
                src, dst, sh = dst, cum[:, 1] if sh in (1, 4) else cum[:, 0], sh * 2
            b_enc = prm("b_enc")
            mul(cb15[:, :], src[:, :, LM - 1], b_enc)
            add(kr[:, 0], src, src[:, :, LM - 1:LM].to_broadcast([P, NB2, LM]), ALU.subtract)
            ch.wait()
            mul(cor[:, :, :], kr[:, 0], b_enc.unsqueeze(2).to_broadcast([P, NB2, LM]))
            enc_t = prm("w_enc_t").rearrange("p (d s) -> p d s", d=NB2)
            for d in range(NB2):
                mul(kw[:, d], enc_t[:, d].unsqueeze(1).to_broadcast([P, LM, C]),
                    kr[:, 3, d].unsqueeze(2).to_broadcast([P, LM, C]))
            ch.wait()
            pool.memset(q["t1"], 0.0).then_inc(S["s4_done"], 1)

            def sample(s, t):
                j, g = divmod(t, GI)
                if j in (0, NT - 1) and g == 0:
                    pool.wait_ge(S["idx_ready"], s * 2 + 1 + j // (NT - 1))
                if t == 0:
                    if isinstance(s, int):
                        pool.wait_ge(S["table_zero"], 16 * TQ)
                        pool.wait_ge(S["k_turned"], 2)
                    for i in range(TRING):
                        pool.wait_ge(table_out[i], FROM + (s + 1) * 16 * len(range(i, TQ, TRING)))
                pool.wait_ge(S["smp_ready"], FROM + s * NT * GI + max(t - GI + 1, 0))
                hold(pool)
                for k in range(KK):
                    pool.indirect_dma_start(
                        gt[:, g, k].rearrange("p a c -> p (a c)"), None, table,
                        bass.IndirectOffsetOnAxis(ap=idx[:, j, g * KK + k:g * KK + k + 1], axis=0),
                    ).then_inc(gathered[g], 16)

            run(pool, dict(sample=sample))

        @block.scalar
        def _(act):
            act.wait_ge(S["par_in"], 32)
            act.activation(dt_t[:, :], prm("log_dt"), ACT.Exp)
            act.activation(s4["ea"][:, :, :], prm("a_real").rearrange("p (d n) -> p d n", d=NB2), ACT.Exp)\
               .then_inc(S["exp_done"], 1)
            act.activation(hb_glu[:, :], prm("b_glu"), ACT.Copy, scale=0.5).then_inc(S["act_chain"], 1)
            act.wait_ge(S["s1_var"], 1)
            act.activation(std[:, 0:1], epst[:, :], ACT.Sqrt).then_inc(S["s1_std"], 1)
            act.wait_ge(S["s1_there"], 1)
            act.wait_ge(S["act_chain"], 1)

            def s4d(s):
                act.wait_ge(S["k_turned"], 1)
                act.activation(wk[:, 0:2].rearrange("p t d m -> p (t d m)"), psum[5][:, :], ACT.Copy)
                act.wait_ge(S["k_turned"], 2)
                act.activation(wk[:, 2:4].rearrange("p t d m -> p (t d m)"), psum[6][:, :], ACT.Copy)
                act.wait_ge(S["k_turned"], 3)
                act.activation(corr[:, :, :].rearrange("p d m -> p (d m)"), psum[7][0:LM, 0:NB2 * P], ACT.Copy)\
                   .then_inc(S["k_there"], 1)

            def root(s, layer):
                act.wait_ge(S[f"var_ready{layer}"], s + 1)
                act.activation(std[:, layer:layer + 1], mv[:, layer, 1:2], ACT.Sqrt, bias=epst[:, :])\
                   .then_inc(S[f"std_ready{layer}"], 1)

            def l0_head(s):
                root(s, 0)
                act.wait_ge(S["max_ready"], s + 1)
                act.activation(ex[:, :, :], lg[:, :, :], ACT.Exp).then_inc(S["exp_ready"], 1)

            def l0_unit(s, u):
                if u == NU:
                    return
                B0.filled(act, s, ("gate", u))
                if u >= 2:
                    B0.filled(act, s, ("out", u - 2))
                act.activation(he[:, u % 2], psum[0][:, :], ACT.Tanh, scale=0.5).then_inc(free[0], 1)

            def l1_conv(s):
                for n in range(2):
                    b = B0.bank(("omc", n))
                    B0.filled(act, s, ("omc", n))
                    act.activation(omt[0:OMC, n * HALF:(n + 1) * HALF], psum[b][0:OMC, :], ACT.Copy)\
                       .then_inc(free[b], 1)
                for t in range(TRING):
                    l1_table(s, t)

            def l1_table(s, t):
                b = B0.bank(("table", t))
                B0.filled(act, s, ("table", t))
                if isinstance(s, int) and s == 0 and t == 0:
                    act.wait_ge(S["table_zero"], 16 * TQ)
                act.wait_ge(table_out[t % TRING],
                            FROM + 16 * (s * len(range(t % TRING, TQ, TRING)) + t // TRING))
                act.activation(tb[:, t % TRING].rearrange("p g (a c) -> p a g c", a=4),
                               psum[b][:, :].rearrange("p (a g c) -> p a g c", a=4, g=GI), ACT.Copy)\
                   .then_inc(free[b], 1)

            def l1_index(s):
                act.wait_ge(S["om_ready"], s + 1)
                act.activation(mk[:, :, :], om[:, :, 2 * NK:OMC], ACT.Tanh, scale=0.5)\
                   .then_inc(S["mask_ready"], 1)

            def turn(s, t):
                j, g = divmod(t, GI)
                B1.filled(act, s, ("sampled", j, g))
                if g == 0:
                    if j % 4:
                        act.wait_ge(S["st_used"], s * 6 + j // 4 * 3 + j % 4)
                    elif j:
                        B1.filled(act, s, ("dcn", 0))
                    else:
                        B1.last_step_filled(act, s, 4)
                act.activation(st[:, g], psum[3][:, 0:3 * P], ACT.Copy).then_inc(free[3], 1)

            def dcn(s, j):
                if j % 4 == 3:
                    n = j // 4
                    B1.filled(act, s, ("dcn", n))
                    act.wait_ge(S["x1_added"], FROM + s * 2 + n)
                    act.activation(r1[:, :], psum[4][:, :], ACT.Relu, bias=bi1[:, :], scale=sc1[:, :])\
                       .then_inc(free[4], 1)

            def l2_y(s, c):
                n, g = divmod(c, GI)
                for d in range(NB2):
                    name = ("y", c, d)
                    B2.filled(act, s, name)
                    if c >= 2:
                        B2.filled(act, s, ("ga", c - 2, NB2 - 1))
                    act.activation(yg[:, c % 2, d], psum[B2.bank(name)][:, :], ACT.Gelu_apprx_tanh,
                                   bias=cb15[:, d:d + 1]).then_inc(free[B2.bank(name)], 1)

            def l2_glu(s, c):
                n, g = divmod(c, GI)
                for d in range(NB2):
                    if c:
                        B2.read(act, s, ("z", c - 1, d))
                    b = B2.bank(("gb", c, d))
                    B2.filled(act, s, ("gb", c, d))
                    act.activation(tg[:, d], psum[b][:, :], ACT.Tanh, scale=0.5,
                                   bias=hb_glu[:, NB2 + d:NB2 + d + 1]).then_inc(free[b], 1)
                    b = B2.bank(("ga", c, d))
                    B2.filled(act, s, ("ga", c, d))
                    act.activation(ae[:, d], psum[b][:, :], ACT.Identity, scale=0.5,
                                   bias=hb_glu[:, d:d + 1]).then_inc(free[b], 1)
                for d in range(NB2):
                    B2.read(act, s, ("z", c, d))
                    if n:
                        B2.filled(act, s, ("sq", 0))
                    else:
                        B2.last_step_filled(act, s, 5)
                    act.activation(sqb[:, g, d], rb[:, g, d], ACT.Square).then_inc(S["sq_ready"], 1)

            def l2_close(s, n):
                B2.filled(act, s, ("mu", n))
                b = B2.bank(("mu", n))
                act.activation(musq[:, :], psum[b][:, :], ACT.Square).then_inc(free[b], 1)
                act.wait_ge(S["var2_ready"], s * 2 + n + 1)
                act.activation(var2[:, :], var2[:, :], ACT.Sqrt, bias=epst[:, :]).then_inc(S["std2_ready"], 1)

            def l3_norm(s):
                for n in range(2):
                    B2.read(act, s, ("mu3", n))
                    act.activation(ysq[:, n * HALF:(n + 1) * HALF], yc[:, n * HALF:(n + 1) * HALF], ACT.Square)\
                       .then_inc(S["ysq_ready"], 1)
                for n in range(2):
                    B2.filled(act, s, ("sq3", n))
                    b = B2.bank(("sq3", n))
                    act.activation(ysq[:, n * HALF:(n + 1) * HALF], psum[b][:, :], ACT.Sqrt, bias=epst[:, :])\
                       .then_inc(free[b], 1)

            def l3_mlp(s, n):
                for g in range(GI):
                    B2.filled(act, s, ("hid", n, g))
                    if n and g == 0:
                        B2.filled(act, s, ("mlp", 0))
                    b = B2.bank(("hid", n, g))
                    act.activation(hg[:, g], psum[b][:, :], ACT.Gelu_apprx_tanh, bias=prm("b1"))\
                       .then_inc(free[b], 1)

            run(act, dict(s4d=s4d, l0_head=l0_head, l0_unit=l0_unit, l1_norm=lambda s: root(s, 1),
                          l1_conv=l1_conv, l1_table=l1_table, l1_index=l1_index, turn=turn, dcn=dcn,
                          l2_head=lambda s: root(s, 2), l2_y=l2_y, l2_glu=l2_glu, l2_close=l2_close,
                          l3_head=lambda s: root(s, 3), l3_norm=l3_norm, l3_mlp=l3_mlp))

        @block.vector
        def _(dve):
            ch = Chain(dve, S["dve_chain"])
            for started in (S["smp_ready"], S["x1_added"]):
                dve.sem_inc(started, FROM)
            tt, ts, stt = dve.tensor_tensor, dve.tensor_scalar, dve.scalar_tensor_tensor
            dve.wait_ge(S["par_in"], 32)
            ts(epst[:, :], prm("l1_var"), EPS, None, ALU.add).then_inc(S["s1_var"], 1)
            dve.wait_ge(S["exp_done"], 1)
            a_im = prm("a_imag").rearrange("p (d n) -> p d n", d=NB2)
            ch.did(ts(s4["ar"][:, :, :], s4["ea"][:, :, :], -1.0, None, ALU.mult))
            ch.did(tt(s4["am"][:, :, :], s4["ea"][:, :, :], s4["ea"][:, :, :], ALU.mult))
            ch.then(tt(s4["t1"][:, :, :], a_im, a_im, ALU.mult))
            ch.then(tt(s4["am"][:, :, :], s4["am"][:, :, :], s4["t1"][:, :, :], ALU.add))
            dve.reciprocal(s4["ra"][:, :, :], s4["am"][:, :, :]).then_inc(S["a_inv"], 1)
            dve.wait_ge(S["s1_std"], 1)
            ch.then(dve.reciprocal(rs[:, 0:1], std[:, 0:1]))
            ch.did(tt(sc1[:, :], rs[:, 0:1], prm("l1_gamma"), ALU.mult))
            ch.then(tt(bi1[:, :], prm("l1_b"), prm("l1_mean"), ALU.subtract))
            ch.then(stt(out=bi1[:, :], in0=bi1[:, :], scalar=sc1[:, 0:1], in1=prm("l1_beta"),
                        op0=ALU.mult, op1=ALU.add))
            dve.memset(epst[:, :], EPS).then_inc(S["s1_there"], 1)
            dve.wait_ge(S["zeros_set"], 1)
            dve.wait_ge(S["x0_in"], 16)
            ch.restart()

            def s4d(s):
                for d in range(NB2):
                    op = ts(wg2[:, d], w_dec4[:, d, 0:C], prm("ln2_g")[:, d:d + 1], None, ALU.mult)
                    if d:
                        op.then_inc(S["wg_done"], 1)
                dve.wait_ge(S["wg_done"], 1)
                dve.wait_ge(S["cm_done"], 1)
                ch.did(tt(wdp[:, :, :], wg2[:, :, :],
                          psum[4][:, 0:C].unsqueeze(1).to_broadcast([P, NB2, C]), ALU.subtract))
                dve.wait_ge(S["cm_done"], 2)
                tt(dconst[:, :], psum[3][:, 0:1], prm("b_dec"), ALU.add).then_inc(S["dec_there"], 1)
                dve.wait_ge(S["dec_there"], 1)

            def weights(s):
                dve.wait_ge(S["wts_in"], 48)
                dve.wait_ge(S["x_in"], 16)
                ch.did(tt(bb[:, :, :], bb[:, :, :], prm("b_om").unsqueeze(1).to_broadcast([P, NT, OMC]), ALU.add))

            def norm(s, layer):
                at = s % NS if layer == 0 else s
                for n in range(2):
                    ch.did(dve.bn_stats(bst[:, layer, n], X[:, bass.ds(at, 1), n * HALF:(n + 1) * HALF]
                                        .rearrange("p o n -> p (o n)")))
                ch.wait()
                dve.bn_aggr(mv[:, layer], bst[:, layer].rearrange("p a b -> p (a b)"))\
                   .then_inc(S[f"var_ready{layer}"], 1)
                dve.wait_ge(S[f"std_ready{layer}"], s + 1)
                ch.then(dve.reciprocal(rs[:, layer:layer + 1], std[:, layer:layer + 1]))
                return mv[:, layer, 0:1], rs[:, layer:layer + 1]

            def l0_head(s):
                mean, r = norm(s, 0)
                dve.wait_ge(S["xp_in"], FROM + s * 256)
                xv = X[:, bass.ds(s % NS, 1), :].rearrange("p o (h a w b) -> p (o h) a w b", a=PT, b=PT, w=W // PT)
                for dy in range(PT):
                    for dx in range(PT):
                        op = ts(xn0[:, dy, dx].rearrange("p (h w) -> p h w", h=H // PT), xv[:, :, dy, :, dx],
                                mean, r, ALU.subtract, ALU.mult)
                        if dy and dx:
                            op.then_inc(S["xn0_ready"], 1)
                        else:
                            ch.did(op)
                B0.filled(dve, s, "router")
                logit = psum[2][:, 0:8 * NE].rearrange("p (t e) -> p t e", t=8)
                ch.then(dve.tensor_reduce(m1[:, :], logit, AX.X, ALU.max))

                def over(v):
                    return v[:, :].unsqueeze(2).to_broadcast([P, 8, NE])
                tt(lg[:, :, :], logit, over(m1), ALU.subtract).then_inc(free[2], 1)
                B0.read(dve, s, "router")
                rank = con("rank").unsqueeze(1).to_broadcast([P, 8, NE])

                def first_max(o, src):
                    ch.then(dve.tensor_reduce(m1[:, :], src, AX.X, ALU.max))
                    ch.then(tt(o, src, over(m1), ALU.is_equal))
                    ch.then(tt(o, o, rank, ALU.mult))
                    ch.then(dve.tensor_reduce(m1[:, :], o, AX.X, ALU.max))
                    ch.then(tt(o, o, over(m1), ALU.is_equal))
                ch.then(ts(gate[:, :, :], lg[:, :, :], 1.0, None, ALU.mult))
                dve.memset(m1[:, :], 0.0).then_inc(S["max_ready"], 1)
                dve.wait_ge(S["max_ready"], s + 1)
                first_max(oh[:, :, :], gate[:, :, :])
                ch.then(stt(out=gate[:, :, :], in0=oh[:, :, :], scalar=-1e30, in1=gate[:, :, :],
                            op0=ALU.mult, op1=ALU.add))
                first_max(oh2[:, :, :], gate[:, :, :])
                ch.then(tt(oh[:, :, :], oh[:, :, :], oh2[:, :, :], ALU.add))
                dve.wait_ge(S["exp_ready"], s + 1)
                ch.then(tt(gate[:, :, :], ex[:, :, :], oh[:, :, :], ALU.mult))
                ch.then(dve.tensor_reduce(m1[:, :], gate[:, :, :], AX.X, ALU.add))
                ch.then(dve.reciprocal(m1[:, :], m1[:, :]))
                ch.then(stt(out=gate[:, :, :], in0=gate[:, :, :], scalar=0.5, in1=over(m1),
                            op0=ALU.mult, op1=ALU.mult))

            def l0_he(s, u):
                B0.filled(dve, s, ("value", u))
                B0.read(dve, s, ("gate", u))
                stt(out=he[:, u % 2], in0=he[:, u % 2], scalar=1.0, in1=psum[1][:, :],
                    op0=ALU.add, op1=ALU.mult).then_inc(free[1], 1)

            def l0_acc(s, u):
                g, e = divmod(u, NE)
                B0.filled(dve, s, ("out", u))
                if e:
                    B0.read(dve, s, ("out", u - 1))
                for t in range(2):
                    sc = gate[:, g * 2 + t, e:e + 1]
                    o = psum[2][:, t * D0:(t + 1) * D0].rearrange("p (a c) -> p a c", c=C)
                    a = acc[:, t, :, g]
                    if e:
                        op = stt(out=a, in0=o, scalar=sc, in1=a, op0=ALU.mult, op1=ALU.add)
                    else:
                        op = ts(a, o, sc, None, ALU.mult)
                    if t:
                        op.then_inc(free[2], 1)

            def l0_tail(s):
                for t in range(2):
                    B0.filled(dve, s, ("back", t))
                    for dy in range(PT):
                        xv = X[:, bass.ds(s, 1), :].rearrange("p o (h a w b) -> p (o h) a b w", a=PT, b=PT,
                                                              w=W // PT)
                        xv = xv[:, t * 8:(t + 1) * 8, dy].rearrange("p h b w -> p b h w")
                        bk = psum[t][:, dy * 2 * P:(dy + 1) * 2 * P].rearrange("p (b h w) -> p b h w", b=PT, h=8)
                        op = tt(xv, xv, bk, ALU.add)
                        if dy:
                            op.then_inc(free[t], 1)
                        else:
                            ch.did(op)
                B0.read(dve, s, ("back", 0))
                B0.read(dve, s, ("back", 1))
                hold(dve)

            def l1_norm(s):
                mean, r = norm(s, 1)
                xv = X[:, bass.ds(s, 1), :].rearrange("p o (h w) -> p (o h) w", w=W)
                ts(xpad_v[:, 1:H + 1, 1:W + 1], xv, mean, r, ALU.subtract, ALU.mult).then_inc(S["xpad_ready"], 1)

            def l1_om(s):
                for n in range(2):
                    B0.filled(dve, s, ("om", n))
                    b = B0.bank(("om", n))
                    tt(om[:, n * 4:(n + 1) * 4], psum[b][:, 0:4 * OMC].rearrange("p (t m) -> p t m", t=4),
                       bb[:, n * 4:(n + 1) * 4], ALU.add).then_inc(free[b], 1)
                B0.read(dve, s, ("om", 0))
                B0.read(dve, s, ("om", 1))
                pos = om[:, :, 0:NXY]
                ts(pos, pos, 0.0, float(H + 1), ALU.max, ALU.min).then_inc(S["om_ready"], 1)

            def l1_index(s):
                pos = om[:, :, 0:NXY]
                dve.wait_ge(S["om_ready"], s + 1)
                ch.then(dve.tensor_copy(fi[:, :, :], pos))
                ch.then(dve.tensor_copy(fl[:, :, :], fi[:, :, :]))
                ch.then(tt(fr[:, :, :], fl[:, :, :], pos, ALU.is_gt))
                ch.then(tt(fl[:, :, :], fl[:, :, :], fr[:, :, :], ALU.subtract))
                ch.then(ts(fl[:, :, :], fl[:, :, :], float(H), None, ALU.min))
                ch.did(tt(fr[:, :, :], pos, fl[:, :, :], ALU.subtract))
                ch.then(stt(out=mk1[:, :, :], in0=fl[:, :, 0:NK], scalar=float(PW), in1=fl[:, :, NK:NXY],
                            op0=ALU.mult, op1=ALU.add))
                ch.then(stt(out=idxn[:, :, :], in0=mk1[:, :, :], scalar=rowoff[:, 0:1],
                            in1=con("image_row").unsqueeze(1).to_broadcast([P, NT, NK]),
                            op0=ALU.add, op1=ALU.add))
                ch.did(ts(rowoff[:, :], rowoff[:, :], -1.0, float(GI * TROWS), ALU.mult, ALU.add))

            def l1_share(s):
                dve.wait_ge(S["mask_ready"], s + 1)
                ch.then(ts(mk1[:, :, :], mk[:, :, :], 0.5, 0.5, ALU.mult, ALU.add))
                fy, fx = fr[:, :, 0:NK], fr[:, :, NK:NXY]
                ch.then(tt(mk[:, :, :], mk1[:, :, :], fy, ALU.mult))
                ch.did(tt(cwn[:, :, :, 3], mk[:, :, :], fx, ALU.mult))
                ch.then(tt(mk1[:, :, :], mk1[:, :, :], mk[:, :, :], ALU.subtract))
                ch.did(tt(cwn[:, :, :, 2], mk[:, :, :], cwn[:, :, :, 3], ALU.subtract))
                ch.then(tt(cwn[:, :, :, 1], mk1[:, :, :], fx, ALU.mult))
                ch.then(tt(cwn[:, :, :, 0], mk1[:, :, :], cwn[:, :, :, 1], ALU.subtract))

            def swap(s, last):
                j = slice(NT - 1, NT) if last else slice(0, NT - 1)
                ch.wait()
                dve.tensor_copy(idx[:, j], idxn[:, j]).then_inc(S["idx_ready"], 1)
                ch.did(dve.tensor_copy(cw[:, j], cwn[:, j]))

            def sample(s, t):
                j, g = divmod(t, GI)
                dve.wait_ge(gathered[g], (s * NT + j + 1) * 16 * KK)
                rows = gt[:, g].rearrange("p k a c -> p (k a) c")
                share = cw[:, j, g * KK:(g + 1) * KK].rearrange("p k a -> p (k a)")
                ch.then(tt(rows, rows, share.unsqueeze(2).to_broadcast([P, 4 * KK, C]), ALU.mult))
                ch.then(tt(gt[:, g, :, 0:2], gt[:, g, :, 0:2], gt[:, g, :, 2:4], ALU.add))
                if t >= 2:
                    B1.filled(dve, s, ("sampled", (t - 2) // GI, (t - 2) % GI))
                else:
                    B1.last_step_filled(dve, s, 3)
                tt(sm[:, t % 2, 0:KK * C].rearrange("p (k c) -> p k c", k=KK), gt[:, g, :, 0], gt[:, g, :, 1],
                   ALU.add).then_inc(S["smp_ready"], 1)

            def dcn(s, j):
                if j % 4 == 3:
                    n = j // 4
                    B1.read(dve, s, ("dcn", n))
                    xh = X[:, bass.ds(s, 1), n * HALF:(n + 1) * HALF].rearrange("p o n -> p (o n)")
                    tt(xh, xh, r1[:, :], ALU.add).then_inc(S["x1_added"], 1)

            def l2_head(s):
                dve.wait_ge(S["x1_added"], FROM + s * 2 + 2)
                hold(dve)
                mean, r = norm(s, 2)
                dve.wait_ge(S["u_in"], FROM + s * 256)
                xv = X[:, bass.ds(s, 1), :].rearrange("p o n -> p (o n)")
                ts(xn2[:, :], xv, mean, r, ALU.subtract, ALU.mult).then_inc(S["u_ready"], 1)

            def l2_glu(s, c):
                n, g = divmod(c, GI)
                for d in range(NB2):
                    B2.read(dve, s, ("ga", c, d))
                    stt(out=tg[:, d], in0=tg[:, d], scalar=1.0, in1=ae[:, d], op0=ALU.add, op1=ALU.mult)\
                        .then_inc(S["glu_done"], 1)
                    dve.wait_ge(S["glu_done"], s * 8 * NB2 + (n * GI + g) * NB2 + d + 1)
                    B2.filled(dve, s, ("z", c, d))
                    if n:
                        B2.filled(dve, s, ("sq", 0))
                        dve.wait_ge(S["sq_ready"], s * 8 * NB2 + GI * NB2)
                    else:
                        B2.last_step_filled(dve, s, 5)
                    b = B2.bank(("z", c, d))
                    stt(out=rb[:, g, d], in0=psum[b][:, :], scalar=prm("b_enc")[:, d:d + 1], in1=tg[:, d],
                        op0=ALU.add, op1=ALU.add).then_inc(free[b], 1)

            def l2_close(s, n):
                b = B2.bank(("sq", n))
                B2.filled(dve, s, ("sq", n))
                B2.read(dve, s, ("mu", n))
                tt(var2[:, :], psum[b][:, :], musq[:, :], ALU.subtract).then_inc(S["var2_ready"], 1)
                dve.wait_ge(S["std2_ready"], s * 2 + n + 1)
                ch.then(dve.reciprocal(var2[:, :], var2[:, :]))
                B2.filled(dve, s, ("dec", n))
                b = B2.bank(("dec", n))
                ch.then(tt(musq[:, :], psum[b][:, :], var2[:, :], ALU.mult))
                xh = X[:, bass.ds(s, 1), n * HALF:(n + 1) * HALF].rearrange("p o n -> p (o n)")
                ch.then(stt(out=xh, in0=musq[:, :], scalar=dconst[:, 0:1], in1=xh, op0=ALU.add, op1=ALU.add))
                dve.memset(tick[:, :], 0.0).then_inc(free[b], 1)
                B2.read(dve, s, ("dec", n))
                dve.memset(tick[:, :], 0.0).then_inc(free[B2.bank(("sq", n))], 1)

            def l3_head(s):
                B2.read(dve, s, ("sq", 1))
                hold(dve)
                mean, r = norm(s, 3)
                xv = X[:, bass.ds(s, 1), :].rearrange("p o (h w) -> p (o h) w", w=W)
                pd = K7 // 2
                ch.then(ts(xp3_v[:, pd:pd + H, pd:pd + W], xv, mean, r, ALU.subtract, ALU.mult))

            last = [0, 0]

            def tap(s, t):
                win = xp3_v[:, t // K7:t // K7 + H, t % K7:t % K7 + W]
                weight = prm("dw")[:, t:t + 1]
                a = t % 2
                y = ya[:, a].rearrange("p (h w) -> p h w", h=H)
                if t == 0:
                    op = ts(y, win, weight, prm("dw_b"), ALU.mult, ALU.add)
                elif t == 1:
                    op = ts(y, win, weight, None, ALU.mult)
                else:
                    ch.wait(last[a])
                    op = stt(out=y, in0=win, scalar=weight, in1=y, op0=ALU.mult, op1=ALU.add)
                last[a] = ch.did(op)

            def l3_norm(s):
                ch.wait()
                tt(ya[:, 0], ya[:, 0], ya[:, 1], ALU.add).then_inc(S["y3_ready"], 1)
                dve.wait_ge(S["y3_ready"], s + 1)
                for n in range(2):
                    h = slice(n * HALF, (n + 1) * HALF)
                    B2.filled(dve, s, ("mu3", n))
                    b = B2.bank(("mu3", n))
                    tt(yc[:, h], ya[:, 0, h], psum[b][:, :], ALU.subtract).then_inc(free[b], 1)
                for n in range(2):
                    h = slice(n * HALF, (n + 1) * HALF)
                    B2.read(dve, s, ("sq3", n))
                    B2.read(dve, s, ("mu3", n))
                    ch.then(dve.reciprocal(ysq[:, h], ysq[:, h]))
                    ch.then(tt(yc[:, h], yc[:, h], ysq[:, h], ALU.mult))
                    ts(yc[:, h], yc[:, h], prm("ln3_g"), prm("ln3_b"), ALU.mult, ALU.add)\
                        .then_inc(S["yn_ready"], 1)

            def l3_mlp(s, n):
                B2.filled(dve, s, ("mlp", n))
                b = B2.bank(("mlp", n))
                ts(t3[n][:, :], psum[b][:, :], prm("b2"), prm("ls"), ALU.add, ALU.mult).then_inc(free[b], 1)
                B2.read(dve, s, ("mlp", n))
                xh = X[:, bass.ds(s, 1), n * HALF:(n + 1) * HALF].rearrange("p o n -> p (o n)")
                tt(xh, xh, t3[n][:, :], ALU.add).then_inc(S["x3_ready"], 1)

            def l0_unit(s, u):
                if u < NU:
                    l0_he(s, u)
                if u:
                    l0_acc(s, u - 1)

            run(dve, dict(s4d=s4d, weights=weights, l0_head=l0_head, l0_unit=l0_unit, l0_tail=l0_tail,
                          l1_norm=l1_norm, l1_om=l1_om, l1_index=l1_index, l1_share=l1_share, swap=swap,
                          sample=sample, dcn=dcn, l2_head=l2_head, l2_glu=l2_glu, l2_close=l2_close,
                          l3_head=l3_head, tap=tap, l3_norm=l3_norm, l3_mlp=l3_mlp), end=ch.restart)

        @block.tensor
        def _(pe):
            mm = pe.matmul
            for started in full + free:
                pe.sem_inc(started, FROM)
            pe.wait_ge(S["par_in"], 32)

            def weights(s):
                pe.wait_ge(S["w1_in"], 16)
                pe.wait_ge(S["w2_in"], 16)
                pe.wait_ge(S["wts_in"], 48)

            def s4d(s):
                pe.wait_ge(S["wg_done"], 1)
                for d in range(NB2):
                    op = mm(psum[4][:, 0:C], con("mean256"), wg2[:, d], start=d == 0, stop=d == NB2 - 1)
                op.then_inc(S["cm_done"], 1)
                for d in range(NB2):
                    op = mm(psum[3][:, 0:1], w_dec4[:, d], prm("ln2_b")[:, d:d + 1], start=d == 0, stop=d == NB2 - 1)
                op.then_inc(S["cm_done"], 1)
                pe.wait_ge(S["s4_done"], 1)
                for t in range(JJ):
                    for d in range(NB2):
                        op = pe.transpose(psum[5 + t // 2][:, (t % 2 * NB2 + d) * P:(t % 2 * NB2 + d + 1) * P],
                                          kw[:, d, t * JJ:(t + 1) * JJ].rearrange("p j s -> p (j s)"), ident)
                    if t % 2:
                        op.then_inc(S["k_turned"], 1)
                for d in range(NB2):
                    op = pe.transpose(psum[7][0:LM, d * P:(d + 1) * P], cor[:, d], ident)
                op.then_inc(S["k_turned"], 1)
                pe.wait_ge(S["k_there"], 1)
                pe.wait_ge(S["dec_there"], 1)

            def l0_head(s):
                pe.wait_ge(S["xp_in"], FROM + s * 256 + 256)
                B0.vacant(pe, s, "router")
                for t in range(8):
                    op = mm(psum[2][:, t * NE:(t + 1) * NE], xp[:, t // 2, t % 2 * P:(t % 2 + 1) * P],
                            prm("router"), start=True, stop=True)
                op.then_inc(full[2], 1)

            def l0_h(s, u):
                g, e = divmod(u, NE)
                for kind, b, first in (("gate", 0, 2), ("value", 1, 0)):
                    B0.vacant(pe, s, (kind, u))
                    for h in range(2):
                        op = mm(psum[b][:, h * TOK:(h + 1) * TOK], w1_sb[:, e, first + h], xp[:, g],
                                start=True, stop=True)
                    op.then_inc(full[b], 1)

            def l0_out(s, u):
                g, e = divmod(u, NE)
                B0.read(pe, s, ("value", u))
                B0.vacant(pe, s, ("out", u))
                for t in range(2):
                    for h in range(2):
                        op = mm(psum[2][:, t * D0:(t + 1) * D0],
                                he[:, u % 2, h * TOK + t * P:h * TOK + (t + 1) * P], w2_sb[:, e, h],
                                start=h == 0, stop=h == 1)
                op.then_inc(full[2], 1)

            def l0_tail(s):
                B0.read(pe, s, ("out", NU - 1))
                for t in range(2):
                    B0.vacant(pe, s, ("back", t))
                    for dyx in range(4):
                        op = pe.transpose(psum[t][:, dyx * P:(dyx + 1) * P], acc[:, t, dyx].rearrange("p g c -> p (g c)"),
                                          ident)
                    op.then_inc(full[t], 1)

            def l1_table(s, t):
                B0.vacant(pe, s, ("table", t))
                b = B0.bank(("table", t))
                for a in range(4):
                    at = t * P + a // 2 * PW + a % 2
                    op = pe.transpose(psum[b][:, a * P:(a + 1) * P], xpad[:, at:at + P], ident)
                op.then_inc(full[b], 1)

            def l1_conv(s):
                pe.wait_ge(S["xpad_ready"], s + 1)
                for n in range(2):
                    B0.vacant(pe, s, ("omc", n))
                    b = B0.bank(("omc", n))
                    for k in range(KK):
                        y0 = n * (H // 2) + k // 3
                        op = mm(psum[b][0:OMC, :], w_om[:, k],
                                xpad_v[:, y0:y0 + H // 2, k % 3:k % 3 + W], start=k == 0, stop=k == KK - 1)
                    op.then_inc(full[b], 1)
                for t in range(TRING):
                    l1_table(s, t)

            def l1_om(s):
                for n in range(2):
                    B0.read(pe, s, ("omc", n))
                    B0.vacant(pe, s, ("om", n))
                    b = B0.bank(("om", n))
                    for t in range(4):
                        at = (n * 4 + t) * P
                        op = pe.transpose(psum[b][:, t * OMC:(t + 1) * OMC], omt[0:OMC, at:at + P],
                                          ident[0:OMC, 0:OMC])
                    op.then_inc(full[b], 1)

            def turn(s, t):
                j, g = divmod(t, GI)
                pe.wait_ge(S["smp_ready"], FROM + s * NT * GI + t + 1)
                B1.vacant(pe, s, ("sampled", j, g))
                for k in range(3):
                    op = pe.transpose(psum[3][:, k * P:(k + 1) * P], sm[:, t % 2, k * P:(k + 1) * P], ident)
                op.then_inc(full[3], 1)

            def dcn(s, j):
                if j % 4 == 0:
                    B1.vacant(pe, s, ("dcn", j // 4))
                B1.read(pe, s, ("sampled", j, GI - 1))
                for k in range(3):
                    for g in range(GI):
                        op = mm(psum[4][g * C:(g + 1) * C, j % 4 * P:(j % 4 + 1) * P], w_dcn[:, k],
                                st[:, g, k * P:(k + 1) * P], start=k == 0, stop=k == 2)
                op.then_inc(full[4] if j % 4 == 3 else S["st_used"], 1)

            def l2_y(s, c):
                n, g = divmod(c, GI)
                if c == 0:
                    pe.wait_ge(S["u_in"], FROM + s * 256 + 256)
                for d in range(NB2):
                    name = ("y", c, d)
                    B2.vacant(pe, s, name)
                    o = psum[B2.bank(name)]
                    for t in range(JJ):
                        at = LM + n * HALF - JJ * t
                        op = mm(o[:, :], wk[:, t, d], u4[:, g, at:at + HALF], start=t == 0,
                                stop=t == JJ - 1 and n > 0)
                    if n == 0:
                        op = mm(o[:, 0:LM], corr[:, d], ident[0:LM, 0:LM], start=False, stop=True)
                    op.then_inc(full[B2.bank(name)], 1)

            def l2_glu(s, c):
                n, g = divmod(c, GI)
                B2.read(pe, s, ("y", c, NB2 - 1))
                B2.read(pe, s, ("y", c, 0))
                for d in range(NB2):
                    for kind, col in (("gb", DM), ("ga", 0)):
                        name = (kind, c, d)
                        B2.vacant(pe, s, name)
                        for k in range(NB2):
                            op = mm(psum[B2.bank(name)][:, :], w_glu[:, k, col + d * P:col + (d + 1) * P],
                                    yg[:, c % 2, k], start=k == 0, stop=k == NB2 - 1)
                        op.then_inc(full[B2.bank(name)], 1)
                    name = ("z", c, d)
                    B2.vacant(pe, s, name)
                    mm(psum[B2.bank(name)][:, :], wenc[:, d * P:(d + 1) * P],
                       u4[0:C, g, LM + n * HALF:LM + (n + 1) * HALF], start=True, stop=True)\
                        .then_inc(full[B2.bank(name)], 1)

            def l2_close(s, n):
                pe.wait_ge(S["sq_ready"], s * 8 * NB2 + (n + 1) * GI * NB2)
                B2.read(pe, s, ("z", n * GI + GI - 1, NB2 - 1))
                B2.read(pe, s, ("z", n * GI + GI - 1, 0))
                for kind, weight, src in (("dec", wdp, rb), ("mu", None, rb), ("sq", None, sqb)):
                    b = B2.bank((kind, n))
                    B2.vacant(pe, s, (kind, n))
                    for d in range(NB2):
                        for g in range(GI):
                            lhs = weight[:, d] if weight is not None else con("mean256")[:, 0:C]
                            op = mm(psum[b][g * C:(g + 1) * C, :], lhs, src[:, g, d], start=d == 0,
                                    stop=d == NB2 - 1)
                    op.then_inc(full[b], 1)

            def l3_norm(s):
                pe.wait_ge(S["y3_ready"], s + 1)
                for n in range(2):
                    b = B2.bank(("mu3", n))
                    B2.vacant(pe, s, ("mu3", n))
                    mm(psum[b][:, :], con("mean32"), ya[:, 0, n * HALF:(n + 1) * HALF], start=True, stop=True)\
                        .then_inc(full[b], 1)
                for n in range(2):
                    pe.wait_ge(S["ysq_ready"], s * 2 + n + 1)
                    b = B2.bank(("sq3", n))
                    B2.vacant(pe, s, ("sq3", n))
                    mm(psum[b][:, :], con("mean32"), ysq[:, n * HALF:(n + 1) * HALF], start=True, stop=True)\
                        .then_inc(full[b], 1)

            def l3_mlp(s, n):
                pe.wait_ge(S["yn_ready"], s * 2 + n + 1)
                for g in range(GI):
                    b = B2.bank(("hid", n, g))
                    B2.vacant(pe, s, ("hid", n, g))
                    mm(psum[b][:, :], wt("w1_3")[g * C:(g + 1) * C, :],
                       yc[g * C:(g + 1) * C, n * HALF:(n + 1) * HALF], start=True, stop=True)\
                        .then_inc(full[b], 1)
                b = B2.bank(("mlp", n))
                B2.vacant(pe, s, ("mlp", n))
                for g in range(GI - 3, GI):
                    B2.read(pe, s, ("hid", n, g))
                for g in range(GI):
                    op = mm(psum[b][g * C:(g + 1) * C, :], wt("w2_3"), hg[:, g], start=True, stop=True)
                op.then_inc(full[b], 1)

            def l0_unit(s, u):
                if u < NU:
                    l0_h(s, u)
                if u:
                    l0_out(s, u - 1)

            run(pe, dict(s4d=s4d, weights=weights, l0_head=l0_head, l0_unit=l0_unit, l0_tail=l0_tail,
                         l1_conv=l1_conv, l1_om=l1_om, l1_table=l1_table, turn=turn, dcn=dcn,
                         l2_y=l2_y, l2_glu=l2_glu, l2_close=l2_close, l3_norm=l3_norm, l3_mlp=l3_mlp))


def shape_constants():
    c = np.zeros((P, NCONST), np.float32)

    def put(name, a):
        lo, hi = CONSTS[name]
        c[:, lo:hi] = a.reshape(P, hi - lo)
    put("ident", np.eye(P, dtype=np.float32))
    put("image_row", np.broadcast_to(np.repeat(np.arange(GI) * TROWS, KK).astype(np.float32), (P, GI * KK)))
    put("mean32", np.kron(np.eye(GI), np.full((C, C), 1.0 / C)).astype(np.float32))
    put("mean256", np.full((P, P), 1.0 / DM, np.float32))
    put("rank", np.broadcast_to(np.arange(NE, 0, -1).astype(np.float32), (P, NE)))
    return c


def tap_places():
    base = np.zeros((P, NT, 3, GI, KK), np.float32)
    p, t, k = np.arange(P)[:, None, None], np.arange(NT)[None, :, None], np.arange(KK)[None, None, :]
    base[:, :, 0] = (t * (P // W) + p // W + k // 3)[:, :, None]
    base[:, :, 1] = (p % W + k % 3 + 0 * t)[:, :, None]
    return base.reshape(P, NT * OMC)


def lay_out(a):
    f = {n: np.asarray(v) for n, v in a.items()}
    L0, L1, L2, L3 = (f"L{i}_conv_" for i in range(4))

    def patch(w, axis):
        w = np.moveaxis(w, axis, 0)
        w = w.reshape((C, PT, PT) + w.shape[1:])
        w = np.moveaxis(w, 0, 2)
        return np.moveaxis(w.reshape((D0,) + w.shape[3:]), 0, axis)

    w1 = patch(f[L0 + "w1"], 1).transpose(1, 0, 2).reshape(P, NE * 4 * P)
    w2 = patch(f[L0 + "w2"], 2).reshape(NE, 2, P, D0).transpose(2, 0, 1, 3).reshape(P, NE * 2 * P)
    params = np.zeros((P, NPARAM), np.float32)

    def put(name, v):
        lo, hi = PARAMS[name]
        params[:, lo:hi] = v.reshape(P, hi - lo)

    def by_image(v):
        return np.concatenate([v.reshape(C, -1)] * GI, axis=0)

    def by_state(v):
        return v.reshape(NB2, P, -1).transpose(1, 0, 2)
    for name, src in (("l1_b", L1 + "b"), ("l1_gamma", L1 + "gamma"), ("l1_beta", L1 + "beta"),
                      ("l1_mean", L1 + "bn_mean"), ("l1_var", L1 + "bn_var"), ("b_dec", L2 + "b_dec"),
                      ("dw_b", L3 + "dw_b"), ("ln3_g", L3 + "ln_g"), ("ln3_b", L3 + "ln_b"),
                      ("b2", L3 + "b2"), ("ls", L3 + "ls"), ("dw", L3 + "dw_w")):
        put(name, by_image(f[src]))
    put("b1", f[L3 + "b1"])
    for name, src in (("b_enc", "b_enc"), ("log_dt", "log_dt"), ("a_real", "A_log_real"), ("a_imag", "A_imag"),
                      ("c_real", "C_real"), ("c_imag", "C_imag"), ("d", "D"), ("ln2_g", "ln_gamma"),
                      ("ln2_b", "ln_beta")):
        put(name, by_state(f[L2 + src]))
    put("b_glu", f[L2 + "b_glu"].reshape(2 * NB2, P).T)
    put("w_enc_t", f[L2 + "W_enc"].T.reshape(NB2, P, C).transpose(1, 0, 2))
    kinds = [list(range(0, 2 * KK, 2)), list(range(1, 2 * KK, 2)), list(range(2 * KK, 3 * KK))]
    b_om = np.stack([f[L1 + "b_om"][k] for k in kinds])
    put("b_om", np.broadcast_to(b_om[:, None], (3, GI, KK)).reshape(1, OMC).repeat(P, 0))
    put("router", patch(f[L0 + "router_w"], 0))

    weights = np.zeros((P, NWEIGHT), np.float32)

    def put_w(name, v):
        lo, hi = WEIGHTS[name]
        weights[:, lo:hi] = v.reshape(P, hi - lo)
    w_om = np.zeros((GI, C, KK, 3, GI, KK), np.float32)
    per = np.stack([f[L1 + "w_om"][k] for k in kinds]).reshape(3, KK, C, KK)
    for g in range(GI):
        w_om[g, :, :, :, g] = per.transpose(2, 3, 0, 1)
    put_w("w_om", w_om)
    w_dcn = np.zeros((3 * P, C), np.float32)
    w_dcn[:KK * C] = f[L1 + "w"].reshape(C, C, KK).transpose(2, 1, 0).reshape(KK * C, C)
    put_w("w_dcn", w_dcn.reshape(3, P, C).transpose(1, 0, 2))
    put_w("w_glu", f[L2 + "W_glu"].reshape(NB2, P, 2 * DM).transpose(1, 0, 2))
    w_dec = f[L2 + "W_dec"].reshape(NB2, P, C).transpose(1, 0, 2)
    put_w("w_dec", np.concatenate([w_dec] * GI, axis=2))
    put_w("w1_3", np.concatenate([f[L3 + "w1"].T] * GI, axis=0))
    put_w("w2_3", f[L3 + "w2"].T)
    return {"x": f["x"], "w1": w1, "w2": w2, "w_enc": f[L2 + "W_enc"], "params": params,
            "consts": shape_constants(), "weights": weights,
            "places": tap_places()}


def kernel(**inputs):
    import concourse.bacc as _bacc
    from concourse.bass_utils import run_bass_kernel_spmd as _run

    nc = _bacc.Bacc("TRN2", target_bir_lowering=False, num_devices=1)
    arrays = {k: np.ascontiguousarray(v) for k, v in lay_out(inputs).items()}
    args = [nc.dram_tensor(name, a.shape, mybir.dt.from_np(a.dtype), kind="ExternalInput").ap()
            for name, a in arrays.items()]
    out = nc.dram_tensor("out", (B, C, H, W), F32, kind="ExternalOutput").ap()
    build(nc, *args, out)
    r = _run(nc, [arrays], core_ids=[0])
    return r.results[0]["out"]
```

```python
from contextlib import ExitStack

import numpy as np

import concourse.bass as bass
from concourse import mybir

B, C, H, W = 16, 32, 32, 32
P = 128
GI = P // C
NS = B // GI
HW = H * W
HALF = 512
EPS = 1e-5
PT = 2
NE = 8
HID = 256
TOK = (H // PT) * (W // PT)
D0 = C * PT * PT
NU = GI * NE
KK = 9
OMC = 3 * GI * KK
PW = W + 2
TQ = 9
TROWS = TQ * P
TRING = 2
PADLEN = 1200
NT = HW // P
DM = 256
NB2 = DM // P
NST = 4
LM = 16
JJ = 4
UL = LM + HW + 4
K7 = 7
DRING = HALF // P
A_PLACES = [(0, 2, 6), (2, 17, 9), (17, 22.5, NU + 2 - 15), (22.5, 23.6, 2), (25.2, 27.8, 3 + TQ - 2)]
C_PLACES = [(0, 1, 1), (3, 17, 22), (17, 17.5, 1), (17.5, 28.5, K7 * K7), (29, 32, 7)]
LATE_PLACES = (27.9, 28.1, 28.6, 30.1)
PE_TAPS, LAST_PE_TAPS = 11, 20
FROM = 1
PW3 = W + K7 - 1

F32 = mybir.dt.float32
I32 = mybir.dt.int32
U32 = mybir.dt.uint32
ALU = mybir.AluOpType
ACT = mybir.ActivationFunctionType
AX = mybir.AxisListType


def columns(fields):
    at, out = 0, {}
    for name, n in fields:
        out[name] = (at, at + n)
        at += n
    return out, at


PARAMS, NPARAM = columns([
    ("l1_b", 1), ("l1_gamma", 1), ("l1_beta", 1), ("l1_mean", 1), ("l1_var", 1), ("b_dec", 1),
    ("dw_b", 1), ("ln3_g", 1), ("ln3_b", 1), ("b2", 1), ("ls", 1), ("dw", K7 * K7), ("b1", 1),
    ("b_enc", NB2), ("log_dt", NB2), ("a_real", NB2 * NST), ("a_imag", NB2 * NST),
    ("c_real", NB2 * NST), ("c_imag", NB2 * NST), ("d", NB2), ("b_glu", 2 * NB2),
    ("ln2_g", NB2), ("ln2_b", NB2), ("w_enc_t", NB2 * C), ("b_om", OMC), ("router", NE),
])
CONSTS, NCONST = columns([
    ("ident", P), ("image_row", GI * KK), ("mean32", P), ("mean256", P),
    ("rank", NE),
])
WEIGHTS, NWEIGHT = columns([
    ("w_om", KK * OMC), ("w_dcn", 3 * C), ("w_glu", NB2 * 2 * DM), ("w_dec", NB2 * P),
    ("w1_3", GI * P), ("w2_3", C),
])


class Banks:

    def __init__(self, full, free, plan):
        self.full, self.free = full, free
        self.where, self.per = {}, {}
        for name, bank in plan:
            self.where[name] = (bank, self.per.get(bank, 0))
            self.per[bank] = self.per.get(bank, 0) + 1

    def bank(self, name):
        return self.where[name][0]

    def vacant(self, eng, s, name):
        b, k = self.where[name]
        eng.wait_ge(self.free[b], FROM + s * self.per[b] + k)

    def filled(self, eng, s, name):
        b, k = self.where[name]
        eng.wait_ge(self.full[b], FROM + s * self.per[b] + k + 1)

    def read(self, eng, s, name):
        b, k = self.where[name]
        eng.wait_ge(self.free[b], FROM + s * self.per[b] + k + 1)

    def last_step_filled(self, eng, s, bank):
        eng.wait_ge(self.full[bank], FROM + s * self.per[bank])


class Chain:

    def __init__(self, eng, sem):
        self.eng, self.sem, self.n = eng, sem, 0

    def did(self, op):
        op.then_inc(self.sem, 1)
        self.n += 1
        return self.n

    def wait(self, n=None):
        self.eng.wait_ge(self.sem, self.n if n is None else n)

    def then(self, op):
        self.did(op)
        self.wait()

    def restart(self):
        self.wait()
        self.eng.sem_clear(self.sem)
        self.n = 0


def plan_a():
    plan = [(("xp", 0), 0), (("xp", 1), 1), ("router", 2)]
    for u in range(NU):
        plan += [(("gate", u), 0), (("value", u), 1)]
        if u:
            plan.append((("out", u - 1), 2))
    plan += [(("out", NU - 1), 2), (("back", 0), 0), (("back", 1), 1)]
    head = [("omc", 0), ("omc", 1), ("table", 0), ("table", 1), ("om", 0), ("om", 1)]
    head += [("table", t) for t in range(2, TQ)]
    return plan + [(name, (i + 2) % 3) for i, name in enumerate(head)]


def plan_b():
    plan = []
    for half in range(2):
        plan.append((("dcn", half), 4))
        plan += [(("sampled", half * 4 + j, g), 3) for j in range(4) for g in range(GI)]
    return plan


def plan_c():
    names = []
    for kind, *k in order_c():
        if kind == "l2_y":
            names += [("y", k[0], d) for d in range(NB2)]
        elif kind == "l2_glu":
            for d in range(NB2):
                names += [("gb", k[0], d), ("ga", k[0], d), ("z", k[0], d)]
        elif kind == "l2_close":
            names += [(x, k[0]) for x in ("mu", "sq", "dec")]
    names += [("tap", 0), ("tap", 1), ("mu3", 0), ("mu3", 1), ("sq3", 0), ("sq3", 1)]
    for n in range(2):
        names += [("hid", n, g) for g in range(GI)] + [("mlp", n)]
    return [(name, 5 + i % 3) for i, name in enumerate(names)]


def order_a():
    parts = [("l0_unit", u) for u in range(NU + 1)] + [("l0_tail",), ("l1_norm",), ("l1_conv",), ("l1_om",)]
    parts += [("l1_table", t) for t in range(2, TQ)]
    parts.insert(parts.index(("l1_table", 3)), ("l1_index",))
    parts.insert(parts.index(("l1_table", 5)), ("l1_share",))
    return parts


def order_b():
    parts = []
    for t in range(NT * GI + 1):
        if t:
            parts.append((t, "turn", t - 1))
        if t and t % GI == 0:
            parts.append((t, "dcn", t // GI - 1))
        if t < NT * GI:
            parts.append((t, "sample", t))
    return parts


def order_c(pe_taps=PE_TAPS):
    parts = [("l2_head",), ("l2_y", 0)]
    for c in range(2 * GI):
        if c < 2 * GI - 1:
            parts.append(("l2_y", c + 1))
        if c == GI:
            parts += [("l2_close", 0), ("l2_var", 0), ("l2_end", 0)]
        parts.append(("l2_glu", c))
    parts += [("l2_close", 1), ("l2_var", 1), ("l2_end", 1)]
    parts.append(("l3_head",))
    mine = K7 * K7 - pe_taps
    done = 0
    for t in range(mine):
        parts.append(("tap", t))
        while done < (t + 1) * pe_taps // mine:
            parts.append(("pe_tap", mine + done, pe_taps))
            done += 1
    parts += [("l3_sum",), ("l3_center",), ("l3_scale",)]
    return parts + [(kind, n) for n in range(2) for kind in ("l3_mlp", "l3_add")]


def spread(stage, parts, places):
    out, parts = [], list(parts)
    for lo, hi, n in places:
        for i in range(n):
            out.append((lo + (i + 0.5) * (hi - lo) / n, stage, *parts.pop(0)))
    assert not parts
    return out


def order(a, b, c):
    if not b and a:
        parts = [("a", *x) for x in order_a()]
        parts.insert(parts.index(("a", "l0_tail")), ("a", "load_conv"))
        parts.insert(parts.index(("a", "l1_index")), ("a", "s4d"))
        head = ("l0_head", "l0_spread", "l0_route")
        parts = [("head", x) for x in head] + [("a", "load_experts")] + parts
        return parts + [("a", "swap", 0), ("a", "swap", 1)] + [("next", x) for x in head]
    if not b:
        return [("c", *x) for x in order_c(LAST_PE_TAPS)]
    parts = [(t, "b", *x) for t, *x in order_b()]
    if c:
        parts += spread("c", order_c(), C_PLACES)
    if a:
        parts += spread("a", order_a(), A_PLACES)
        late = [("a", "swap", 0), ("next", "l0_head"), ("next", "l0_spread"), ("next", "l0_route")]
        parts += [(at, *x) for at, x in zip(LATE_PLACES, late)]
        parts.append((NT * GI, "a", "swap", 1))
    return [x[1:] for x in sorted(parts, key=lambda x: x[0])]


def build(nc, x, w1, w2, w_enc, params, consts, weights, places, out):
    x_v = x.rearrange("(s b) c h w -> (b c) s (h w)", s=NS)
    out_v = out.rearrange("(s b) c h w -> (b c) s (h w)", s=NS)
    table = nc.dram_tensor("corner_table", (2 * GI * TROWS, 4 * C), F32, kind="Internal").ap()

    with ExitStack() as ctx:
        def sb(name, shape, dt=F32):
            return ctx.enter_context(nc.sbuf_tensor(name, shape, dt))

        def sem(name):
            return ctx.enter_context(nc.semaphore(name))

        psum = [ctx.enter_context(nc.psum_tensor(f"bank{b}", [P, HALF], F32)) for b in range(8)]
        full = [sem(f"bank{b}_full") for b in range(8)]
        free = [sem(f"bank{b}_free") for b in range(8)]
        B0, B1, B2 = (Banks(full, free, plan) for plan in (plan_a(), plan_b(), plan_c()))

        par = sb("par", [P, NPARAM])
        cst = sb("cst", [P, NCONST])
        wts = sb("wts", [P, NWEIGHT])
        w1_sb = sb("w1_sb", [P, NE, 4, P])
        w2_sb = sb("w2_sb", [P, NE, 2, P])
        wenc = sb("wenc", [P, DM])

        def prm(name):
            a, b = PARAMS[name]
            return par[:, a:b]

        def con(name):
            a, b = CONSTS[name]
            return cst[:, a:b]

        def wt(name):
            a, b = WEIGHTS[name]
            return wts[:, a:b]

        ident = con("ident")
        w_om = wt("w_om").rearrange("p (k m) -> p k m", k=KK)
        w_dcn = wt("w_dcn").rearrange("p (b m) -> p b m", b=3)
        w_glu = wt("w_glu").rearrange("p (k m) -> p k m", k=NB2)
        w1_3 = wt("w1_3").rearrange("p (g m) -> p g m", g=GI)
        w_dec4 = wt("w_dec").rearrange("p (k m) -> p k m", k=NB2)

        X = sb("X", [P, NS, HW])
        bst = sb("bst", [P, 4, 2, 6])
        mv = sb("mv", [P, 4, 2])
        std = sb("std", [P, 4])
        rs = sb("rs", [P, 4])
        epst = sb("epst", [P, 1])
        b2ls = sb("b2ls", [P, 1])

        xp = sb("xp", [P, GI, TOK])
        lg = sb("lg", [P, 8, NE])
        ex = sb("ex", [P, 8, NE])
        m1 = sb("m1", [P, 8])
        oh = sb("oh", [P, 8, NE])
        oh2 = sb("oh2", [P, 8, NE])
        gate = sb("gate", [P, 8, NE])
        he = sb("he", [P, 2, HALF])
        acc = sb("acc", [P, 2, PT * PT, GI, C])
        xn0 = acc[:, :, :, :, :].rearrange("p t a g c -> p (t a g c)")

        xpad = sb("xpad", [P, PADLEN])
        bb = sb("bb", [P, NT, OMC])
        NK = GI * KK
        NXY = 2 * NK
        cwn = sb("cwn", [P, NT, NK, 4])
        om = cwn[:, :, :, :].rearrange("p t k a -> p (t k a)")[:, 0:NT * OMC].rearrange("p (t m) -> p t m", t=NT)
        fl = sb("fl", [P, NT, 2 * NK])
        fi = fl[:, :, :].bitcast(I32)
        fr = sb("fr", [P, NT, 2 * NK])
        mk = sb("mk", [P, NT, NK])
        mk1 = sb("mk1", [P, NT, NK])
        idxn = sb("idxn", [P, NT, NK], U32)
        idx = sb("idx", [P, NT, NK], U32)
        cw = sb("cw", [P, NT, NK, 4])
        rowoff = sb("rowoff", [P, 1])
        tb = sb("tb", [P, TRING, GI, 4 * C])
        gt = sb("gt", [P, GI, KK, 4, C])
        sm = sb("sm", [P, 2, 3 * P])
        st = sb("st", [P, GI, 3 * P])
        omt = acc[:, :, :, :, :].rearrange("p t a g c -> p (t a g c)")
        r1 = sb("r1", [P, HALF])
        sc1 = sb("sc1", [P, 1])
        bi1 = sb("bi1", [P, 1])

        u4 = sb("u4", [P, GI, UL])
        wk = sb("wk", [P, JJ, NB2, P])
        corr = sb("corr", [LM, NB2, P])
        yg = sb("yg", [P, 2, NB2, HALF])
        tg = sb("tg", [P, 2, HALF])
        ae = sb("ae", [P, 2, HALF])
        rb = sb("rb", [P, GI, NB2, HALF])
        sqb = sb("sqb", [P, GI, NB2, HALF])
        xn2 = sqb[:, GI - 1].rearrange("p d n -> p (d n)")
        musq = sb("musq", [P, HALF])
        var2 = sb("var2", [P, HALF])
        hb_glu = sb("hb_glu", [P, 2 * NB2])
        wdp = sb("wdp", [P, NB2, C])
        wg2 = sb("wg2", [P, NB2, C])
        dconst = sb("dconst", [P, 1])
        dt_t = sb("dt_t", [P, NB2])
        gflat = gt[:, :, :, :, :].rearrange("p g k a c -> p (g k a c)")
        nv = NB2 * NST * LM
        vr = gflat[:, 0:nv].rearrange("p (d n l) -> p d n l", d=NB2, n=NST)
        vi = gflat[:, nv:2 * nv].rearrange("p (d n l) -> p d n l", d=NB2, n=NST)
        kw = gflat[:, 2 * nv:2 * nv + NB2 * LM * C].rearrange("p (d l s) -> p d l s", d=NB2, l=LM)
        at = 2 * nv + NB2 * LM * C
        v1, v2 = (gflat[:, at + i * nv // 2:at + (i + 1) * nv // 2]
                  .rearrange("p (d n l) -> p d n l", d=NB2, n=NST) for i in range(2))
        at += nv
        kr, cum, cor = (gflat[:, at + a * NB2 * LM:at + b * NB2 * LM].rearrange("p (i d l) -> p i d l", d=NB2, l=LM)
                        for a, b in ((0, 4), (4, 6), (6, 7)))
        cor = cor[:, 0]
        at += 7 * NB2 * LM
        s4 = {}
        for n in ("ea ar am ra zr zi hr hi t1 t2 t3 t4 wr wi er ei cr ci").split():
            s4[n] = gflat[:, at:at + NB2 * NST].rearrange("p (d n) -> p d n", d=NB2)
            at += NB2 * NST
        cb15 = sb("cb15", [P, NB2])

        xp3 = sb("xp3", [P, PW3 * PW3])
        rbf = rb[:, :, :, :].rearrange("p g d n -> p (g d n)")
        sqf = sqb[:, :, :, :].rearrange("p g d n -> p (g d n)")
        ya = rbf[:, 0:2 * HW].rearrange("p (i n) -> p i n", i=2)
        yc, ysq = sqf[:, 0:HW], sqf[:, HW:2 * HW]
        hg = yg[:, :, :, :].rearrange("p a d n -> p (a d) n")
        t3 = (musq, var2)
        diag = musq[:, :].rearrange("p (i m) -> p i m", i=DRING)

        xpad_v = xpad[:, 0:PW * PW].rearrange("p (y x) -> p y x", y=PW)
        xp3_v = xp3[:, :].rearrange("p (y x) -> p y x", y=PW3)

        names = """x0_in x_in par_in wts_in w1_in w2_in table_zero zeros_set exp_done a_inv eps_set s1_std
            s4_done wg_done cm_done k_turned k_there dec_there
            var_ready0 var_ready1 var_ready2 var_ready3 std_ready0 std_ready1 std_ready2 std_ready3
            xn0_ready max_ready exp_ready
            xpad_ready om_ready mask_ready idx_ready smp_ready st_used x1_added
            u_ready glu_done sq_ready ln2_ready rstd2_ready x2_added
            xp3_ready diag_ready diag_used ysq_ready rstd3_ready yz_ready yn_ready x3_ready out_done
            dve_chain act_chain pool_chain held""".split()
        S = {n: sem(n) for n in names}
        table_out = [sem(f"table_out{t}") for t in range(TRING)]
        u_in = [sem(f"u_in{g}") for g in range(GI)]
        gathered = [sem(f"gathered{g}") for g in range(GI)]

        block = ctx.enter_context(nc.Block())

        def hold(eng):
            eng.sem_inc(S["held"])

        def run(eng, parts, end=None):
            def body(s, a, b, c):
                step = {"head": s + 1, "next": s + 2, "a": s + 1, "b": s, "c": s - 1}
                for stage, name, *args in order(a, b, c):
                    if name in parts:
                        parts[name](step[stage], *args)
                if end:
                    end()
            body(-1, True, False, False)
            body(0, True, True, False)
            with eng.Fori(1, NS - 1) as s:
                body(s, True, True, True)
            body(NS - 1, False, True, True)
            body(NS, False, False, True)

        @block.sync
        def _(sp):
            sp.dma_start(X[:, 0], x_v[:, 0]).then_inc(S["x0_in"], 16)
            sp.dma_start(par[:, :], params).then_inc(S["par_in"], 16)
            sp.dma_start(cst[:, :], consts).then_inc(S["par_in"], 16)
            sp.dma_start(wts[:, :], weights).then_inc(S["wts_in"], 16)
            sp.dma_start(bb[:, :, :].rearrange("p t m -> p (t m)"), places).then_inc(S["wts_in"], 16)
            sp.dma_start(wenc[:, :], w_enc).then_inc(S["wts_in"], 16)
            sp.dma_start(X[:, 1:NS], x_v[:, 1:NS]).then_inc(S["x_in"], 16)
            for started in u_in + table_out:
                sp.sem_inc(started, FROM)
            sp.wait_ge(S["zeros_set"], 1)
            tables = table.rearrange("(h g q p) e -> h q p g e", h=2, g=GI, p=P)
            for t in range(TQ):
                sp.dma_start(tables[1, t], tb[:, 0]).then_inc(S["table_zero"], 16)

            def l1_table(s, t):
                if t == 0 and (not isinstance(s, int) or s > 1):
                    sp.wait_ge(S["smp_ready"], FROM + (s - 1) * NT * GI)
                    hold(sp)
                B0.read(sp, s, ("table", t))
                hold(sp)
                half = s % 2
                dst = tables[half, t] if isinstance(half, int) else tables[bass.ds(half, 1), t]
                if not isinstance(half, int):
                    dst = dst.rearrange("h p g e -> p (h g) e")
                sp.dma_start(dst, tb[:, t % TRING]).then_inc(table_out[t % TRING], 16)

            def l1_conv(s):
                for t in range(TRING):
                    l1_table(s, t)

            def l2_head(s):
                sp.wait_ge(S["u_ready"], s + 1)
                hold(sp)
                B2.last_step_filled(sp, s, 5)
                hold(sp)
                for g in range(GI):
                    for j in range(JJ):
                        sp.dma_start(u4[j * C:(j + 1) * C, g, LM + j:LM + j + HW],
                                     xn2[g * C:(g + 1) * C, :]).then_inc(u_in[g], 16)

            def l3_add(s, n):
                sp.wait_ge(S["x3_ready"], s * 2 + n + 1)
                hold(sp)
                sp.dma_start(out_v[:, bass.ds(s, 1), n * HALF:(n + 1) * HALF],
                             X[:, bass.ds(s, 1), n * HALF:(n + 1) * HALF]).then_inc(S["out_done"], 16)

            run(sp, dict(l1_conv=l1_conv, l1_table=l1_table, l2_head=l2_head, l3_add=l3_add))
            sp.wait_ge(S["out_done"], 16 * 2 * NS)

        @block.gpsimd
        def _(pool):
            ch = Chain(pool, S["pool_chain"])
            pool.memset(u4[:, :, :], 0.0)
            pool.memset(xp3[:, :], 0.0)
            pool.memset(xpad[:, :], 0.0)
            pool.memset(sm[:, :, :], 0.0)
            pool.memset(rowoff[:, :], 0.0)
            pool.memset(tb[:, :, :, :], 0.0).then_inc(S["zeros_set"], 1)

            def mul(o, a, b):
                ch.did(pool.tensor_tensor(o, a, b, ALU.mult))

            def add(o, a, b, op=ALU.add):
                ch.did(pool.tensor_tensor(o, a, b, op))

            def cmul(ore, oim, ar, ai, br, bi, ta, tb_):
                mul(ta[0], ar, br)
                mul(ta[1], ai, bi)
                mul(tb_[0], ar, bi)
                mul(tb_[1], ai, br)
                ch.wait()
                add(ore, ta[0], ta[1], ALU.subtract)
                add(oim, tb_[0], tb_[1])
                ch.wait()

            q = {n: t[:, :, :] for n, t in s4.items()}
            ta, tb_ = (q["t1"], q["t2"]), (q["t3"], q["t4"])
            pool.wait_ge(S["a_inv"], 1)
            pool.wait_ge(S["par_in"], 32)
            a_im = prm("a_imag").rearrange("p (d n) -> p d n", d=NB2)
            dt_b = dt_t[:, :].unsqueeze(2).to_broadcast([P, NB2, NST])
            mul(q["t1"], q["ar"], dt_b)
            mul(q["t2"], a_im, dt_b)
            ch.wait()
            ch.did(pool.tensor_scalar(q["zr"], q["t1"], 2.0 ** -6, None, ALU.mult))
            ch.did(pool.tensor_scalar(q["zi"], q["t2"], 2.0 ** -6, None, ALU.mult))
            ch.did(pool.memset(q["hr"], 1.0))
            ch.did(pool.memset(q["hi"], 0.0))
            ch.wait()
            for k in range(9, 1, -1):
                cmul(q["wr"], q["wi"], q["zr"], q["zi"], q["hr"], q["hi"], ta, tb_)
                ch.did(pool.tensor_scalar(q["hr"], q["wr"], 1.0 / k, 1.0, ALU.mult, ALU.add))
                ch.did(pool.tensor_scalar(q["hi"], q["wi"], 1.0 / k, None, ALU.mult))
                ch.wait()
            cmul(q["wr"], q["wi"], q["zr"], q["zi"], q["hr"], q["hi"], ta, tb_)
            for _ in range(6):
                ch.did(pool.tensor_scalar(q["hr"], q["wr"], 2.0, None, ALU.add))
                ch.wait()
                cmul(q["er"], q["ei"], q["wr"], q["wi"], q["hr"], q["wi"], ta, tb_)
                ch.did(pool.tensor_copy(q["wr"], q["er"]))
                ch.did(pool.tensor_copy(q["wi"], q["ei"]))
                ch.wait()
            ch.did(pool.tensor_scalar(q["er"], q["wr"], 1.0, None, ALU.add))
            ch.did(pool.tensor_scalar(q["hi"], a_im, -1.0, None, ALU.mult))
            ch.wait()
            cmul(q["zr"], q["zi"], q["wr"], q["wi"], q["ar"], q["hi"], ta, tb_)
            mul(q["hr"], q["zr"], q["ra"])
            mul(q["wr"], q["zi"], q["ra"])
            ch.wait()
            c_re = prm("c_real").rearrange("p (d n) -> p d n", d=NB2)
            c_im = prm("c_imag").rearrange("p (d n) -> p d n", d=NB2)
            cmul(vr[:, :, :, 0], vi[:, :, :, 0], c_re, c_im, q["hr"], q["wr"], ta, tb_)
            er, ei, nr, ni = q["er"], q["wi"], q["cr"], q["ci"]
            m = 1
            while m < LM:
                eb = er.unsqueeze(3).to_broadcast([P, NB2, NST, m])
                ib = ei.unsqueeze(3).to_broadcast([P, NB2, NST, m])
                for d in range(NB2):
                    mul(v1[:, d, :, 0:m], vr[:, d, :, 0:m], eb[:, d])
                    mul(v2[:, d, :, 0:m], vi[:, d, :, 0:m], ib[:, d])
                    ch.wait()
                    add(vr[:, d, :, m:2 * m], v1[:, d, :, 0:m], v2[:, d, :, 0:m], ALU.subtract)
                    ch.wait()
                    mul(v1[:, d, :, 0:m], vr[:, d, :, 0:m], ib[:, d])
                    mul(v2[:, d, :, 0:m], vi[:, d, :, 0:m], eb[:, d])
                    ch.wait()
                    add(vi[:, d, :, m:2 * m], v1[:, d, :, 0:m], v2[:, d, :, 0:m])
                    ch.wait()
                m *= 2
                if m < LM:
                    cmul(nr, ni, er, ei, er, ei, ta, tb_)
                    er, ei, nr, ni = nr, ni, er, ei
            add(kr[:, 0], vr[:, :, 0], vr[:, :, 1])
            add(kr[:, 1], vr[:, :, 2], vr[:, :, 3])
            ch.wait()
            add(kr[:, 2], kr[:, 0], kr[:, 1])
            ch.wait()
            ch.did(pool.tensor_scalar(kr[:, 3], kr[:, 2], 2.0, None, ALU.mult))
            ch.wait()
            add(kr[:, 3, :, 0], kr[:, 3, :, 0], prm("d"))
            ch.wait()
            src, dst, sh = kr[:, 3], cum[:, 0], 1
            while sh < LM:
                ch.did(pool.tensor_copy(dst[:, :, 0:sh], src[:, :, 0:sh]))
                add(dst[:, :, sh:LM], src[:, :, sh:LM], src[:, :, 0:LM - sh])
                ch.wait()
                src, dst, sh = dst, cum[:, 1] if sh in (1, 4) else cum[:, 0], sh * 2
            b_enc = prm("b_enc")
            mul(cb15[:, :], src[:, :, LM - 1], b_enc)
            add(kr[:, 0], src, src[:, :, LM - 1:LM].to_broadcast([P, NB2, LM]), ALU.subtract)
            ch.wait()
            mul(cor[:, :, :], kr[:, 0], b_enc.unsqueeze(2).to_broadcast([P, NB2, LM]))
            enc_t = prm("w_enc_t").rearrange("p (d s) -> p d s", d=NB2)
            for d in range(NB2):
                mul(kw[:, d], enc_t[:, d].unsqueeze(1).to_broadcast([P, LM, C]),
                    kr[:, 3, d].unsqueeze(2).to_broadcast([P, LM, C]))
            ch.wait()
            pool.memset(q["t1"], 0.0).then_inc(S["s4_done"], 1)

            def sample(s, t):
                j, g = divmod(t, GI)
                if j in (0, NT - 1) and g == 0:
                    pool.wait_ge(S["idx_ready"], s * 2 + 1 + j // (NT - 1))
                if t == 0:
                    if isinstance(s, int):
                        pool.wait_ge(S["table_zero"], 16 * TQ)
                        pool.wait_ge(S["k_turned"], 3)
                    for i in range(TRING):
                        pool.wait_ge(table_out[i], FROM + (s + 1) * 16 * len(range(i, TQ, TRING)))
                if not isinstance(s, int) or s or t >= GI:
                    pool.wait_ge(S["smp_ready"], FROM + s * NT * GI + t - GI + 1)
                hold(pool)
                for k in range(KK):
                    pool.indirect_dma_start(
                        gt[:, g, k].rearrange("p a c -> p (a c)"), None, table,
                        bass.IndirectOffsetOnAxis(ap=idx[:, j, g * KK + k:g * KK + k + 1], axis=0),
                    ).then_inc(gathered[g], 16)

            run(pool, dict(sample=sample))

        @block.scalar
        def _(act):
            for e in range(0, NE, NE // 2):
                half = slice(e, e + NE // 2)
                act.dma_start(w1_sb[:, half].rearrange("p e b m -> p (e b m)"),
                              w1[:, e * 4 * P:(e + NE // 2) * 4 * P]).then_inc(S["w1_in"], 16)
                act.dma_start(w2_sb[:, half].rearrange("p e b m -> p (e b m)"),
                              w2[:, e * 2 * P:(e + NE // 2) * 2 * P]).then_inc(S["w2_in"], 16)
            act.wait_ge(S["par_in"], 32)
            act.activation(dt_t[:, :], prm("log_dt"), ACT.Exp)
            act.activation(s4["ea"][:, :, :], prm("a_real").rearrange("p (d n) -> p d n", d=NB2), ACT.Exp)\
               .then_inc(S["exp_done"], 1)
            act.activation(hb_glu[:, :], prm("b_glu"), ACT.Copy, scale=0.5).then_inc(S["act_chain"], 1)
            act.wait_ge(S["act_chain"], 1)
            act.wait_ge(S["eps_set"], 1)
            act.activation(std[:, 0:1], prm("l1_var"), ACT.Sqrt, bias=epst[:, :]).then_inc(S["s1_std"], 1)

            def s4d(s):
                act.wait_ge(S["k_turned"], 1)
                act.activation(wk[:, 0:2].rearrange("p t d m -> p (t d m)"), psum[5][:, :], ACT.Copy)
                act.wait_ge(S["k_turned"], 2)
                act.activation(wk[:, 2:4].rearrange("p t d m -> p (t d m)"), psum[6][:, :], ACT.Copy)
                act.wait_ge(S["k_turned"], 3)
                act.activation(corr[:, :, :].rearrange("p d m -> p (d m)"), psum[7][0:LM, 0:NB2 * P], ACT.Copy)\
                   .then_inc(S["k_there"], 1)

            def root(s, layer):
                act.wait_ge(S[f"var_ready{layer}"], s + 1)
                act.activation(std[:, layer:layer + 1], mv[:, layer, 1:2], ACT.Sqrt, bias=epst[:, :])\
                   .then_inc(S[f"std_ready{layer}"], 1)

            def l0_spread(s):
                for b in range(2):
                    B0.filled(act, s, ("xp", b))
                    act.activation(xp[:, 2 * b:2 * b + 2].rearrange("p g n -> p (g n)"), psum[b][:, :], ACT.Copy)\
                       .then_inc(free[b], 1)

            def l0_route(s):
                act.wait_ge(S["max_ready"], s + 1)
                act.activation(ex[:, :, :], lg[:, :, :], ACT.Exp).then_inc(S["exp_ready"], 1)

            def l0_unit(s, u):
                if u == NU:
                    return
                B0.filled(act, s, ("gate", u))
                if u >= 2:
                    B0.filled(act, s, ("out", u - 2))
                act.activation(he[:, u % 2], psum[0][:, :], ACT.Tanh, scale=0.5).then_inc(free[0], 1)

            def l1_conv(s):
                for n in range(2):
                    b = B0.bank(("omc", n))
                    B0.filled(act, s, ("omc", n))
                    act.activation(omt[0:OMC, n * HALF:(n + 1) * HALF], psum[b][0:OMC, :], ACT.Copy)\
                       .then_inc(free[b], 1)
                for t in range(TRING):
                    l1_table(s, t)

            def l1_table(s, t):
                b = B0.bank(("table", t))
                B0.filled(act, s, ("table", t))
                if isinstance(s, int) and s == 0 and t == 0:
                    act.wait_ge(S["table_zero"], 16 * TQ)
                act.wait_ge(table_out[t % TRING],
                            FROM + 16 * (s * len(range(t % TRING, TQ, TRING)) + t // TRING))
                act.activation(tb[:, t % TRING].rearrange("p g (a c) -> p a g c", a=4),
                               psum[b][:, :].rearrange("p (a g c) -> p a g c", a=4, g=GI), ACT.Copy)\
                   .then_inc(free[b], 1)

            def l1_index(s):
                act.wait_ge(S["om_ready"], s + 1)
                act.activation(mk[:, :, :], om[:, :, 2 * NK:OMC], ACT.Tanh, scale=0.5)\
                   .then_inc(S["mask_ready"], 1)

            def turn(s, t):
                j, g = divmod(t, GI)
                B1.filled(act, s, ("sampled", j, g))
                if g == 0:
                    if j % 4:
                        act.wait_ge(S["st_used"], s * 6 + j // 4 * 3 + j % 4)
                    elif j:
                        B1.filled(act, s, ("dcn", 0))
                    else:
                        B1.last_step_filled(act, s, 4)
                act.activation(st[:, g], psum[3][:, 0:3 * P], ACT.Copy).then_inc(free[3], 1)

            def dcn(s, j):
                if j % 4 == 3:
                    n = j // 4
                    B1.filled(act, s, ("dcn", n))
                    act.wait_ge(S["x1_added"], FROM + s * 2 + n)
                    act.activation(r1[:, :], psum[4][:, :], ACT.Relu, bias=bi1[:, :], scale=sc1[:, :])\
                       .then_inc(free[4], 1)


            def l2_y(s, c):
                n, g = divmod(c, GI)
                for d in range(NB2):
                    name = ("y", c, d)
                    B2.filled(act, s, name)
                    if c >= 2:
                        B2.filled(act, s, ("ga", c - 2, NB2 - 1))
                    act.activation(yg[:, c % 2, d], psum[B2.bank(name)][:, :], ACT.Gelu_apprx_tanh,
                                   bias=cb15[:, d:d + 1]).then_inc(free[B2.bank(name)], 1)

            def l2_glu(s, c):
                n, g = divmod(c, GI)
                for d in range(NB2):
                    if c:
                        B2.read(act, s, ("z", c - 1, d))
                    b = B2.bank(("gb", c, d))
                    B2.filled(act, s, ("gb", c, d))
                    act.activation(tg[:, d], psum[b][:, :], ACT.Tanh, scale=0.5,
                                   bias=hb_glu[:, NB2 + d:NB2 + d + 1]).then_inc(free[b], 1)
                    b = B2.bank(("ga", c, d))
                    B2.filled(act, s, ("ga", c, d))
                    act.activation(ae[:, d], psum[b][:, :], ACT.Identity, scale=0.5,
                                   bias=hb_glu[:, d:d + 1]).then_inc(free[b], 1)
                for d in range(NB2):
                    B2.read(act, s, ("z", c, d))
                    if n:
                        B2.filled(act, s, ("sq", 0))
                    else:
                        B2.last_step_filled(act, s, 5)
                    act.activation(sqb[:, g, d], rb[:, g, d], ACT.Square).then_inc(S["sq_ready"], 1)

            def l2_close(s, n):
                B2.filled(act, s, ("mu", n))
                b = B2.bank(("mu", n))
                act.wait_ge(S["x2_added"], FROM + s * 2 + n)
                act.activation(musq[:, :], psum[b][:, :], ACT.Square).then_inc(free[b], 1)

            def l2_end(s, n):
                B2.read(act, s, ("sq", n))
                act.activation(var2[:, :], var2[:, :], ACT.Ln, bias=epst[:, :]).then_inc(S["ln2_ready"], 1)
                act.wait_ge(S["ln2_ready"], s * 2 + n + 1)
                act.activation(var2[:, :], var2[:, :], ACT.Exp, scale=-0.5).then_inc(S["rstd2_ready"], 1)

            def pe_tap(s, t, many):
                i = t - (K7 * K7 - many)
                if i == 0:
                    act.wait_ge(S["x2_added"], FROM + s * 2 + 2)
                if i >= DRING:
                    act.wait_ge(S["diag_used"], FROM + s * (PE_TAPS - 1) + i - DRING + 1)
                act.activation(diag[:, i % DRING], ident, ACT.Copy, scale=prm("dw")[:, t:t + 1])\
                   .then_inc(S["diag_ready"], 1)

            def l3_center(s):
                for n in range(2):
                    B2.read(act, s, ("mu3", n))
                    act.activation(ysq[:, n * HALF:(n + 1) * HALF], yc[:, n * HALF:(n + 1) * HALF], ACT.Square)\
                       .then_inc(S["ysq_ready"], 1)
                for n in range(2):
                    B2.filled(act, s, ("sq3", n))
                    b = B2.bank(("sq3", n))
                    h = slice(n * HALF, (n + 1) * HALF)
                    act.activation(ysq[:, h], psum[b][:, :], ACT.Ln, bias=epst[:, :]).then_inc(free[b], 1)
                for n in range(2):
                    h = slice(n * HALF, (n + 1) * HALF)
                    B2.read(act, s, ("sq3", n))
                    act.activation(ysq[:, h], ysq[:, h], ACT.Exp, scale=-0.5).then_inc(S["rstd3_ready"], 1)

            def l3_scale(s):
                for n in range(2):
                    h = slice(n * HALF, (n + 1) * HALF)
                    act.wait_ge(S["yz_ready"], s * 2 + n + 1)
                    act.activation(yc[:, h], yc[:, h], ACT.Identity, scale=prm("ln3_g"), bias=prm("ln3_b"))\
                       .then_inc(S["yn_ready"], 1)

            def l3_mlp(s, n):
                for g in range(GI):
                    B2.filled(act, s, ("hid", n, g))
                    if n and g == 0:
                        B2.filled(act, s, ("mlp", 0))
                    b = B2.bank(("hid", n, g))
                    act.activation(hg[:, g], psum[b][:, :], ACT.Gelu_apprx_tanh, bias=prm("b1"))\
                       .then_inc(free[b], 1)

            def l3_add(s, n):
                b = B2.bank(("mlp", n))
                B2.filled(act, s, ("mlp", n))
                act.activation(t3[n][:, :], psum[b][:, :], ACT.Identity, bias=b2ls[:, :], scale=prm("ls"))\
                   .then_inc(free[b], 1)

            run(act, dict(s4d=s4d, l0_head=lambda s: root(s, 0), l0_spread=l0_spread, l0_route=l0_route,
                          l0_unit=l0_unit, l1_norm=lambda s: root(s, 1), l1_conv=l1_conv, l1_table=l1_table,
                          l1_index=l1_index, turn=turn, dcn=dcn, l2_head=lambda s: root(s, 2), l2_y=l2_y,
                          l2_glu=l2_glu, l2_close=l2_close, l2_end=l2_end, l3_head=lambda s: root(s, 3),
                          pe_tap=pe_tap, l3_center=l3_center, l3_scale=l3_scale, l3_mlp=l3_mlp, l3_add=l3_add))

        @block.vector
        def _(dve):
            ch = Chain(dve, S["dve_chain"])
            for started in (S["smp_ready"], S["x1_added"], S["x2_added"]):
                dve.sem_inc(started, FROM)
            tt, ts, stt = dve.tensor_tensor, dve.tensor_scalar, dve.scalar_tensor_tensor
            dve.wait_ge(S["par_in"], 32)
            dve.memset(epst[:, :], EPS).then_inc(S["eps_set"], 1)
            dve.wait_ge(S["exp_done"], 1)
            a_im = prm("a_imag").rearrange("p (d n) -> p d n", d=NB2)
            ch.did(ts(s4["ar"][:, :, :], s4["ea"][:, :, :], -1.0, None, ALU.mult))
            ch.did(tt(s4["am"][:, :, :], s4["ea"][:, :, :], s4["ea"][:, :, :], ALU.mult))
            ch.then(tt(s4["t1"][:, :, :], a_im, a_im, ALU.mult))
            ch.then(tt(s4["am"][:, :, :], s4["am"][:, :, :], s4["t1"][:, :, :], ALU.add))
            dve.reciprocal(s4["ra"][:, :, :], s4["am"][:, :, :]).then_inc(S["a_inv"], 1)
            dve.wait_ge(S["s1_std"], 1)
            ch.then(dve.reciprocal(sc1[:, :], std[:, 0:1]))
            ch.did(tt(sc1[:, :], sc1[:, :], prm("l1_gamma"), ALU.mult))
            ch.then(tt(bi1[:, :], prm("l1_b"), prm("l1_mean"), ALU.subtract))
            ch.then(stt(out=bi1[:, :], in0=bi1[:, :], scalar=sc1[:, 0:1], in1=prm("l1_beta"),
                        op0=ALU.mult, op1=ALU.add))
            dve.wait_ge(S["zeros_set"], 1)
            dve.wait_ge(S["x0_in"], 16)
            ch.restart()

            def s4d(s):
                for d in range(NB2):
                    op = ts(wg2[:, d], w_dec4[:, d, 0:C], prm("ln2_g")[:, d:d + 1], None, ALU.mult)
                    if d:
                        op.then_inc(S["wg_done"], 1)
                dve.wait_ge(S["wg_done"], 1)
                dve.wait_ge(S["cm_done"], 1)
                ch.did(tt(wdp[:, :, :], wg2[:, :, :],
                          psum[4][:, 0:C].unsqueeze(1).to_broadcast([P, NB2, C]), ALU.subtract))
                dve.wait_ge(S["cm_done"], 2)
                ch.did(tt(b2ls[:, :], prm("b2"), prm("ls"), ALU.mult))
                tt(dconst[:, :], psum[3][:, 0:1], prm("b_dec"), ALU.add).then_inc(S["dec_there"], 1)
                dve.wait_ge(S["dec_there"], 1)

            def load_conv(s):
                dve.wait_ge(S["wts_in"], 48)
                dve.wait_ge(S["x_in"], 16)
                ch.did(tt(bb[:, :, :], bb[:, :, :], prm("b_om").unsqueeze(1).to_broadcast([P, NT, OMC]), ALU.add))

            def norm(s, layer):
                at = s % NS if layer == 0 else s
                for n in range(2):
                    ch.did(dve.bn_stats(bst[:, layer, n], X[:, bass.ds(at, 1), n * HALF:(n + 1) * HALF]
                                        .rearrange("p o n -> p (o n)")))
                ch.wait()
                dve.bn_aggr(mv[:, layer], bst[:, layer].rearrange("p a b -> p (a b)"))\
                   .then_inc(S[f"var_ready{layer}"], 1)
                dve.wait_ge(S[f"std_ready{layer}"], s + 1)
                ch.then(dve.reciprocal(rs[:, layer:layer + 1], std[:, layer:layer + 1]))
                return mv[:, layer, 0:1], rs[:, layer:layer + 1]

            def l0_head(s):
                mean, r = norm(s, 0)
                xv = X[:, bass.ds(s % NS, 1), :].rearrange("p o n -> p (o n)")
                ts(xn0[:, :], xv, mean, r, ALU.subtract, ALU.mult).then_inc(S["xn0_ready"], 1)

            def l0_route(s):
                B0.filled(dve, s, "router")
                logit = psum[2][:, 0:8 * NE].rearrange("p (t e) -> p t e", t=8)
                ch.then(dve.tensor_reduce(m1[:, :], logit, AX.X, ALU.max))

                def over(v):
                    return v[:, :].unsqueeze(2).to_broadcast([P, 8, NE])
                tt(lg[:, :, :], logit, over(m1), ALU.subtract).then_inc(free[2], 1)
                B0.read(dve, s, "router")
                rank = con("rank").unsqueeze(1).to_broadcast([P, 8, NE])

                def first_max(o, src):
                    ch.then(dve.tensor_reduce(m1[:, :], src, AX.X, ALU.max))
                    ch.then(tt(o, src, over(m1), ALU.is_equal))
                    ch.then(tt(o, o, rank, ALU.mult))
                    ch.then(dve.tensor_reduce(m1[:, :], o, AX.X, ALU.max))
                    ch.then(tt(o, o, over(m1), ALU.is_equal))
                ch.then(ts(gate[:, :, :], lg[:, :, :], 1.0, None, ALU.mult))
                dve.memset(m1[:, :], 0.0).then_inc(S["max_ready"], 1)
                dve.wait_ge(S["max_ready"], s + 1)
                first_max(oh[:, :, :], gate[:, :, :])
                ch.then(stt(out=gate[:, :, :], in0=oh[:, :, :], scalar=-1e30, in1=gate[:, :, :],
                            op0=ALU.mult, op1=ALU.add))
                first_max(oh2[:, :, :], gate[:, :, :])
                ch.then(tt(oh[:, :, :], oh[:, :, :], oh2[:, :, :], ALU.add))
                dve.wait_ge(S["exp_ready"], s + 1)
                ch.then(tt(gate[:, :, :], ex[:, :, :], oh[:, :, :], ALU.mult))
                ch.then(dve.tensor_reduce(m1[:, :], gate[:, :, :], AX.X, ALU.add))
                ch.then(dve.reciprocal(m1[:, :], m1[:, :]))
                ch.then(stt(out=gate[:, :, :], in0=gate[:, :, :], scalar=0.5, in1=over(m1),
                            op0=ALU.mult, op1=ALU.mult))

            def l0_he(s, u):
                B0.filled(dve, s, ("value", u))
                B0.read(dve, s, ("gate", u))
                stt(out=he[:, u % 2], in0=he[:, u % 2], scalar=1.0, in1=psum[1][:, :],
                    op0=ALU.add, op1=ALU.mult).then_inc(free[1], 1)

            def l0_acc(s, u):
                g, e = divmod(u, NE)
                B0.filled(dve, s, ("out", u))
                if e:
                    B0.read(dve, s, ("out", u - 1))
                for t in range(2):
                    sc = gate[:, g * 2 + t, e:e + 1]
                    o = psum[2][:, t * D0:(t + 1) * D0].rearrange("p (a c) -> p a c", c=C)
                    a = acc[:, t, :, g]
                    if e:
                        op = stt(out=a, in0=o, scalar=sc, in1=a, op0=ALU.mult, op1=ALU.add)
                    else:
                        op = ts(a, o, sc, None, ALU.mult)
                    if t:
                        op.then_inc(free[2], 1)

            def l0_tail(s):
                for t in range(2):
                    B0.filled(dve, s, ("back", t))
                    for dy in range(PT):
                        xv = X[:, bass.ds(s, 1), :].rearrange("p o (h a w b) -> p (o h) a b w", a=PT, b=PT,
                                                              w=W // PT)
                        xv = xv[:, t * 8:(t + 1) * 8, dy].rearrange("p h b w -> p b h w")
                        bk = psum[t][:, dy * 2 * P:(dy + 1) * 2 * P].rearrange("p (b h w) -> p b h w", b=PT, h=8)
                        op = tt(xv, xv, bk, ALU.add)
                        if dy:
                            op.then_inc(free[t], 1)
                        else:
                            ch.did(op)
                B0.read(dve, s, ("back", 0))
                B0.read(dve, s, ("back", 1))
                hold(dve)

            def l1_norm(s):
                mean, r = norm(s, 1)
                xv = X[:, bass.ds(s, 1), :].rearrange("p o (h w) -> p (o h) w", w=W)
                ts(xpad_v[:, 1:H + 1, 1:W + 1], xv, mean, r, ALU.subtract, ALU.mult).then_inc(S["xpad_ready"], 1)

            def l1_om(s):
                for n in range(2):
                    B0.filled(dve, s, ("om", n))
                    b = B0.bank(("om", n))
                    tt(om[:, n * 4:(n + 1) * 4], psum[b][:, 0:4 * OMC].rearrange("p (t m) -> p t m", t=4),
                       bb[:, n * 4:(n + 1) * 4], ALU.add).then_inc(free[b], 1)
                B0.read(dve, s, ("om", 0))
                B0.read(dve, s, ("om", 1))
                pos = om[:, :, 0:NXY]
                ts(pos, pos, 0.0, float(H + 1), ALU.max, ALU.min).then_inc(S["om_ready"], 1)

            def l1_index(s):
                pos = om[:, :, 0:NXY]
                dve.wait_ge(S["om_ready"], s + 1)
                ch.then(dve.tensor_copy(fi[:, :, :], pos))
                ch.then(dve.tensor_copy(fl[:, :, :], fi[:, :, :]))
                ch.then(tt(fr[:, :, :], fl[:, :, :], pos, ALU.is_gt))
                ch.then(tt(fl[:, :, :], fl[:, :, :], fr[:, :, :], ALU.subtract))
                ch.then(ts(fl[:, :, :], fl[:, :, :], float(H), None, ALU.min))
                ch.did(tt(fr[:, :, :], pos, fl[:, :, :], ALU.subtract))
                ch.then(stt(out=mk1[:, :, :], in0=fl[:, :, 0:NK], scalar=float(PW), in1=fl[:, :, NK:NXY],
                            op0=ALU.mult, op1=ALU.add))
                ch.then(stt(out=idxn[:, :, :], in0=mk1[:, :, :], scalar=rowoff[:, 0:1],
                            in1=con("image_row").unsqueeze(1).to_broadcast([P, NT, NK]),
                            op0=ALU.add, op1=ALU.add))
                ch.did(ts(rowoff[:, :], rowoff[:, :], -1.0, float(GI * TROWS), ALU.mult, ALU.add))

            def l1_share(s):
                dve.wait_ge(S["mask_ready"], s + 1)
                ch.then(ts(mk1[:, :, :], mk[:, :, :], 0.5, 0.5, ALU.mult, ALU.add))
                fy, fx = fr[:, :, 0:NK], fr[:, :, NK:NXY]
                ch.then(tt(mk[:, :, :], mk1[:, :, :], fy, ALU.mult))
                ch.did(tt(cwn[:, :, :, 3], mk[:, :, :], fx, ALU.mult))
                ch.then(tt(mk1[:, :, :], mk1[:, :, :], mk[:, :, :], ALU.subtract))
                ch.did(tt(cwn[:, :, :, 2], mk[:, :, :], cwn[:, :, :, 3], ALU.subtract))
                ch.then(tt(cwn[:, :, :, 1], mk1[:, :, :], fx, ALU.mult))
                ch.then(tt(cwn[:, :, :, 0], mk1[:, :, :], cwn[:, :, :, 1], ALU.subtract))

            def swap(s, last):
                j = slice(NT - 1, NT) if last else slice(0, NT - 1)
                ch.wait()
                dve.tensor_copy(idx[:, j], idxn[:, j]).then_inc(S["idx_ready"], 1)
                ch.did(dve.tensor_copy(cw[:, j], cwn[:, j]))

            def sample(s, t):
                j, g = divmod(t, GI)
                dve.wait_ge(gathered[g], (s * NT + j + 1) * 16 * KK)
                rows = gt[:, g].rearrange("p k a c -> p (k a) c")
                share = cw[:, j, g * KK:(g + 1) * KK].rearrange("p k a -> p (k a)")
                ch.then(tt(rows, rows, share.unsqueeze(2).to_broadcast([P, 4 * KK, C]), ALU.mult))
                ch.then(tt(gt[:, g, :, 0:2], gt[:, g, :, 0:2], gt[:, g, :, 2:4], ALU.add))
                if t >= 2:
                    B1.filled(dve, s, ("sampled", (t - 2) // GI, (t - 2) % GI))
                else:
                    B1.last_step_filled(dve, s, 3)
                tt(sm[:, t % 2, 0:KK * C].rearrange("p (k c) -> p k c", k=KK), gt[:, g, :, 0], gt[:, g, :, 1],
                   ALU.add).then_inc(S["smp_ready"], 1)

            def dcn(s, j):
                if j % 4 == 3:
                    n = j // 4
                    B1.read(dve, s, ("dcn", n))
                    xh = X[:, bass.ds(s, 1), n * HALF:(n + 1) * HALF].rearrange("p o n -> p (o n)")
                    tt(xh, xh, r1[:, :], ALU.add).then_inc(S["x1_added"], 1)

            def l2_head(s):
                dve.wait_ge(S["x1_added"], FROM + s * 2 + 2)
                hold(dve)
                mean, r = norm(s, 2)
                for g in range(GI):
                    dve.wait_ge(u_in[g], FROM + s * 16 * JJ)
                xv = X[:, bass.ds(s, 1), :].rearrange("p o n -> p (o n)")
                ts(xn2[:, :], xv, mean, r, ALU.subtract, ALU.mult).then_inc(S["u_ready"], 1)

            def l2_glu(s, c):
                n, g = divmod(c, GI)
                for d in range(NB2):
                    B2.read(dve, s, ("ga", c, d))
                    stt(out=tg[:, d], in0=tg[:, d], scalar=1.0, in1=ae[:, d], op0=ALU.add, op1=ALU.mult)\
                        .then_inc(S["glu_done"], 1)
                    dve.wait_ge(S["glu_done"], s * 8 * NB2 + (n * GI + g) * NB2 + d + 1)
                    B2.filled(dve, s, ("z", c, d))
                    if n:
                        dve.wait_ge(S["sq_ready"], s * 8 * NB2 + GI * NB2)
                    else:
                        B2.last_step_filled(dve, s, 5)
                    b = B2.bank(("z", c, d))
                    stt(out=rb[:, g, d], in0=psum[b][:, :], scalar=prm("b_enc")[:, d:d + 1], in1=tg[:, d],
                        op0=ALU.add, op1=ALU.add).then_inc(free[b], 1)

            def l2_var(s, n):
                b = B2.bank(("sq", n))
                B2.filled(dve, s, ("sq", n))
                B2.read(dve, s, ("mu", n))
                tt(var2[:, :], psum[b][:, :], musq[:, :], ALU.subtract).then_inc(free[b], 1)

            def l2_end(s, n):
                dve.wait_ge(S["rstd2_ready"], s * 2 + n + 1)
                B2.filled(dve, s, ("dec", n))
                b = B2.bank(("dec", n))
                tt(musq[:, :], psum[b][:, :], var2[:, :], ALU.mult).then_inc(free[b], 1)
                B2.read(dve, s, ("dec", n))
                xh = X[:, bass.ds(s, 1), n * HALF:(n + 1) * HALF].rearrange("p o n -> p (o n)")
                stt(out=xh, in0=musq[:, :], scalar=dconst[:, 0:1], in1=xh, op0=ALU.add, op1=ALU.add)\
                    .then_inc(S["x2_added"], 1)

            def l3_head(s):
                dve.wait_ge(S["x2_added"], FROM + s * 2 + 2)
                hold(dve)
                mean, r = norm(s, 3)
                xv = X[:, bass.ds(s, 1), :].rearrange("p o (h w) -> p (o h) w", w=W)
                pd = K7 // 2
                ts(xp3_v[:, pd:pd + H, pd:pd + W], xv, mean, r, ALU.subtract, ALU.mult).then_inc(S["xp3_ready"], 1)
                dve.wait_ge(S["xp3_ready"], s + 1)

            last = [0, 0]

            def tap(s, t):
                win = xp3_v[:, t // K7:t // K7 + H, t % K7:t % K7 + W]
                weight = prm("dw")[:, t:t + 1]
                a = t % 2
                y = ya[:, a].rearrange("p (h w) -> p h w", h=H)
                if t == 0:
                    op = ts(y, win, weight, prm("dw_b"), ALU.mult, ALU.add)
                elif t == 1:
                    op = ts(y, win, weight, None, ALU.mult)
                else:
                    ch.wait(last[a])
                    op = stt(out=y, in0=win, scalar=weight, in1=y, op0=ALU.mult, op1=ALU.add)
                last[a] = ch.did(op)

            def l3_sum(s):
                ch.wait()
                ch.then(tt(ya[:, 0], ya[:, 0], ya[:, 1], ALU.add))
                for n in range(2):
                    h = slice(n * HALF, (n + 1) * HALF)
                    B2.filled(dve, s, ("tap", n))
                    b = B2.bank(("tap", n))
                    tt(ya[:, 0, h], ya[:, 0, h], psum[b][:, :], ALU.add).then_inc(free[b], 1)

            def l3_center(s):
                for n in range(2):
                    h = slice(n * HALF, (n + 1) * HALF)
                    B2.filled(dve, s, ("mu3", n))
                    B2.read(dve, s, ("tap", n))
                    b = B2.bank(("mu3", n))
                    tt(yc[:, h], ya[:, 0, h], psum[b][:, :], ALU.subtract).then_inc(free[b], 1)

            def l3_scale(s):
                for n in range(2):
                    h = slice(n * HALF, (n + 1) * HALF)
                    dve.wait_ge(S["rstd3_ready"], s * 2 + n + 1)
                    B2.read(dve, s, ("mu3", n))
                    tt(yc[:, h], yc[:, h], ysq[:, h], ALU.mult).then_inc(S["yz_ready"], 1)

            def l3_add(s, n):
                B2.read(dve, s, ("mlp", n))
                xh = X[:, bass.ds(s, 1), n * HALF:(n + 1) * HALF].rearrange("p o n -> p (o n)")
                tt(xh, xh, t3[n][:, :], ALU.add).then_inc(S["x3_ready"], 1)

            def l0_unit(s, u):
                if u < NU:
                    l0_he(s, u)
                if u:
                    l0_acc(s, u - 1)

            run(dve, dict(load_conv=load_conv, s4d=s4d, l0_head=l0_head, l0_route=l0_route, l0_unit=l0_unit,
                          l0_tail=l0_tail, l1_norm=l1_norm, l1_om=l1_om, l1_index=l1_index, l1_share=l1_share,
                          swap=swap, sample=sample, dcn=dcn, l2_head=l2_head, l2_glu=l2_glu, l2_var=l2_var,
                          l2_end=l2_end, l3_head=l3_head, tap=tap, l3_sum=l3_sum, l3_center=l3_center,
                          l3_scale=l3_scale, l3_add=l3_add), end=ch.restart)

        @block.tensor
        def _(pe):
            mm = pe.matmul
            for started in full + free + [S["diag_used"]]:
                pe.sem_inc(started, FROM)
            pe.wait_ge(S["par_in"], 32)

            def load_experts(s):
                pe.wait_ge(S["w1_in"], 32)
                pe.wait_ge(S["w2_in"], 32)

            def load_conv(s):
                pe.wait_ge(S["wts_in"], 48)

            def s4d(s):
                pe.wait_ge(S["wg_done"], 1)
                for d in range(NB2):
                    op = mm(psum[4][:, 0:C], con("mean256"), wg2[:, d], start=d == 0, stop=d == NB2 - 1)
                op.then_inc(S["cm_done"], 1)
                for d in range(NB2):
                    op = mm(psum[3][:, 0:1], w_dec4[:, d], prm("ln2_b")[:, d:d + 1], start=d == 0, stop=d == NB2 - 1)
                op.then_inc(S["cm_done"], 1)
                pe.wait_ge(S["s4_done"], 1)
                for t in range(JJ):
                    for d in range(NB2):
                        op = pe.transpose(psum[5 + t // 2][:, (t % 2 * NB2 + d) * P:(t % 2 * NB2 + d + 1) * P],
                                          kw[:, d, t * JJ:(t + 1) * JJ].rearrange("p j s -> p (j s)"), ident)
                    if t % 2:
                        op.then_inc(S["k_turned"], 1)
                for d in range(NB2):
                    op = pe.transpose(psum[7][0:LM, d * P:(d + 1) * P], cor[:, d], ident)
                op.then_inc(S["k_turned"], 1)
                pe.wait_ge(S["k_there"], 1)
                pe.wait_ge(S["dec_there"], 1)

            def l0_spread(s):
                pe.wait_ge(S["xn0_ready"], s + 1)
                patches = xn0[:, :].rearrange("p (h a w b) -> p a b h w", h=H // PT, a=PT, b=PT)
                for b in range(2):
                    B0.vacant(pe, s, ("xp", b))
                    for i in range(2):
                        g = 2 * b + i
                        for dyx in range(PT * PT):
                            op = mm(psum[b][dyx * C:(dyx + 1) * C, i * TOK:(i + 1) * TOK],
                                    ident[:, g * C:(g + 1) * C], patches[:, dyx // PT, dyx % PT],
                                    start=True, stop=True)
                    op.then_inc(full[b], 1)

            def l0_route(s):
                B0.read(pe, s, ("xp", 0))
                B0.read(pe, s, ("xp", 1))
                B0.vacant(pe, s, "router")
                for t in range(8):
                    op = mm(psum[2][:, t * NE:(t + 1) * NE], xp[:, t // 2, t % 2 * P:(t % 2 + 1) * P],
                            prm("router"), start=True, stop=True)
                op.then_inc(full[2], 1)

            def l0_h(s, u):
                g, e = divmod(u, NE)
                for kind, b, first in (("gate", 0, 2), ("value", 1, 0)):
                    B0.vacant(pe, s, (kind, u))
                    for h in range(2):
                        op = mm(psum[b][:, h * TOK:(h + 1) * TOK], w1_sb[:, e, first + h], xp[:, g],
                                start=True, stop=True)
                    op.then_inc(full[b], 1)

            def l0_out(s, u):
                g, e = divmod(u, NE)
                B0.read(pe, s, ("value", u))
                B0.vacant(pe, s, ("out", u))
                for t in range(2):
                    for h in range(2):
                        op = mm(psum[2][:, t * D0:(t + 1) * D0],
                                he[:, u % 2, h * TOK + t * P:h * TOK + (t + 1) * P], w2_sb[:, e, h],
                                start=h == 0, stop=h == 1)
                op.then_inc(full[2], 1)

            def l0_tail(s):
                B0.read(pe, s, ("out", NU - 1))
                for t in range(2):
                    B0.vacant(pe, s, ("back", t))
                    for dyx in range(4):
                        op = pe.transpose(psum[t][:, dyx * P:(dyx + 1) * P],
                                          acc[:, t, dyx].rearrange("p g c -> p (g c)"),
                                          ident)
                    op.then_inc(full[t], 1)

            def l1_table(s, t):
                B0.vacant(pe, s, ("table", t))
                b = B0.bank(("table", t))
                for a in range(4):
                    at = t * P + a // 2 * PW + a % 2
                    op = pe.transpose(psum[b][:, a * P:(a + 1) * P], xpad[:, at:at + P], ident)
                op.then_inc(full[b], 1)

            def l1_conv(s):
                pe.wait_ge(S["xpad_ready"], s + 1)
                for n in range(2):
                    B0.vacant(pe, s, ("omc", n))
                    b = B0.bank(("omc", n))
                    for k in range(KK):
                        y0 = n * (H // 2) + k // 3
                        op = mm(psum[b][0:OMC, :], w_om[:, k],
                                xpad_v[:, y0:y0 + H // 2, k % 3:k % 3 + W], start=k == 0, stop=k == KK - 1)
                    op.then_inc(full[b], 1)
                for t in range(TRING):
                    l1_table(s, t)

            def l1_om(s):
                for n in range(2):
                    B0.read(pe, s, ("omc", n))
                    B0.vacant(pe, s, ("om", n))
                    b = B0.bank(("om", n))
                    for t in range(4):
                        at = (n * 4 + t) * P
                        op = pe.transpose(psum[b][:, t * OMC:(t + 1) * OMC], omt[0:OMC, at:at + P],
                                          ident[0:OMC, 0:OMC])
                    op.then_inc(full[b], 1)

            def turn(s, t):
                j, g = divmod(t, GI)
                pe.wait_ge(S["smp_ready"], FROM + s * NT * GI + t + 1)
                B1.vacant(pe, s, ("sampled", j, g))
                for k in range(3):
                    op = pe.transpose(psum[3][:, k * P:(k + 1) * P], sm[:, t % 2, k * P:(k + 1) * P], ident)
                op.then_inc(full[3], 1)

            def dcn(s, j):
                if j % 4 == 0:
                    B1.vacant(pe, s, ("dcn", j // 4))
                B1.read(pe, s, ("sampled", j, GI - 1))
                for k in range(3):
                    for g in range(GI):
                        op = mm(psum[4][g * C:(g + 1) * C, j % 4 * P:(j % 4 + 1) * P], w_dcn[:, k],
                                st[:, g, k * P:(k + 1) * P], start=k == 0, stop=k == 2)
                op.then_inc(full[4] if j % 4 == 3 else S["st_used"], 1)

            def l2_y(s, c):
                n, g = divmod(c, GI)
                if n == 0:
                    pe.wait_ge(u_in[g], FROM + (s + 1) * 16 * JJ)
                for d in range(NB2):
                    name = ("y", c, d)
                    B2.vacant(pe, s, name)
                    o = psum[B2.bank(name)]
                    for t in range(JJ):
                        at = LM + n * HALF - JJ * t
                        op = mm(o[:, :], wk[:, t, d], u4[:, g, at:at + HALF], start=t == 0,
                                stop=t == JJ - 1 and n > 0)
                    if n == 0:
                        op = mm(o[:, 0:LM], corr[:, d], ident[0:LM, 0:LM], start=False, stop=True)
                    op.then_inc(full[B2.bank(name)], 1)

            def l2_glu(s, c):
                n, g = divmod(c, GI)
                B2.read(pe, s, ("y", c, NB2 - 1))
                B2.read(pe, s, ("y", c, 0))
                for d in range(NB2):
                    for kind, col in (("gb", DM), ("ga", 0)):
                        name = (kind, c, d)
                        B2.vacant(pe, s, name)
                        for k in range(NB2):
                            op = mm(psum[B2.bank(name)][:, :], w_glu[:, k, col + d * P:col + (d + 1) * P],
                                    yg[:, c % 2, k], start=k == 0, stop=k == NB2 - 1)
                        op.then_inc(full[B2.bank(name)], 1)
                    name = ("z", c, d)
                    B2.vacant(pe, s, name)
                    mm(psum[B2.bank(name)][:, :], wenc[:, d * P:(d + 1) * P],
                       u4[:, g, LM + n * HALF:LM + (n + 1) * HALF], start=True, stop=True)\
                        .then_inc(full[B2.bank(name)], 1)

            def l2_close(s, n):
                pe.wait_ge(S["sq_ready"], s * 8 * NB2 + (n + 1) * GI * NB2)
                B2.read(pe, s, ("z", n * GI + GI - 1, NB2 - 1))
                for kind, weight, src in (("mu", None, rb), ("sq", None, sqb), ("dec", wdp, rb)):
                    b = B2.bank((kind, n))
                    B2.vacant(pe, s, (kind, n))
                    for d in range(NB2):
                        for g in range(GI):
                            lhs = weight[:, d] if weight is not None else con("mean256")[:, 0:C]
                            op = mm(psum[b][g * C:(g + 1) * C, :], lhs, src[:, g, d], start=d == 0,
                                    stop=d == NB2 - 1)
                    op.then_inc(full[b], 1)

            def pe_tap(s, t, many):
                i = t - (K7 * K7 - many)
                if i == 0:
                    pe.wait_ge(S["xp3_ready"], s + 1)
                    for n in range(2):
                        B2.vacant(pe, s, ("tap", n))
                pe.wait_ge(S["diag_ready"], s * PE_TAPS + i + 1)
                for n in range(2):
                    y0 = n * (H // 2) + t // K7
                    op = mm(psum[B2.bank(("tap", n))][:, :], diag[:, i % DRING],
                            xp3_v[:, y0:y0 + H // 2, t % K7:t % K7 + W], start=i == 0, stop=i == many - 1)
                    if i == many - 1:
                        op.then_inc(full[B2.bank(("tap", n))], 1)
                if i < many - 1:
                    op.then_inc(S["diag_used"], 1)

            def l3_sum(s):
                for n in range(2):
                    B2.read(pe, s, ("tap", n))
                    b = B2.bank(("mu3", n))
                    B2.vacant(pe, s, ("mu3", n))
                    mm(psum[b][:, :], con("mean32"), ya[:, 0, n * HALF:(n + 1) * HALF], start=True, stop=True)\
                        .then_inc(full[b], 1)

            def l3_center(s):
                for n in range(2):
                    pe.wait_ge(S["ysq_ready"], s * 2 + n + 1)
                    b = B2.bank(("sq3", n))
                    B2.vacant(pe, s, ("sq3", n))
                    mm(psum[b][:, :], con("mean32"), ysq[:, n * HALF:(n + 1) * HALF], start=True, stop=True)\
                        .then_inc(full[b], 1)

            def l3_mlp(s, n):
                pe.wait_ge(S["yn_ready"], s * 2 + n + 1)
                for g in range(GI):
                    b = B2.bank(("hid", n, g))
                    B2.vacant(pe, s, ("hid", n, g))
                    mm(psum[b][:, :], w1_3[:, g], yc[:, n * HALF:(n + 1) * HALF], start=True, stop=True)\
                        .then_inc(full[b], 1)
                b = B2.bank(("mlp", n))
                B2.vacant(pe, s, ("mlp", n))
                for g in range(GI - 3, GI):
                    B2.read(pe, s, ("hid", n, g))
                for g in range(GI):
                    op = mm(psum[b][g * C:(g + 1) * C, :], wt("w2_3"), hg[:, g], start=True, stop=True)
                op.then_inc(full[b], 1)

            def l0_unit(s, u):
                if u < NU:
                    l0_h(s, u)
                if u:
                    l0_out(s, u - 1)

            run(pe, dict(load_experts=load_experts, load_conv=load_conv, s4d=s4d, l0_spread=l0_spread,
                         l0_route=l0_route, l0_unit=l0_unit, l0_tail=l0_tail, l1_conv=l1_conv,
                         l1_om=l1_om, l1_table=l1_table, turn=turn, dcn=dcn,
                         l2_y=l2_y, l2_glu=l2_glu, l2_close=l2_close, pe_tap=pe_tap, l3_sum=l3_sum,
                         l3_center=l3_center, l3_mlp=l3_mlp))


def shape_constants():
    c = np.zeros((P, NCONST), np.float32)

    def put(name, a):
        lo, hi = CONSTS[name]
        c[:, lo:hi] = a.reshape(P, hi - lo)
    put("ident", np.eye(P, dtype=np.float32))
    put("image_row", np.broadcast_to(np.repeat(np.arange(GI) * TROWS, KK).astype(np.float32), (P, GI * KK)))
    put("mean32", np.kron(np.eye(GI), np.full((C, C), 1.0 / C)).astype(np.float32))
    put("mean256", np.full((P, P), 1.0 / DM, np.float32))
    put("rank", np.broadcast_to(np.arange(NE, 0, -1).astype(np.float32), (P, NE)))
    return c


def tap_places():
    base = np.zeros((P, NT, 3, GI, KK), np.float32)
    p, t, k = np.arange(P)[:, None, None], np.arange(NT)[None, :, None], np.arange(KK)[None, None, :]
    base[:, :, 0] = (t * (P // W) + p // W + k // 3)[:, :, None]
    base[:, :, 1] = (p % W + k % 3 + 0 * t)[:, :, None]
    return base.reshape(P, NT * OMC)


def lay_out(a):
    f = {n: np.asarray(v) for n, v in a.items()}
    L0, L1, L2, L3 = (f"L{i}_conv_" for i in range(4))

    def patch(w, axis):
        w = np.moveaxis(w, axis, 0)
        w = w.reshape((C, PT, PT) + w.shape[1:])
        w = np.moveaxis(w, 0, 2)
        return np.moveaxis(w.reshape((D0,) + w.shape[3:]), 0, axis)

    w1 = patch(f[L0 + "w1"], 1).transpose(1, 0, 2).reshape(P, NE * 4 * P)
    w2 = patch(f[L0 + "w2"], 2).reshape(NE, 2, P, D0).transpose(2, 0, 1, 3).reshape(P, NE * 2 * P)
    params = np.zeros((P, NPARAM), np.float32)

    def put(name, v):
        lo, hi = PARAMS[name]
        params[:, lo:hi] = v.reshape(P, hi - lo)

    def by_image(v):
        return np.concatenate([v.reshape(C, -1)] * GI, axis=0)

    def by_state(v):
        return v.reshape(NB2, P, -1).transpose(1, 0, 2)
    for name, src in (("l1_b", L1 + "b"), ("l1_gamma", L1 + "gamma"), ("l1_beta", L1 + "beta"),
                      ("l1_mean", L1 + "bn_mean"), ("l1_var", L1 + "bn_var"), ("b_dec", L2 + "b_dec"),
                      ("dw_b", L3 + "dw_b"), ("ln3_g", L3 + "ln_g"), ("ln3_b", L3 + "ln_b"),
                      ("b2", L3 + "b2"), ("ls", L3 + "ls"), ("dw", L3 + "dw_w")):
        put(name, by_image(f[src]))
    put("b1", f[L3 + "b1"])
    for name, src in (("b_enc", "b_enc"), ("log_dt", "log_dt"), ("a_real", "A_log_real"), ("a_imag", "A_imag"),
                      ("c_real", "C_real"), ("c_imag", "C_imag"), ("d", "D"), ("ln2_g", "ln_gamma"),
                      ("ln2_b", "ln_beta")):
        put(name, by_state(f[L2 + src]))
    put("b_glu", f[L2 + "b_glu"].reshape(2 * NB2, P).T)
    put("w_enc_t", f[L2 + "W_enc"].T.reshape(NB2, P, C).transpose(1, 0, 2))
    kinds = [list(range(0, 2 * KK, 2)), list(range(1, 2 * KK, 2)), list(range(2 * KK, 3 * KK))]
    b_om = np.stack([f[L1 + "b_om"][k] for k in kinds])
    put("b_om", np.broadcast_to(b_om[:, None], (3, GI, KK)).reshape(1, OMC).repeat(P, 0))
    put("router", patch(f[L0 + "router_w"], 0))

    weights = np.zeros((P, NWEIGHT), np.float32)

    def put_w(name, v):
        lo, hi = WEIGHTS[name]
        weights[:, lo:hi] = v.reshape(P, hi - lo)
    w_om = np.zeros((GI, C, KK, 3, GI, KK), np.float32)
    per = np.stack([f[L1 + "w_om"][k] for k in kinds]).reshape(3, KK, C, KK)
    for g in range(GI):
        w_om[g, :, :, :, g] = per.transpose(2, 3, 0, 1)
    put_w("w_om", w_om)
    w_dcn = np.zeros((3 * P, C), np.float32)
    w_dcn[:KK * C] = f[L1 + "w"].reshape(C, C, KK).transpose(2, 1, 0).reshape(KK * C, C)
    put_w("w_dcn", w_dcn.reshape(3, P, C).transpose(1, 0, 2))
    put_w("w_glu", f[L2 + "W_glu"].reshape(NB2, P, 2 * DM).transpose(1, 0, 2))
    w_dec = f[L2 + "W_dec"].reshape(NB2, P, C).transpose(1, 0, 2)
    put_w("w_dec", np.concatenate([w_dec] * GI, axis=2))
    w1_3 = np.zeros((GI, C, GI, P), np.float32)
    for g in range(GI):
        w1_3[g, :, g] = f[L3 + "w1"].T
    put_w("w1_3", w1_3)
    put_w("w2_3", f[L3 + "w2"].T)
    w_enc = np.zeros((P, DM), np.float32)
    w_enc[:C] = f[L2 + "W_enc"]
    return {"x": f["x"], "w1": w1, "w2": w2, "w_enc": w_enc, "params": params,
            "consts": shape_constants(), "weights": weights, "places": tap_places()}


def kernel(**inputs):
    import concourse.bacc as _bacc
    from concourse.bass_utils import run_bass_kernel_spmd as _run

    nc = _bacc.Bacc("TRN2", target_bir_lowering=False, num_devices=1)
    arrays = {k: np.ascontiguousarray(v) for k, v in lay_out(inputs).items()}
    args = [nc.dram_tensor(name, a.shape, mybir.dt.from_np(a.dtype), kind="ExternalInput").ap()
            for name, a in arrays.items()]
    out = nc.dram_tensor("out", (B, C, H, W), F32, kind="ExternalOutput").ap()
    build(nc, *args, out)
    r = _run(nc, [arrays], core_ids=[0])
    return r.results[0]["out"]
```
